# Optimizing a Trainium2 kernel written in Bass

```python
import numpy as np
import jax
import jax.numpy as jnp

def _softmax(x, axis=-1):
    return jax.nn.softmax(x, axis=axis)

def _gelu(x):
    return jax.nn.gelu(x, approximate=True)

def _silu(x):
    return jax.nn.silu(x)

def _sigmoid(x):
    return jax.nn.sigmoid(x)

def _layernorm(x, axis=-1, eps=1e-05):
    m = jnp.mean(x, axis=axis, keepdims=True)
    v = jnp.var(x, axis=axis, keepdims=True)
    return (x - m) / jnp.sqrt(v + eps)

def _scatter_add(tgt, idx, src, axis=0):
    return tgt.at[idx].add(src)

def _segment_sum(src, seg, n):
    return jax.ops.segment_sum(src, seg, n)
kernel_name = 'mk_decoder_preln_d1_seqx_r4_a3a8f2'

def setup_inputs(seed: int=0):
    np.random.seed(seed)
    _w = jnp.asarray

    def _rec_inputs():
        import jax
        import jax.numpy as jnp
        _rk = jax.random.key(seed)
        x = -0.0002928 + 1 * jax.random.normal(jax.random.fold_in(_rk, 1), (4, 512, 256), jnp.float32)
        _lenS = 512 - jax.random.randint(jax.random.fold_in(_rk, 7), (4,), 0, max(1, 512 // 4) + 1, jnp.int32)
        _lenS2 = 1024 - jax.random.randint(jax.random.fold_in(_rk, 8), (4,), 0, max(1, 1024 // 4) + 1, jnp.int32)
        _ctx_1024P = jax.random.normal(jax.random.fold_in(_rk, 11), (4, 16, 256), jnp.float32)
        _ctx_1024c = jax.random.dirichlet(jax.random.fold_in(_rk, 511), 0.3 * jnp.ones((16,), jnp.float32), (4, 1024))
        _ctx_1024t = jnp.einsum('bsk,bkd->bsd', _ctx_1024c, _ctx_1024P)
        _ctx_1024t = _ctx_1024t * jax.lax.rsqrt(jnp.mean(jnp.square(_ctx_1024t)) + 1e-12) * 0.953939
        ctx_1024 = 0.00222621 + 0.99962 * (_ctx_1024t + 0.3 * jax.random.normal(jax.random.fold_in(_rk, 611), (4, 1024, 256), jnp.float32))
        return (x, ctx_1024)
    x, ctx_1024 = _rec_inputs()

    def _L0_attn_setup():
        import math
        import jax, jax.numpy as jnp
        import numpy as np
        DIM = 256
        N_HEADS = 16
        HEAD_DIM = DIM // N_HEADS
        SEQ_LEN = 512
        BASE = 10000.0
        EPS = 1e-05

        def rope_cache(seq_len, dim):
            pos = jnp.arange(seq_len, dtype=jnp.float32)[:, None]
            di = jnp.arange(0, dim, 2, dtype=jnp.float32) / dim
            theta = pos * jnp.exp(-di * math.log(BASE))
            cos = jnp.repeat(jnp.cos(theta), 2, axis=1)
            sin = jnp.repeat(jnp.sin(theta), 2, axis=1)
            return (cos, sin)

        def rotate_half(x):
            x1 = x[..., ::2]
            x2 = x[..., 1::2]
            return jnp.concatenate((-x2, x1), axis=-1)

        def layernorm(x, gamma, beta):
            mu = jnp.mean(x, axis=-1, keepdims=True)
            var = jnp.var(x, axis=-1, keepdims=True)
            return (x - mu) * jax.lax.rsqrt(var + EPS) * gamma + beta
        key = jax.random.key(seed)
        ks = jax.random.split(key, 7)
        s = 1.0 / math.sqrt(DIM)
        return {'x': jax.random.normal(ks[0], (2, SEQ_LEN, DIM), dtype=jnp.float32), 'Wq': jax.random.normal(ks[1], (DIM, DIM), dtype=jnp.float32) * s, 'Wk': jax.random.normal(ks[2], (DIM, DIM), dtype=jnp.float32) * s, 'Wv': jax.random.normal(ks[3], (DIM, DIM), dtype=jnp.float32) * s, 'q_gamma': jnp.ones((HEAD_DIM,), jnp.float32), 'q_beta': jnp.zeros((HEAD_DIM,), jnp.float32), 'k_gamma': jnp.ones((HEAD_DIM,), jnp.float32), 'k_beta': jnp.zeros((HEAD_DIM,), jnp.float32), 'Wo': jax.random.normal(ks[4], (DIM, DIM), dtype=jnp.float32) * s, 'bo': jnp.zeros((DIM,), jnp.float32)}
    _L0_attn_all = _L0_attn_setup()
    _L0_attn_in = {k: v for k, v in _L0_attn_all.items() if k in ('Wq', 'Wk', 'Wv', 'q_gamma', 'q_beta', 'k_gamma', 'k_beta', 'Wo', 'bo')}
    del _L0_attn_all

    def _L0_xattn_setup():
        import jax, jax.numpy as jnp
        import numpy as np
        DIM = 256
        HEADS = 16
        DIM_HEAD = 64
        INNER = HEADS * DIM_HEAD
        EPS = 1e-05

        def _split_heads(t):
            b, n, _ = t.shape
            return t.reshape(b, n, HEADS, DIM_HEAD).transpose(0, 2, 1, 3)
        key = jax.random.key(seed)
        ks = jax.random.split(key, 9)
        b, n, m = (2, 512, 64)
        s = DIM ** (-0.5)
        return {'x': jax.random.normal(ks[0], (b, n, DIM), jnp.float32), 'memories': jax.random.normal(ks[1], (b, m, DIM), jnp.float32), 'ln_g': jnp.ones((DIM,), jnp.float32), 'ln_b': jnp.zeros((DIM,), jnp.float32), 'Wq': jax.random.normal(ks[2], (DIM, INNER), jnp.float32) * s, 'Wkv': jax.random.normal(ks[3], (DIM, 2 * INNER), jnp.float32) * s, 'Wm': jax.random.normal(ks[4], (DIM, INNER), jnp.float32) * s, 'Wo': jax.random.normal(ks[5], (INNER, DIM), jnp.float32) * s, 'bo': jnp.zeros((DIM,), jnp.float32)}
    _L0_xattn_all = _L0_xattn_setup()
    _L0_xattn_in = {k: v for k, v in _L0_xattn_all.items() if k in ('ln_g', 'ln_b', 'Wq', 'Wkv', 'Wm', 'Wo', 'bo')}
    del _L0_xattn_all

    def _L0_ffn_setup():
        import jax, jax.numpy as jnp
        import numpy as np
        D = 256
        H = 4
        DF = 1024
        E = 8
        EPS = 1e-05

        def _layer_norm(x, g, b):
            mu = jnp.mean(x, axis=-1, keepdims=True)
            var = jnp.mean(jnp.square(x - mu), axis=-1, keepdims=True)
            return (x - mu) * jax.lax.rsqrt(var + EPS) * g + b

        def _mha(x, Wqkv, bqkv, Wo, bo):
            S, B, _ = x.shape
            hd = D // H
            qkv = x @ Wqkv.T + bqkv
            q, k, v = jnp.split(qkv, 3, axis=-1)
            to_heads = lambda t: t.reshape(S, B, H, hd).transpose(1, 2, 0, 3)
            q, k, v = (to_heads(q), to_heads(k), to_heads(v))
            scores = jnp.einsum('bhqd,bhkd->bhqk', q, k) * (1.0 / np.sqrt(hd))
            att = jax.nn.softmax(scores, axis=-1)
            o = jnp.einsum('bhqk,bhkd->bhqd', att, v)
            o = o.transpose(2, 0, 1, 3).reshape(S, B, D)
            return o @ Wo.T + bo

        def _moe(x, Wg, W1, b1, W2, b2):
            S, B, _ = x.shape
            xf = x.reshape(S * B, D)
            logits = xf @ Wg.T
            idx = jnp.argmax(logits, axis=-1)
            out = jnp.zeros_like(xf)
            for e in range(E):
                m = (idx == e)[:, None].astype(xf.dtype)
                h = jax.nn.relu(xf @ W1[e] + b1[e])
                out = out + m * (h @ W2[e] + b2[e])
            return out.reshape(S, B, D)
        key = jax.random.key(seed)
        ks = jax.random.split(key, 16)
        S, B = (128, 8)
        s = lambda k, shape, fan: jax.random.normal(k, shape, jnp.float32) * (1.0 / np.sqrt(fan))
        return {'x': jax.random.normal(ks[0], (S, B, D), jnp.float32), 'Wqkv': s(ks[1], (3 * D, D), D), 'bqkv': jnp.zeros((3 * D,), jnp.float32), 'Wo': s(ks[2], (D, D), D), 'bo': jnp.zeros((D,), jnp.float32), 'g1': jnp.ones((D,), jnp.float32), 'be1': jnp.zeros((D,), jnp.float32), 'g2': jnp.ones((D,), jnp.float32), 'be2': jnp.zeros((D,), jnp.float32), 'Wg': s(ks[3], (E, D), D), 'W1': s(ks[4], (E, D, DF), D), 'b1': jnp.zeros((E, DF), jnp.float32), 'W2': s(ks[5], (E, DF, D), DF), 'b2': jnp.zeros((E, D), jnp.float32)}
    _L0_ffn_all = _L0_ffn_setup()
    _L0_ffn_in = {k: v for k, v in _L0_ffn_all.items() if k in ('Wqkv', 'bqkv', 'Wo', 'bo', 'g1', 'be1', 'g2', 'be2', 'Wg', 'W1', 'b1', 'W2', 'b2')}
    del _L0_ffn_all
    return {'x': x, 'ctx_1024': ctx_1024, 'L0_attn_Wq': _L0_attn_in['Wq'], 'L0_attn_Wk': _L0_attn_in['Wk'], 'L0_attn_Wv': _L0_attn_in['Wv'], 'L0_attn_q_gamma': _L0_attn_in['q_gamma'], 'L0_attn_q_beta': _L0_attn_in['q_beta'], 'L0_attn_k_gamma': _L0_attn_in['k_gamma'], 'L0_attn_k_beta': _L0_attn_in['k_beta'], 'L0_attn_Wo': _L0_attn_in['Wo'], 'L0_attn_bo': _L0_attn_in['bo'], 'L0_xattn_ln_g': _L0_xattn_in['ln_g'], 'L0_xattn_ln_b': _L0_xattn_in['ln_b'], 'L0_xattn_Wq': _L0_xattn_in['Wq'], 'L0_xattn_Wkv': _L0_xattn_in['Wkv'], 'L0_xattn_Wm': _L0_xattn_in['Wm'], 'L0_xattn_Wo': _L0_xattn_in['Wo'], 'L0_xattn_bo': _L0_xattn_in['bo'], 'L0_ffn_Wqkv': _L0_ffn_in['Wqkv'], 'L0_ffn_bqkv': _L0_ffn_in['bqkv'], 'L0_ffn_Wo': _L0_ffn_in['Wo'], 'L0_ffn_bo': _L0_ffn_in['bo'], 'L0_ffn_g1': _L0_ffn_in['g1'], 'L0_ffn_be1': _L0_ffn_in['be1'], 'L0_ffn_g2': _L0_ffn_in['g2'], 'L0_ffn_be2': _L0_ffn_in['be2'], 'L0_ffn_Wg': _L0_ffn_in['Wg'], 'L0_ffn_W1': _L0_ffn_in['W1'], 'L0_ffn_b1': _L0_ffn_in['b1'], 'L0_ffn_W2': _L0_ffn_in['W2'], 'L0_ffn_b2': _L0_ffn_in['b2']}

def reference(x, ctx_1024, L0_attn_Wq, L0_attn_Wk, L0_attn_Wv, L0_attn_q_gamma, L0_attn_q_beta, L0_attn_k_gamma, L0_attn_k_beta, L0_attn_Wo, L0_attn_bo, L0_xattn_ln_g, L0_xattn_ln_b, L0_xattn_Wq, L0_xattn_Wkv, L0_xattn_Wm, L0_xattn_Wo, L0_xattn_bo, L0_ffn_Wqkv, L0_ffn_bqkv, L0_ffn_Wo, L0_ffn_bo, L0_ffn_g1, L0_ffn_be1, L0_ffn_g2, L0_ffn_be2, L0_ffn_Wg, L0_ffn_W1, L0_ffn_b1, L0_ffn_W2, L0_ffn_b2):
    import jax
    import jax.numpy as jnp

    def _L0_attn_ref(x, Wq, Wk, Wv, q_gamma, q_beta, k_gamma, k_beta, Wo, bo):
        import math
        import jax, jax.numpy as jnp
        import numpy as np
        DIM = 256
        N_HEADS = 16
        HEAD_DIM = DIM // N_HEADS
        SEQ_LEN = 512
        BASE = 10000.0
        EPS = 1e-05

        def rope_cache(seq_len, dim):
            pos = jnp.arange(seq_len, dtype=jnp.float32)[:, None]
            di = jnp.arange(0, dim, 2, dtype=jnp.float32) / dim
            theta = pos * jnp.exp(-di * math.log(BASE))
            cos = jnp.repeat(jnp.cos(theta), 2, axis=1)
            sin = jnp.repeat(jnp.sin(theta), 2, axis=1)
            return (cos, sin)

        def rotate_half(x):
            x1 = x[..., ::2]
            x2 = x[..., 1::2]
            return jnp.concatenate((-x2, x1), axis=-1)

        def layernorm(x, gamma, beta):
            mu = jnp.mean(x, axis=-1, keepdims=True)
            var = jnp.var(x, axis=-1, keepdims=True)
            return (x - mu) * jax.lax.rsqrt(var + EPS) * gamma + beta
        B, S, D = x.shape
        H, hd = (N_HEADS, HEAD_DIM)
        q = (x @ Wq.T).reshape(B, S, H, hd).transpose(0, 2, 1, 3)
        k = (x @ Wk.T).reshape(B, S, H, hd).transpose(0, 2, 1, 3)
        v = (x @ Wv.T).reshape(B, S, H, hd).transpose(0, 2, 1, 3)
        q = layernorm(q, q_gamma, q_beta)
        k = layernorm(k, k_gamma, k_beta)
        cos, sin = rope_cache(S, hd)
        cos = cos[None, None]
        sin = sin[None, None]
        q = q * cos + rotate_half(q) * sin
        k = k * cos + rotate_half(k) * sin
        scale = 1.0 / math.sqrt(hd)
        scores = scale * jnp.einsum('bhqd,bhkd->bhqk', q, k)
        mask = jnp.tril(jnp.ones((S, S), dtype=bool))
        scores = jnp.where(mask, scores, -jnp.inf)
        attn = jax.nn.softmax(scores, axis=-1)
        out = jnp.einsum('bhqk,bhkd->bhqd', attn, v)
        out = out.transpose(0, 2, 1, 3).reshape(B, S, D)
        return out @ Wo.T + bo

    def _L0_xattn_ref(x, memories, ln_g, ln_b, Wq, Wkv, Wm, Wo, bo):
        import jax, jax.numpy as jnp
        import numpy as np
        DIM = 256
        HEADS = 16
        DIM_HEAD = 64
        INNER = HEADS * DIM_HEAD
        EPS = 1e-05

        def _split_heads(t):
            b, n, _ = t.shape
            return t.reshape(b, n, HEADS, DIM_HEAD).transpose(0, 2, 1, 3)
        mu = jnp.mean(x, axis=-1, keepdims=True)
        var = jnp.mean(jnp.square(x - mu), axis=-1, keepdims=True)
        xn = (x - mu) * jax.lax.rsqrt(var + EPS) * ln_g + ln_b
        q = _split_heads(xn @ Wq)
        kv = xn @ Wkv
        k = _split_heads(kv[..., :INNER])
        v = _split_heads(kv[..., INNER:])
        mem = _split_heads(memories @ Wm)
        k = jnp.concatenate([k, mem], axis=2)
        v = jnp.concatenate([v, mem], axis=2)
        scale = DIM_HEAD ** (-0.5)
        dots = jnp.einsum('bhid,bhjd->bhij', q, k) * scale
        attn = jax.nn.softmax(dots, axis=-1)
        out = jnp.einsum('bhij,bhjd->bhid', attn, v)
        b, h, n, d = out.shape
        out = out.transpose(0, 2, 1, 3).reshape(b, n, h * d)
        return out @ Wo + bo

    def _L0_ffn_ref(x, Wqkv, bqkv, Wo, bo, g1, be1, g2, be2, Wg, W1, b1, W2, b2):
        import jax, jax.numpy as jnp
        import numpy as np
        D = 256
        H = 4
        DF = 1024
        E = 8
        EPS = 1e-05

        def _layer_norm(x, g, b):
            mu = jnp.mean(x, axis=-1, keepdims=True)
            var = jnp.mean(jnp.square(x - mu), axis=-1, keepdims=True)
            return (x - mu) * jax.lax.rsqrt(var + EPS) * g + b

        def _mha(x, Wqkv, bqkv, Wo, bo):
            S, B, _ = x.shape
            hd = D // H
            qkv = x @ Wqkv.T + bqkv
            q, k, v = jnp.split(qkv, 3, axis=-1)
            to_heads = lambda t: t.reshape(S, B, H, hd).transpose(1, 2, 0, 3)
            q, k, v = (to_heads(q), to_heads(k), to_heads(v))
            scores = jnp.einsum('bhqd,bhkd->bhqk', q, k) * (1.0 / np.sqrt(hd))
            att = jax.nn.softmax(scores, axis=-1)
            o = jnp.einsum('bhqk,bhkd->bhqd', att, v)
            o = o.transpose(2, 0, 1, 3).reshape(S, B, D)
            return o @ Wo.T + bo

        def _moe(x, Wg, W1, b1, W2, b2):
            S, B, _ = x.shape
            xf = x.reshape(S * B, D)
            logits = xf @ Wg.T
            idx = jnp.argmax(logits, axis=-1)
            out = jnp.zeros_like(xf)
            for e in range(E):
                m = (idx == e)[:, None].astype(xf.dtype)
                h = jax.nn.relu(xf @ W1[e] + b1[e])
                out = out + m * (h @ W2[e] + b2[e])
            return out.reshape(S, B, D)
        y = _layer_norm(x + _mha(x, Wqkv, bqkv, Wo, bo), g1, be1)
        z = _layer_norm(y + _moe(y, Wg, W1, b1, W2, b2), g2, be2)
        return z
    x = x + _L0_attn_ref(_layernorm(x, axis=-1), L0_attn_Wq, L0_attn_Wk, L0_attn_Wv, L0_attn_q_gamma, L0_attn_q_beta, L0_attn_k_gamma, L0_attn_k_beta, L0_attn_Wo, L0_attn_bo)
    x = x + _L0_xattn_ref(_layernorm(x, axis=-1), ctx_1024, L0_xattn_ln_g, L0_xattn_ln_b, L0_xattn_Wq, L0_xattn_Wkv, L0_xattn_Wm, L0_xattn_Wo, L0_xattn_bo)
    x = x + _L0_ffn_ref(_layernorm(x, axis=-1), L0_ffn_Wqkv, L0_ffn_bqkv, L0_ffn_Wo, L0_ffn_bo, L0_ffn_g1, L0_ffn_be1, L0_ffn_g2, L0_ffn_be2, L0_ffn_Wg, L0_ffn_W1, L0_ffn_b1, L0_ffn_W2, L0_ffn_b2)
    return x

_drawn_inputs = setup_inputs


def setup_inputs(seed=0):
    import zlib

    import numpy as np

    out = dict(_drawn_inputs(seed))
    spreads = {'L0_attn_q_gamma': (1.0, 0.2),
     'L0_attn_q_beta': (0.0, 0.1),
     'L0_attn_k_gamma': (1.0, 0.2),
     'L0_attn_k_beta': (0.0, 0.1),
     'L0_attn_bo': (0.0, 0.1),
     'L0_xattn_ln_g': (1.0, 0.2),
     'L0_xattn_ln_b': (0.0, 0.1),
     'L0_xattn_bo': (0.0, 0.1),
     'L0_ffn_bqkv': (0.0, 0.1),
     'L0_ffn_bo': (0.0, 0.1),
     'L0_ffn_g1': (1.0, 0.2),
     'L0_ffn_be1': (0.0, 0.1),
     'L0_ffn_g2': (1.0, 0.2),
     'L0_ffn_be2': (0.0, 0.1),
     'L0_ffn_b1': (0.0, 0.286),
     'L0_ffn_b2': (0.0, 0.1)}
    factors = {}
    for name, (base, spread) in spreads.items():
        noise = np.random.default_rng([zlib.crc32(name.encode()), seed]).standard_normal(out[name].shape)
        drawn = base * np.exp(spread * noise) if base else spread * noise
        out[name] = jnp.asarray(drawn.astype(out[name].dtype))
    for name, factor in factors.items():
        out[name] = (out[name] * factor).astype(out[name].dtype)
    return out
```

```python
from contextlib import ExitStack

import numpy as np
import concourse.bass as bass
from concourse import mybir

F32 = mybir.dt.float32
F32R = mybir.dt.float32r
ALU = mybir.AluOpType
ACT = mybir.ActivationFunctionType
AX = mybir.AxisListType.X
ds = bass.ds

P = 128
B, S, D = 4, 512, 256
KT = D // P
TPB = S // P
NT = B * TPB
EPS = 1e-5

HA, DA = 16, 16
QUADS = HA // 4
TRI = [0, 128, 384, 768]
TRI_KEYS = [0, 512, 896, 1152]
TRI_LEN = 1280
HB, DB = 16, 64
CTX = 1024
KEYS = S + CTX
KC = KEYS // 512
KEY_TILES = KEYS // P
PAIRS = HB // 2
C_O, C_Y, C_ALL = 22, 29, 40
HC, DC = 4, 64
E, DF = 8, 1024
FT = DF // P


class Chain:

    def __init__(self, eng, sem, base, per, alone=None):
        self.alone = alone
        self.eng, self.sem, self.base, self.per, self.k = eng, sem, base, per, 0

    def link(self, ins):
        self.k += 1
        ins.then_inc(self.sem, 1)
        self.eng.wait_ge(self.sem, self.base + self.k + 1)
        if self.alone is not None:
            self.eng.sem_inc(self.alone, 1)

    def done(self):
        assert self.k == self.per, (self.k, self.per)


def build(nc, io, out, last_stage=3):
    top = ExitStack()
    with top:
        def sb(name, shape, dt=F32, ctx=top):
            return ctx.enter_context(nc.sbuf_tensor(name, shape, dt))

        def sem(name):
            return top.enter_context(nc.semaphore(name))

        ps = top.enter_context(nc.psum_tensor("ps", [P, 8, 512], F32))

        x_sb = sb("x_sb", [P, NT, D])
        ident = sb("ident", [P, P])
        ident_r = sb("ident_r", [P, P], F32R)
        mask = sb("mask", [P, P])
        mask_r = sb("mask_r", [P, P], F32R)
        neg_half = sb("neg_half", [P, P])
        stats = sb("stats", [P, TPB, 6])
        mv = sb("mv", [P, TPB, 2])
        ve = sb("ve", [P, TPB])
        rstd = sb("rstd", [P, TPB])
        ve2 = sb("ve2", [P, TPB])
        rstd2 = sb("rstd2", [P, TPB])
        xn = sb("xn", [P, TPB, D])

        ctx_a = ExitStack()
        wqkv_a = sb("wqkv_a", [P, KT, 3 * D], ctx=ctx_a)
        wo_a = sb("wo_a", [P, QUADS, D], ctx=ctx_a)
        bo_a = sb("bo_a", [P, D], ctx=ctx_a)
        rope_cos = sb("rope_cos", [P, TPB, DA], ctx=ctx_a)
        rope_sin = sb("rope_sin", [P, TPB, DA], ctx=ctx_a)
        gb = sb("gb", [P, 8, DA], ctx=ctx_a)
        t_cos = sb("t_cos", [P, TPB, 2, DA], ctx=ctx_a)
        t_sin = sb("t_sin", [P, TPB, 2, DA], ctx=ctx_a)
        t_add = sb("t_add", [P, TPB, 2, DA], ctx=ctx_a)
        t_add2 = sb("t_add2", [P, TPB, 2, DA], ctx=ctx_a)
        xnT_a = sb("xnT_a", [P, KT, S], ctx=ctx_a)
        qk = sb("qk", [P, TPB, 2 * D], ctx=ctx_a)
        cen = sb("cen", [P, TPB, 2 * D], ctx=ctx_a)
        sq = sb("sq", [P, TPB, 2 * D], ctx=ctx_a)
        qkr = sb("qkr", [P, TPB, 2 * D], ctx=ctx_a)
        v_nat = sb("v_nat", [P, TPB, D], ctx=ctx_a)
        hsum = sb("hsum", [P, TPB * 32], ctx=ctx_a)
        hmean = sb("hmean", [P, TPB * 32], ctx=ctx_a)
        hvar = sb("hvar", [P, TPB * 32], ctx=ctx_a)
        hrstd = sb("hrstd", [P, TPB * 32], ctx=ctx_a)
        q_st = sb("q_st", [P, TPB, 4, 4 * DA], F32R, ctx=ctx_a)
        k_st = sb("k_st", [P, TPB, 4, 4 * DA], F32R, ctx=ctx_a)
        qT_a = sb("qT_a", [P, 2, S], F32R, ctx=ctx_a)
        kT_a = sb("kT_a", [P, 2, S], F32R, ctx=ctx_a)
        v_pad = sb("v_pad", [P, TPB, 4, 32], ctx=ctx_a)
        prob_a = sb("prob_a", [P, 2, TRI_LEN], ctx=ctx_a)
        probT_a = sb("probT_a", [P, 4, TRI_LEN], ctx=ctx_a)
        nmax_a = sb("nmax_a", [P, 4, TPB], ctx=ctx_a)
        rsum_a = sb("rsum_a", [P, 4, TPB], ctx=ctx_a)
        rinv_a = sb("rinv_a", [P, 4, TPB], ctx=ctx_a)
        oT_a = sb("oT_a", [P, S], ctx=ctx_a)
        ctx_a.close()

        ctx_b = ExitStack()
        xnT = sb("xnT", [P, KT, NT * P], ctx=ctx_b)
        lng = sb("lng", [P, KT], ctx=ctx_b)
        lnb = sb("lnb", [P, KT], ctx=ctx_b)
        bo_b = sb("bo_b", [P, D], ctx=ctx_b)
        wq_s = sb("wq_s", [P, KT, P], ctx=ctx_b)
        wk_s = sb("wk_s", [P, KT, P], ctx=ctx_b)
        wv_s = sb("wv_s", [P, KT, P], ctx=ctx_b)
        wm_s = sb("wm_s", [P, KT, P], ctx=ctx_b)
        wo_s = sb("wo_s", [P, D], ctx=ctx_b)
        memT = sb("memT", [P, KT, CTX], ctx=ctx_b)
        q_dup = sb("q_dup", [P, 2, 2, S], F32R, ctx=ctx_b)
        k_st2 = sb("k_st2", [P, 2, KEYS], F32R, ctx=ctx_b)
        kv_f = sb("kv_f", [P, 4, 512], ctx=ctx_b)
        v_b = sb("v_b", [P, KEY_TILES, P], ctx=ctx_b)
        prob = sb("prob", [P, 2, KEYS], ctx=ctx_b)
        probT = sb("probT", [P, 2, KEY_TILES, S], ctx=ctx_b)
        nmax = sb("nmax", [P, 8], ctx=ctx_b)
        rsum = sb("rsum", [P, 8], ctx=ctx_b)
        rinv = sb("rinv", [P, 8], ctx=ctx_b)
        oT = sb("oT", [P, S], ctx=ctx_b)
        ctx_b.close()

        yT = sb("yT", [P, KT, NT * P])
        y_sb = sb("y_sb", [P, NT, D])
        emask = sb("emask", [P, NT, E])
        g2 = sb("g2", [P, D])
        be2 = sb("be2", [P, D])
        ctx_c = ExitStack()
        wqkv_c = sb("wqkv_c", [P, KT, 3 * D], ctx=ctx_c)
        wo_c = sb("wo_c", [P, KT, D], ctx=ctx_c)
        wg_c = sb("wg_c", [P, KT, E], ctx=ctx_c)
        bqkv = sb("bqkv", [P, 3 * D], ctx=ctx_c)
        bo_c = sb("bo_c", [P, D], ctx=ctx_c)
        g1 = sb("g1", [P, D], ctx=ctx_c)
        be1 = sb("be1", [P, D], ctx=ctx_c)
        rank = sb("rank", [P, E], ctx=ctx_c)
        uT = sb("uT", [P, KT, S], ctx=ctx_c)
        qkv = sb("qkv", [P, TPB, 3 * D], ctx=ctx_c)
        prod = sb("prod", [P, B, D], ctx=ctx_c)
        prod2 = sb("prod2", [P, B, D], ctx=ctx_c)
        sc = sb("sc", [P, B, B, HC], ctx=ctx_c)
        scm = sb("scm", [P, B, HC], ctx=ctx_c)
        scs = sb("scs", [P, B, HC], ctx=ctx_c)
        o_c = sb("o_c", [P, B, D], ctx=ctx_c)
        r_c = sb("r_c", [P, B, D], ctx=ctx_c)
        oT_c = sb("oT_c", [P, KT, S], ctx=ctx_c)
        yT_c = sb("yT_c", [P, KT, S], ctx=ctx_c)
        lg = sb("lg", [P, B, E], ctx=ctx_c)
        lgm = sb("lgm", [P, B], ctx=ctx_c)
        lge = sb("lge", [P, B, E], ctx=ctx_c)
        lgi = sb("lgi", [P, B], ctx=ctx_c)
        ctx_c.close()
        w1 = sb("w1", [P, 2, KT, DF])
        w2 = sb("w2", [P, 2, FT, D])
        b1 = sb("b1", [P, E, FT])
        b2 = sb("b2", [P, E, D])
        hT = sb("hT", [P, FT, S])
        moe_t = sb("moe_t", [P, 2, D])
        z = sb("z", [P, TPB, D])

        load_x = sem("load_x")
        load_a = sem("load_a")
        load_b = sem("load_b")
        load_c = sem("load_c")
        load_e = sem("load_e")
        stage_end = sem("stage_end")
        alone = sem("alone")
        const_set = sem("const_set")
        counters = []

        def counter(name):
            counters.append(sem(name))
            return counters[-1]

        dve_setup = counter("dve_setup")
        ln_dve = [counter(f"ln_dve_{s}") for s in "abc"]
        ln_var = [counter(f"ln_var_{s}") for s in "abc"]
        ln_rstd = [counter(f"ln_rstd_{s}") for s in "abc"]
        ln_xn = [counter(f"ln_xn_{s}") for s in "abc"]
        ln_tr = [counter(f"ln_tr_{s}") for s in "abc"]
        ln_xnT = [counter(f"ln_xnT_{s}") for s in "abc"]
        bias_added = [counter(f"bias_added_{s}") for s in "abc"]
        a_qk_ps, a_v_ps, a_qk, a_v = counter("a_qk_ps"), counter("a_v_ps"), counter("a_qk"), counter("a_v")
        a_cen, a_sq, a_hvar, a_hrstd = counter("a_cen"), counter("a_sq"), counter("a_hvar"), counter("a_hrstd")
        a_norm_qk, a_rot, a_rope = counter("a_norm_qk"), counter("a_rot"), counter("a_rope")
        a_hi, a_lo, a_tr = counter("a_hi"), counter("a_lo"), counter("a_tr")
        a_T_act, a_T_dve = counter("a_T_act"), counter("a_T_dve")
        a_s, a_max, a_exp, a_rinv, a_prob = counter("a_s"), counter("a_max"), counter("a_exp"), counter("a_rinv"), counter("a_prob")
        a_pt, a_pt_act, a_pt_dve = counter("a_pt"), counter("a_pt_act"), counter("a_pt_dve")
        a_vpad, a_pv, a_o, a_y, a_x = counter("a_vpad"), counter("a_pv"), counter("a_o"), counter("a_y"), counter("a_x")
        b_w, b_wo, b_mem = counter("b_w"), counter("b_wo"), counter("b_mem")
        b_pq, b_pv_ps = counter("b_pq"), counter("b_pv_ps")
        b_hi, b_lo, b_kv, b_vtr, b_v = counter("b_hi"), counter("b_lo"), counter("b_kv"), counter("b_vtr"), counter("b_v")
        b_khi_act, b_khi_dve = counter("b_khi_act"), counter("b_khi_dve")
        b_s, b_max, b_exp, b_rinv, b_prob = counter("b_s"), counter("b_max"), counter("b_exp"), counter("b_rinv"), counter("b_prob")
        b_pt, b_pt_act, b_pt_dve = counter("b_pt"), counter("b_pt_act"), counter("b_pt_dve")
        b_out, b_o, b_y, b_x = counter("b_out"), counter("b_o"), counter("b_y"), counter("b_x")
        c_qk_ps, c_dve, c_exp_in, c_exp = counter("c_qk_ps"), counter("c_dve"), counter("c_exp_in"), counter("c_exp")
        c_otr, c_oT, c_proj, c_var, c_rstd = counter("c_otr"), counter("c_oT"), counter("c_proj"), counter("c_var"), counter("c_rstd")
        c_ytr, c_yT, c_yTg, c_lg = counter("c_ytr"), counter("c_yT"), counter("c_yTg"), counter("c_lg")
        e_w, e_h_ps, e_h, e_o_ps, e_o, e_t = [counter("e_w0"), counter("e_w1")], counter("e_h_ps"), counter("e_h"), counter("e_o_ps"), counter("e_o"), counter("e_t")
        z_dve, z_var, z_rstd, z_out, stored = counter("z_dve"), counter("z_var"), counter("z_rstd"), counter("z_out"), counter("stored")

        block = top.enter_context(nc.Block())
        ENGINES = 5

        def end_stage(eng, n):
            eng.drain().then_inc(stage_end, 1)
            eng.wait_ge(stage_end, ENGINES * n)

        def cast(ap):
            return ap.bitcast(F32)


        def ln_stats(v, s, j, tiles, chained=1):
            per = 3 + 2 * (chained - 1)
            c = Chain(v, ln_dve[s], j * per, per, alone)
            for t in range(TPB):
                last = v.bn_stats(stats[:, t, :], tiles(t))
            c.link(last)
            for t in range(TPB):
                last = v.bn_aggr(mv[:, t, :], stats[:, t, :])
            c.link(last)
            v.tensor_scalar(ve[:, :], mv[:, :, 1], EPS, None, ALU.add).then_inc(ln_var[s], 1)
            v.wait_ge(ln_rstd[s], j * chained + 2)
            if chained == 2:
                c.link(v.tensor_tensor(ve2[:, :], mv[:, :, 1], rstd[:, :], ALU.mult))
                c.link(v.tensor_tensor(ve2[:, :], ve2[:, :], rstd[:, :], ALU.mult))
                v.tensor_scalar(ve2[:, :], ve2[:, :], EPS, None, ALU.add).then_inc(ln_var[s], 1)
                v.wait_ge(ln_rstd[s], j * chained + 2 + 1)
                c.link(v.tensor_tensor(rstd[:, :], rstd[:, :], rstd2[:, :], ALU.mult))
            else:
                c.link(v.tensor_copy(rstd2[:, :], rstd[:, :]))
            c.done()
            v.wait_ge(ln_tr[s], j * KT + 1)
            for t in range(TPB):
                last = v.tensor_scalar(xn[:, t, :], tiles(t), mv[:, t, 0:1], rstd[:, t:t + 1],
                                       ALU.subtract, ALU.mult)
            last.then_inc(ln_xn[s], 1)

        def ln_power(g, s, j, chained=1):
            g.wait_ge(ln_var[s], j * chained + 2)
            if chained == 2:
                g.wait_ge(ln_xn[s], j + 1)
            g.tensor_tensor(rstd[:, :], ve[:, :], neg_half[:, 0:TPB], ALU.pow).then_inc(ln_rstd[s], 1)
            if chained == 2:
                g.wait_ge(ln_var[s], j * chained + 2 + 1)
                g.tensor_tensor(rstd2[:, :], ve2[:, :], neg_half[:, 0:TPB], ALU.pow).then_inc(ln_rstd[s], 1)

        def ln_transpose(pe, s, j, bank):
            pe.wait_ge(ln_xn[s], j + 2)
            for k in range(KT):
                for t in range(TPB):
                    last = pe.transpose(ps[:, bank + k, t * P:(t + 1) * P], xn[:, t, k * P:(k + 1) * P], ident[:, :])
                last.then_inc(ln_tr[s], 1)

        def row(ap, n):
            return ap.rearrange("(a n) -> a n", a=1).broadcast_to([P, n])

        @block.sync
        def _(sp):
            sp.dma_start(x_sb[:, :, :], io["x"].rearrange("(t p) d -> p t d", p=P)).then_inc(load_x, 16)
            sp.dma_start(ident[:, :], io["ident"]).then_inc(load_a, 16)
            sp.dma_start(mask[:, :], io["mask"]).then_inc(load_a, 16)
            sp.dma_start(wqkv_a[:, :, :], io["a_wqkv"].rearrange("(k p) n -> p k n", p=P)).then_inc(load_a, 16)
            sp.dma_start(rope_cos[:, :, :], io["cos"].rearrange("(t p) d -> p t d", p=P)).then_inc(load_a, 16)
            sp.dma_start(rope_sin[:, :, :], io["sin"].rearrange("(t p) d -> p t d", p=P)).then_inc(load_a, 16)
            sp.dma_start(gb[:, :, :].rearrange("p a d -> p (a d)"), row(io["gb"], 8 * DA)).then_inc(load_a, 16)
            sp.dma_start(bo_a[:, :], row(io["a_bo"], D)).then_inc(load_a, 16)
            for c in counters:
                sp.sem_inc(c, 1)
            sp.wait_ge(const_set, 1)
            for h in range(4):
                sp.dma_start(wo_a[32 * h:32 * h + DA, :, :],
                             io["a_wo"].rearrange("(g h d) n -> h d g n", h=4, d=DA)[h]).then_inc(load_a, 16)
            end_stage(sp, 1)
            if last_stage >= 2:
                sp.dma_start(lng[:, :], io["ln_g"]).then_inc(load_b, 16)
                sp.dma_start(lnb[:, :], io["ln_b"]).then_inc(load_b, 16)
                sp.dma_start(bo_b[:, :], row(io["b_bo"], D)).then_inc(load_b, 16)
                with sp.Fori(0, B * PAIRS) as i:
                    b = sp.snap(i // PAIRS)
                    hp = sp.snap(i % PAIRS)
                    sp.wait_ge(b_pv_ps, i + 1)
                    for w_s, name in ((wq_s, "b_wq"), (wk_s, "b_wk"), (wv_s, "b_wv"), (wm_s, "b_wm")):
                        sp.dma_start(w_s[:, :, :], io[name].rearrange("(k p) (h n) -> h p k n", p=P, n=P)[hp])\
                            .then_inc(b_w, 16)
                    sp.dma_start(memT[:, :, :], io["ctxT"].rearrange("b (k p) n -> b p k n", p=P)[b])\
                        .then_inc(b_mem, 16)
                    sp.wait_ge(b_y, i + 1)
                    sp.dma_start(wo_s[:, :], io["b_wo"].rearrange("(h p) n -> h p n", p=P)[hp]).then_inc(b_wo, 16)
            end_stage(sp, 2)
            if last_stage >= 3:
                for dst, src in ((wqkv_c, "c_wqkv"), (wo_c, "c_wo"), (wg_c, "c_wg")):
                    sp.dma_start(dst[:, :, :], io[src].rearrange("(k p) n -> p k n", p=P)).then_inc(load_c, 16)
                for dst, src, n in ((bqkv, "c_bqkv", 3 * D), (bo_c, "c_bo", D), (g1, "c_g1", D), (be1, "c_be1", D),
                                    (g2, "c_g2", D), (be2, "c_be2", D), (rank, "rank", E)):
                    sp.dma_start(dst[:, :], row(io[src], n)).then_inc(load_c, 16)
            end_stage(sp, 3)
            if last_stage >= 3:
                sp.dma_start(b1[:, :, :], io["b1"]).then_inc(load_e, 16)
                sp.dma_start(b2[:, :, :].rearrange("p e d -> p (e d)"), row(io["b2"], E * D)).then_inc(load_e, 16)
                with sp.Fori(0, E // 2) as i:
                    for q in range(2):
                        sp.wait_ge(e_o_ps, i * 32 + 1)
                        sp.dma_start(w1[:, q, :, :], io["w1"].rearrange("(i q) (k p) n -> i q p k n", q=2, p=P)[i, q])\
                            .then_inc(e_w[q], 16)
                        sp.dma_start(w2[:, q, :, :], io["w2"].rearrange("(i q) (f p) n -> i q p f n", q=2, p=P)[i, q])\
                            .then_inc(e_w[q], 16)
            outv = out.rearrange("(j t p) d -> j p t d", t=TPB, p=P)
            with sp.Fori(0, B) as j:
                sp.wait_ge(z_out, j + 2)
                sp.dma_start(outv[j], z[:, :, :]).then_inc(stored, 16)
            sp.wait_ge(stored, 16 * B + 1)

        @block.gpsimd
        def _(g):
            g.memset(wo_a[:, :, :], 0.0).then_inc(const_set, 1)
            g.memset(neg_half[:, :], -0.5).then_inc(const_set, 1)
            g.memset(v_pad[:, :, :, :], 0.0).then_inc(const_set, 1)
            g.wait_ge(const_set, 3)
            g.wait_ge(load_a, 16 * 11)
            with g.Fori(0, B) as b:
                ln_power(g, 0, b)
                g.wait_ge(ln_xn[0], b + 2)
                g.tensor_tensor(x_sb[:, ds(b * TPB, TPB), :], x_sb[:, ds(b * TPB, TPB), :],
                                bo_a[:, :].unsqueeze(1).broadcast_to([P, TPB, D]), ALU.add).then_inc(bias_added[0], 1)
                g.wait_ge(a_hvar, b + 2)
                g.tensor_tensor(hrstd[:, :], hvar[:, :], neg_half[:, :], ALU.pow).then_inc(a_hrstd, 1)
                g.wait_ge(a_norm_qk, b + 2)
                nv = qk[:, :, :].rearrange("p t (c h d two) -> p (t c) h d two", c=2, h=HA, two=2)
                for half in range(2):
                    mv2 = cen[:, :, :].rearrange("p t (c h e d) -> p (t c) h e d", c=2, h=HA, e=2)[:, :, :, half, :]
                    ts = t_sin[:, :, :, :].rearrange("p t c (e d) -> p (t c) e d", e=2)[:, :, half, :]
                    g.tensor_tensor(mv2, nv[:, :, :, :, 1 - half],
                                    ts.unsqueeze(2).broadcast_to([P, 2 * TPB, HA, DA // 2]), ALU.mult)\
                        .then_inc(a_rot, 1)
                with g.Fori(0, QUADS) as q:
                    n = g.snap(b * QUADS + q)
                    g.wait_ge(a_v, b + 2)
                    g.wait_ge(a_pv, n + 1)
                    g.tensor_copy(v_pad[:, :, :, 0:DA],
                                  v_nat[:, :, ds(q * 64, 64)].rearrange("p t (h d) -> p t h d", h=4)).then_inc(a_vpad, 1)
                    for h in range(4):
                        g.wait_ge(a_rinv, n * 4 + h + 2)
                        g.sem_inc(alone, 1)
                        for qt in range(TPB):
                            pr = prob_a[:, h % 2, TRI[qt]:TRI[qt] + (qt + 1) * P]
                            g.tensor_scalar(pr, pr, rinv_a[:, h, qt:qt + 1], 1.0, ALU.mult, ALU.mult)\
                                .then_inc(a_prob, 1)
            end_stage(g, 1)
            if last_stage >= 2:
                g.wait_ge(load_b, 48)
                with g.Fori(0, B) as b:
                    ln_power(g, 1, b, 2)
                    g.wait_ge(ln_xn[1], b + 2)
                    g.tensor_tensor(x_sb[:, ds(b * TPB, TPB), :], x_sb[:, ds(b * TPB, TPB), :],
                                    bo_b[:, :].unsqueeze(1).broadcast_to([P, TPB, D]), ALU.add)\
                        .then_inc(bias_added[1], 1)
                with g.Fori(0, B * PAIRS) as i:
                    for u in range(8):
                        g.wait_ge(b_rinv, i * 8 + u + 2)
                        g.sem_inc(alone, 1)
                        g.tensor_scalar(prob[:, u % 2, :], prob[:, u % 2, :], rinv[:, u:u + 1], 1.0, ALU.mult, ALU.mult)\
                            .then_inc(b_prob, 1)
            end_stage(g, 2)
            if last_stage >= 3:
                g.wait_ge(load_c, 160)
                with g.Fori(0, TPB) as p:
                    ln_power(g, 2, p)
                    g.wait_ge(ln_xn[2], p + 2)
                    g.wait_ge(c_var, p + 2)
                    g.tensor_tensor(rstd2[:, :], ve2[:, :], neg_half[:, 0:TPB], ALU.pow).then_inc(c_rstd, 1)
                    g.wait_ge(c_yT, (p + 1) * 2 + 1)
                    for s in range(B):
                        g.tensor_copy(yT[:, :, ds((s * TPB + p) * P, P)], yT_c[:, :, s * P:(s + 1) * P]).then_inc(c_yTg, 1)
            end_stage(g, 3)
            if last_stage >= 3:
                with g.Fori(0, B) as j:
                    g.wait_ge(z_var, j + 2)
                    g.tensor_tensor(rstd2[:, :], ve2[:, :], neg_half[:, 0:TPB], ALU.pow).then_inc(z_rstd, 1)

        @block.scalar
        def _(a):
            a.wait_ge(load_x, 16)
            with a.Fori(0, B) as b:
                a.wait_ge(a_qk_ps, b * 4 + 1)
                for k in range(KT):
                    a.wait_ge(ln_tr[0], b * KT + k + 2)
                    a.activation(xnT_a[:, k, :], ps[:, 6 + k, :], ACT.Copy).then_inc(ln_xnT[0], 1)
                a.wait_ge(a_qk_ps, b * 4 + 4 + 1)
                a.activation(qk[:, :, :], ps[:, 0:4, :], ACT.Copy).then_inc(a_qk, 1)
                a.wait_ge(a_cen, b + 2)
                a.activation(sq[:, :, :], cen[:, :, :], ACT.Square).then_inc(a_sq, 1)
                with a.Fori(0, QUADS) as q:
                    n = a.snap(b * QUADS + q)
                    a.wait_ge(a_rope, b * 6 + 6 + 1)
                    a.wait_ge(a_tr, n * 4 + 1)
                    for c, (st, places) in enumerate(((q_st, (0, 2)), (k_st, (0, 1)))):
                        src = qkr[:, :, ds(q * 64 + c * D, 64)].rearrange("p t (h d) -> p t h d", h=4)
                        for e in places:
                            a.activation(st[:, :, :, e * DA:(e + 1) * DA], src, ACT.Copy).then_inc(a_hi, 1)
                    a.wait_ge(a_tr, n * 4 + 2)
                    a.activation(qT_a[:, 0, :], ps[:, 2, :], ACT.Copy).then_inc(a_T_act, 1)
                    a.wait_ge(a_tr, n * 4 + 3 + 1)
                    a.activation(kT_a[:, 0, :], ps[:, 4, :], ACT.Copy).then_inc(a_T_act, 1)

                    def exps(h):
                        a.wait_ge(a_max, n * 4 + h + 2)
                        base = 3 * (h % 2)
                        for qt in range(TPB):
                            bank, off = (base, TRI[qt]) if qt < 2 else (base + qt - 1, 0)
                            last = a.activation(prob_a[:, h % 2, TRI[qt]:TRI[qt] + (qt + 1) * P],
                                                ps[:, bank, off:off + (qt + 1) * P], ACT.Exp,
                                                bias=nmax_a[:, h, qt:qt + 1], accum_out=rsum_a[:, h, qt:qt + 1])
                        last.then_inc(a_exp, 1)

                    exps(0)
                    exps(1)
                    for h in range(4):
                        a.wait_ge(a_pt, n * 12 + 3 * h + 2)
                        a.wait_ge(a_pv, n + 1)
                        a.activation(probT_a[:, h, 0:512], ps[:, 6 + (3 * h) % 2, :], ACT.Copy).then_inc(a_pt_act, 1)
                        if h < 2:
                            a.wait_ge(a_pt, n * 12 + 3 * h + 3 + 1)
                            exps(h + 2)
                    a.wait_ge(a_pv, n + 2)
                    a.activation(oT_a[:, :], ps[:, 6, :], ACT.Copy).then_inc(a_o, 1)
            end_stage(a, 1)
            if last_stage >= 2:
                a.wait_ge(load_b, 48)
                with a.Fori(0, B) as b:
                    for k in range(KT):
                        a.wait_ge(ln_tr[1], b * KT + k + 2)
                        a.activation(xnT[:, k, ds(b * S, S)], ps[:, 6 + k, :], ACT.Identity,
                                     bias=lnb[:, k:k + 1], scale=lng[:, k:k + 1]).then_inc(ln_xnT[1], 1)
                with a.Fori(0, B * PAIRS) as i:
                    a.wait_ge(b_pq, i + 2)
                    for h in range(2):
                        for half in range(2):
                            a.activation(q_dup[64 * half:64 * half + 64, h, 0, :], ps[64 * h:64 * h + 64, 6, :],
                                         ACT.Copy, scale=DB ** -0.5).then_inc(b_hi, 1)
                    a.wait_ge(b_pv_ps, i + 2)
                    a.activation(kv_f[:, :, :], ps[:, 0:4, :], ACT.Copy).then_inc(b_kv, 1)
                    a.wait_ge(b_kv, i + 2)
                    a.activation(k_st2[0:64, 0, :], kv_f[0:64, 0:3, :], ACT.Copy).then_inc(b_khi_act, 1)
                    a.wait_ge(b_vtr, i * 3 + 2)
                    a.activation(v_b[:, 0:4, :], ps[:, 4, :], ACT.Copy).then_inc(b_v, 1)
                    a.wait_ge(b_vtr, i * 3 + 2 + 1)
                    a.activation(v_b[:, 4:8, :], ps[:, 5, :], ACT.Copy).then_inc(b_v, 1)

                    def exp(u):
                        a.wait_ge(b_max, i * 8 + u + 2)
                        a.activation(prob[:, u % 2, :], ps[:, 3 * (u % 2):3 * (u % 2) + 3, :], ACT.Exp,
                                     bias=nmax[:, u:u + 1], accum_out=rsum[:, u:u + 1]).then_inc(b_exp, 1)

                    exp(0)
                    exp(1)
                    for u in range(8):
                        for c in (0, 2):
                            a.wait_ge(b_pt, i * 24 + 3 * u + c + 2)
                            a.activation(probT[:, u // 4, 4 * c:4 * c + 4, (u % 4) * P:(u % 4 + 1) * P],
                                         ps[:, 6 + (3 * u + c) % 2, :], ACT.Copy).then_inc(b_pt_act, 1)
                        if u < 6:
                            exp(u + 2)
                    a.wait_ge(b_out, i + 2)
                    a.activation(oT[:, :], ps[:, 0, :], ACT.Copy).then_inc(b_o, 1)
            end_stage(a, 2)
            if last_stage >= 3:
                with a.Fori(0, TPB) as p:
                    for k in range(KT):
                        a.wait_ge(ln_tr[2], p * KT + k + 2)
                        a.wait_ge(c_qk_ps, p + 1)
                        a.activation(uT[:, k, :], ps[:, 6 + k, :], ACT.Copy).then_inc(ln_xnT[2], 1)
                    a.wait_ge(c_exp_in, p + 2)
                    a.activation(sc[:, :, :, :], sc[:, :, :, :], ACT.Exp, scale=DC ** -0.5).then_inc(c_exp, 1)
                    for k in range(KT):
                        a.wait_ge(c_otr, p * KT + k + 2)
                        a.activation(oT_c[:, k, :], ps[:, 6 + k, :], ACT.Copy).then_inc(c_oT, 1)
                    a.wait_ge(c_yTg, p * 4 + 1)
                    for k in range(KT):
                        a.wait_ge(c_ytr, p * KT + k + 2)
                        a.activation(yT_c[:, k, :], ps[:, 6 + k, :], ACT.Copy).then_inc(c_yT, 1)
            end_stage(a, 3)
            if last_stage >= 3:
                a.wait_ge(load_e, 32)
                with a.Fori(0, E // 2) as i:
                    for q in range(2):
                        with a.Fori(0, B) as c:
                            n = a.snap(i * 8 + q * 4 + c)
                            a.wait_ge(e_o_ps, n * 4 + 1)
                            for f in range(FT):
                                a.wait_ge(e_h_ps, n * FT + f + 2)
                                a.activation(hT[:, f, :], ps[:, f % 4, :], ACT.Relu,
                                             bias=b1[:, ds(i * 2 + q, 1), f]).then_inc(e_h, 1)

        @block.vector
        def _(v):
            v.wait_ge(load_a, 16 * 11)
            v.wait_ge(load_x, 16)
            v.wait_ge(const_set, 3)
            c = Chain(v, dve_setup, 0, 8)
            c.link(v.tensor_copy(ident_r[:, :], ident[:, :]))
            c.link(v.tensor_copy(mask_r[:, :], mask[:, :]))
            gbv = gb[:, :, :].rearrange("p (a c) d -> p a c d", c=2)
            c.link(v.tensor_scalar(gbv[:, :, 0, :], gbv[:, :, 0, :], DA ** -0.5, None, ALU.mult))
            full = [P, TPB, 2, DA]

            def table(dst, trig, r):
                return v.tensor_tensor(dst[:, :, :, :], trig[:, :, :].unsqueeze(2).broadcast_to(full),
                                       gb[:, 2 * r:2 * r + 2, :].unsqueeze(1).broadcast_to(full), ALU.mult)

            c.link(table(t_cos, rope_cos, 0))
            c.link(table(t_sin, rope_sin, 1))
            c.link(table(t_add, rope_cos, 2))
            c.link(table(t_add2, rope_sin, 3))
            c.link(v.tensor_tensor(t_add[:, :, :, :], t_add[:, :, :, :], t_add2[:, :, :, :], ALU.add))
            c.done()

            heads = lambda ap: ap[:, :, :].rearrange("p t (h d) -> p (t h) d", d=DA)
            heads4 = lambda ap: ap[:, :, :].rearrange("p t (c h d) -> p (t c) h d", c=2, h=HA)
            tab = lambda ap: ap[:, :, :, :].rearrange("p t c d -> p (t c) d").unsqueeze(2).broadcast_to([P, 8, HA, DA])
            wide = lambda ap: ap[:, :].unsqueeze(2).broadcast_to([P, TPB * 32, DA])
            with v.Fori(0, B) as b:
                ln_stats(v, 0, b, lambda t: x_sb[:, b * TPB + t, :])
                v.wait_ge(a_v_ps, b + 2)
                v.wait_ge(a_vpad, b * QUADS + 1)
                v.tensor_copy(v_nat[:, :, :], ps[:, 4:6, :].rearrange("p a n -> p (a n)")
                              .rearrange("p (t n) -> p t n", n=D)).then_inc(a_v, 1)
                v.wait_ge(a_qk, b + 2)
                c = Chain(v, a_rope, b * 6, 6)
                c.link(v.tensor_reduce(hsum[:, :], heads(qk), AX, ALU.add))
                c.link(v.tensor_scalar(hmean[:, :], hsum[:, :], 1.0 / DA, None, ALU.mult))
                v.tensor_tensor(heads(cen), heads(qk), wide(hmean), ALU.subtract).then_inc(a_cen, 1)
                v.wait_ge(a_sq, b + 2)
                c.link(v.tensor_reduce(hsum[:, :], heads(sq), AX, ALU.add))
                v.tensor_scalar(hvar[:, :], hsum[:, :], 1.0 / DA, EPS, ALU.mult, ALU.add).then_inc(a_hvar, 1)
                v.wait_ge(a_hrstd, b + 2)
                v.tensor_tensor(heads(qk), heads(cen), wide(hrstd), ALU.mult).then_inc(a_norm_qk, 1)
                v.wait_ge(a_norm_qk, b + 2)
                c.link(v.tensor_tensor(heads4(sq), heads4(qk), tab(t_cos), ALU.mult))
                v.wait_ge(a_rot, b * 2 + 2 + 1)
                v.wait_ge(a_hi, b * 16 + 1)
                c.link(v.tensor_tensor(qkr[:, :, :], sq[:, :, :], cen[:, :, :], ALU.add))
                c.link(v.tensor_tensor(heads4(qkr), heads4(qkr), tab(t_add), ALU.add))
                c.done()
                v.sem_inc(alone, 1)
                with v.Fori(0, QUADS) as q:
                    n = v.snap(b * QUADS + q)
                    k = 0
                    for c2, (st, hi, places) in enumerate(((q_st, 0, (1, 3)), (k_st, 0, (2, 3)))):
                        src = qkr[:, :, ds(q * 64 + c2 * D, 64)].rearrange("p t (h d) -> p t h d", h=4)
                        v.wait_ge(a_hi, n * 4 + 2 * c2 + 2)
                        v.wait_ge(a_tr, n * 4 + 1)
                        for e in places:
                            v.tensor_tensor(st[:, :, :, e * DA:(e + 1) * DA], src,
                                            cast(st[:, :, :, 0:DA]), ALU.subtract).then_inc(a_lo, 1)
                    v.wait_ge(a_tr, n * 4 + 2 + 1)
                    v.tensor_copy(qT_a[:, 1, :], ps[:, 3, :]).then_inc(a_T_dve, 1)
                    v.wait_ge(a_tr, n * 4 + 4 + 1)
                    v.tensor_copy(kT_a[:, 1, :], ps[:, 5, :]).then_inc(a_T_dve, 1)

                    def maxes(h):
                        v.wait_ge(a_s, n * 4 + h + 2)
                        base = 3 * (h % 2)
                        for qt in range(TPB):
                            bank, off = (base, TRI[qt]) if qt < 2 else (base + qt - 1, 0)
                            last = v.tensor_reduce(nmax_a[:, h, qt:qt + 1], ps[:, bank, off:off + (qt + 1) * P],
                                                   AX, ALU.max, negate=True)
                        last.then_inc(a_max, 1)

                    def inverse(h):
                        v.wait_ge(a_exp, n * 4 + h + 2)
                        v.reciprocal(rinv_a[:, h, :], rsum_a[:, h, :]).then_inc(a_rinv, 1)

                    maxes(0)
                    maxes(1)
                    inverse(0)
                    for h in range(4):
                        if h < 3:
                            inverse(h + 1) if h == 0 else None
                        for j in (1, 2):
                            cc = 3 * h + j
                            v.wait_ge(a_pt, n * 12 + cc + 2)
                            v.wait_ge(a_pv, n + 1)
                            v.tensor_copy(probT_a[:, h, 512 + 384 * (j - 1):512 + 384 * j], ps[:, 6 + cc % 2, 0:384])\
                                .then_inc(a_pt_dve, 1)
                        if h < 2:
                            maxes(h + 2)
                            inverse(h + 2)
                    v.wait_ge(a_y, n + 2)
                    v.wait_ge(bias_added[0], b + 2)
                    xb = x_sb[:, ds(b * TPB, TPB), :]
                    v.tensor_tensor(xb, ps[:, 0:2, :].rearrange("p a n -> p (a n)").rearrange("p (t n) -> p t n", n=D),
                                    xb, ALU.add).then_inc(a_x, 1)
                    v.wait_ge(a_x, n + 2)
            end_stage(v, 1)
            if last_stage >= 2:
                with v.Fori(0, B) as b:
                    ln_stats(v, 1, b, lambda t: x_sb[:, b * TPB + t, :], 2)
                v.wait_ge(bias_added[1], B + 1)
                with v.Fori(0, B * PAIRS) as i:
                    b = v.snap(i // PAIRS)
                    for h in range(2):
                        v.wait_ge(b_hi, i * 4 + 4 + 1)
                        for half in range(2):
                            v.scalar_tensor_tensor(q_dup[64 * half:64 * half + 64, h, 1, :],
                                                   ps[64 * h:64 * h + 64, 6, :], DB ** -0.5,
                                                   cast(q_dup[64 * h:64 * h + 64, h, 0, :]), ALU.mult, ALU.subtract)\
                                .then_inc(b_lo, 1)
                    v.wait_ge(b_kv, i + 2)
                    v.tensor_copy(k_st2[64:128, 1, :], kv_f[64:128, 0:3, :].rearrange("p a n -> p (a n)"))\
                        .then_inc(b_khi_dve, 1)
                    for h in (1, 0):
                        v.wait_ge((b_khi_act, b_khi_dve)[h], i + 2)
                        o = 64 * (1 - h)
                        v.tensor_tensor(k_st2[o:o + 64, h, :], kv_f[64 * h:64 * h + 64, 0:3, :].rearrange("p a n -> p (a n)"),
                                        cast(k_st2[64 * h:64 * h + 64, h, :]), ALU.subtract).then_inc(b_lo, 1)
                    v.wait_ge(b_vtr, i * 3 + 3 + 1)
                    v.tensor_copy(v_b[:, 8:12, :], ps[:, 7, :]).then_inc(b_v, 1)

                    def rowmax(u):
                        v.wait_ge(b_s, i * 8 + u + 2)
                        v.tensor_reduce(nmax[:, u:u + 1], ps[:, 3 * (u % 2):3 * (u % 2) + 3, :]
                                        .rearrange("p a n -> p (a n)"), AX, ALU.max, negate=True).then_inc(b_max, 1)

                    def inverse_b(u):
                        v.wait_ge(b_exp, i * 8 + u + 2)
                        v.reciprocal(rinv[:, u:u + 1], rsum[:, u:u + 1]).then_inc(b_rinv, 1)

                    rowmax(0)
                    rowmax(1)
                    inverse_b(0)
                    for u in range(8):
                        if u < 7:
                            inverse_b(u + 1)
                        cc = 3 * u + 1
                        v.wait_ge(b_pt, i * 24 + cc + 2)
                        v.tensor_copy(probT[:, u // 4, 4:8, (u % 4) * P:(u % 4 + 1) * P],
                                      ps[:, 6 + cc % 2, :].rearrange("p (a n) -> p a n", a=4)).then_inc(b_pt_dve, 1)
                        if u < 6:
                            rowmax(u + 2)
                    v.wait_ge(b_y, i + 2)
                    xb = x_sb[:, ds(b * TPB, TPB), :]
                    v.tensor_tensor(xb, ps[:, 1:3, :].rearrange("p a n -> p (a n)").rearrange("p (t n) -> p t n", n=D),
                                    xb, ALU.add).then_inc(b_x, 1)
                    v.wait_ge(b_x, i + 2)
            end_stage(v, 2)
            if last_stage >= 3:
                v.wait_ge(load_c, 160)
                with v.Fori(0, TPB) as p:
                    ln_stats(v, 2, p, lambda t: x_sb[:, t * TPB + p, :])
                    c = Chain(v, c_dve, p * C_ALL, C_ALL, alone)
                    v.wait_ge(c_qk_ps, p + 2)
                    c.link(v.tensor_tensor(qkv[:, :, 0:2 * D], ps[:, 0:4, :],
                                           bqkv[:, 0:2 * D].unsqueeze(1).broadcast_to([P, B, 2 * D]), ALU.add))
                    c.link(v.tensor_tensor(qkv[:, :, 2 * D:3 * D], ps[:, 4:6, :].rearrange("p a n -> p (a n)")
                                           .rearrange("p (t n) -> p t n", n=D),
                                           bqkv[:, 2 * D:3 * D].unsqueeze(1).broadcast_to([P, B, D]), ALU.add))
                    for s in range(B):
                        c.link(v.tensor_tensor(prod[:, :, :], qkv[:, :, D:2 * D],
                                               qkv[:, s, 0:D].unsqueeze(1).broadcast_to([P, B, D]), ALU.mult))
                        c.link(v.tensor_reduce(sc[:, s, :, :], prod[:, :, :].rearrange("p s (h d) -> p s h d", h=HC),
                                               AX, ALU.add))
                    c.link(v.tensor_reduce(scm[:, :, :], sc[:, :, :, :].rearrange("p s k h -> p s h k"), AX, ALU.max))
                    v.tensor_tensor(sc[:, :, :, :], sc[:, :, :, :], scm[:, :, :].unsqueeze(2)
                                    .broadcast_to([P, B, B, HC]), ALU.subtract).then_inc(c_exp_in, 1)
                    v.wait_ge(c_exp, p + 2)
                    c.link(v.tensor_reduce(scs[:, :, :], sc[:, :, :, :].rearrange("p s k h -> p s h k"), AX, ALU.add))
                    c.link(v.reciprocal(scs[:, :, :], scs[:, :, :]))
                    c.link(v.tensor_tensor(sc[:, :, :, :], sc[:, :, :, :], scs[:, :, :].unsqueeze(2)
                                           .broadcast_to([P, B, B, HC]), ALU.mult))
                    for s in range(B):
                        for k in range(B):
                            last = v.tensor_tensor(prod2[:, k, :].rearrange("p (h d) -> p h d", h=HC),
                                                   qkv[:, k, 2 * D:3 * D].rearrange("p (h d) -> p h d", h=HC),
                                                   sc[:, s, k, :].unsqueeze(2).broadcast_to([P, HC, DC]), ALU.mult)
                        c.link(last)
                        c.link(v.tensor_reduce(o_c[:, s, :], prod2[:, :, :].rearrange("p k n -> p n k"), AX, ALU.add))
                    assert c.k == C_O
                    v.wait_ge(c_proj, p + 2)
                    c.link(v.tensor_tensor(r_c[:, :, :], xn[:, :, :], ps[:, 0:2, :].rearrange("p a n -> p (a n)")
                                           .rearrange("p (t n) -> p t n", n=D), ALU.add))
                    c.link(v.tensor_tensor(r_c[:, :, :], r_c[:, :, :], bo_c[:, :].unsqueeze(1)
                                           .broadcast_to([P, B, D]), ALU.add))
                    for t in range(B):
                        last = v.bn_stats(stats[:, t, :], r_c[:, t, :])
                    c.link(last)
                    for t in range(B):
                        last = v.bn_aggr(mv[:, t, :], stats[:, t, :])
                    c.link(last)
                    v.tensor_scalar(ve2[:, :], mv[:, :, 1], EPS, None, ALU.add).then_inc(c_var, 1)
                    v.wait_ge(c_rstd, p + 2)
                    for t in range(B):
                        last = v.tensor_scalar(r_c[:, t, :], r_c[:, t, :], mv[:, t, 0:1], rstd2[:, t:t + 1],
                                               ALU.subtract, ALU.mult)
                    c.link(last)
                    c.link(v.tensor_tensor(r_c[:, :, :], r_c[:, :, :], g1[:, :].unsqueeze(1)
                                           .broadcast_to([P, B, D]), ALU.mult))
                    c.link(v.tensor_tensor(r_c[:, :, :], r_c[:, :, :], be1[:, :].unsqueeze(1)
                                           .broadcast_to([P, B, D]), ALU.add))
                    assert c.k == C_Y
                    c.link(v.tensor_copy(y_sb[:, :, :].rearrange("p (s q) d -> p q s d", s=B)[:, ds(p, 1), :, :]
                                         .rearrange("p a s d -> p (a s) d"), r_c[:, :, :]))
                    v.wait_ge(c_lg, p + 2)
                    c.link(v.tensor_copy(lg[:, :, :], ps[:, 4, 0:B * E].rearrange("p (s e) -> p s e", e=E)))
                    c.link(v.tensor_reduce(lgm[:, :], lg[:, :, :], AX, ALU.max))
                    c.link(v.tensor_tensor(lge[:, :, :], lg[:, :, :], lgm[:, :].unsqueeze(2)
                                           .broadcast_to([P, B, E]), ALU.is_equal))
                    c.link(v.tensor_scalar(lge[:, :, :], lge[:, :, :], -float(E), float(E), ALU.mult, ALU.add))
                    c.link(v.tensor_tensor(lge[:, :, :], lge[:, :, :], rank[:, :].unsqueeze(1)
                                           .broadcast_to([P, B, E]), ALU.add))
                    c.link(v.tensor_reduce(lgi[:, :], lge[:, :, :], AX, ALU.min))
                    for s in range(B):
                        c.link(v.tensor_scalar(emask[:, ds(s * TPB + p, 1), :].rearrange("p a e -> p (a e)"),
                                               rank[:, :], lgi[:, s:s + 1], None, ALU.is_equal))
                    c.done()
            end_stage(v, 3)
            if last_stage >= 3:
                v.wait_ge(load_e, 32)
                with v.Fori(0, E // 2) as i:
                    for q in range(2):
                        with v.Fori(0, B) as c4:
                            n = v.snap(i * 8 + q * 4 + c4)
                            ex = v.snap(i * 2 + q)
                            for t in range(TPB):
                                v.wait_ge(e_o_ps, n * 4 + t + 2)
                                v.tensor_tensor(moe_t[:, t % 2, :], ps[:, 4 + t, 0:D],
                                                b2[:, ds(ex, 1), :].rearrange("p a d -> p (a d)"), ALU.add)\
                                    .then_inc(e_t, 1)
                                v.wait_ge(e_t, n * 4 + t + 2)
                                yt = y_sb[:, ds(c4 * TPB + t, 1), :].rearrange("p a d -> p (a d)")
                                v.scalar_tensor_tensor(yt, moe_t[:, t % 2, :],
                                                       emask[:, ds(c4 * TPB + t, 1), ds(ex, 1)].rearrange("p a e -> p (a e)"),
                                                       yt, ALU.mult, ALU.add).then_inc(e_o, 1)
                v.wait_ge(e_o, E * NT + 1)
                with v.Fori(0, B) as j:
                    c = Chain(v, z_dve, j * 5, 5, alone)
                    yt = lambda t: y_sb[:, j * TPB + t, :]
                    for t in range(TPB):
                        last = v.bn_stats(stats[:, t, :], yt(t))
                    c.link(last)
                    for t in range(TPB):
                        last = v.bn_aggr(mv[:, t, :], stats[:, t, :])
                    c.link(last)
                    v.tensor_scalar(ve2[:, :], mv[:, :, 1], EPS, None, ALU.add).then_inc(z_var, 1)
                    v.wait_ge(z_rstd, j + 2)
                    v.wait_ge(stored, j * 16 + 1)
                    for t in range(TPB):
                        last = v.tensor_scalar(z[:, t, :], yt(t), mv[:, t, 0:1], rstd2[:, t:t + 1],
                                               ALU.subtract, ALU.mult)
                    c.link(last)
                    c.link(v.tensor_tensor(z[:, :, :], z[:, :, :], g2[:, :].unsqueeze(1)
                                           .broadcast_to([P, TPB, D]), ALU.mult))
                    c.link(v.tensor_tensor(z[:, :, :], z[:, :, :], be2[:, :].unsqueeze(1)
                                           .broadcast_to([P, TPB, D]), ALU.add))
                    c.done()
                    v.tensor_tensor(z[:, :, :], z[:, :, :], x_sb[:, ds(j * TPB, TPB), :], ALU.add).then_inc(z_out, 1)
            else:
                with v.Fori(0, B) as j:
                    v.wait_ge(stored, j * 16 + 1)
                    v.tensor_copy(z[:, :, :], x_sb[:, ds(j * TPB, TPB), :]).then_inc(z_out, 1)

        @block.tensor
        def _(pe):
            pe.wait_ge(load_a, 16 * 11)
            pe.wait_ge(dve_setup, 9)
            with pe.Fori(0, B) as b:
                pe.wait_ge(a_x, b * QUADS + 1)
                ln_transpose(pe, 0, b, 6)
                pe.wait_ge(ln_xnT[0], b * KT + 2 + 1)
                for t in range(TPB):
                    for k in range(KT):
                        last = pe.matmul(ps[:, t, :], xnT_a[:, k, t * P:(t + 1) * P], wqkv_a[:, k, 0:2 * D],
                                         start=k == 0, stop=k == KT - 1)
                    last.then_inc(a_qk_ps, 1)
                for t in range(TPB):
                    for k in range(KT):
                        last = pe.matmul(ps[:, 4 + t // 2, (t % 2) * D:(t % 2 + 1) * D],
                                         xnT_a[:, k, t * P:(t + 1) * P], wqkv_a[:, k, 2 * D:3 * D],
                                         start=k == 0, stop=k == KT - 1)
                last.then_inc(a_v_ps, 1)
                with pe.Fori(0, QUADS) as q:
                    n = pe.snap(b * QUADS + q)
                    pe.wait_ge(a_hi, n * 4 + 4 + 1)
                    pe.wait_ge(a_lo, n * 4 + 4 + 1)
                    pe.wait_ge(a_qk, b + 2)
                    pe.wait_ge(a_v, b + 2)
                    for bank, st, hp in ((2, q_st, 0), (3, q_st, 1), (4, k_st, 0), (5, k_st, 1)):
                        for t in range(TPB):
                            last = pe.transpose(ps[:, bank, t * P:(t + 1) * P],
                                                cast(st[:, t, 2 * hp:2 * hp + 2, :].rearrange("p h d -> p (h d)")),
                                                ident[:, :])
                        last.then_inc(a_tr, 1)

                    def scores(h):
                        hp, rows = h // 2, slice(64 * (h % 2), 64 * (h % 2) + 64)
                        base = 3 * (h % 2)
                        for qt in range(TPB):
                            bank, off = (base, TRI[qt]) if qt < 2 else (base + qt - 1, 0)
                            pe.matmul(ps[:, bank, off:off + (qt + 1) * P], qT_a[rows, hp, qt * P:(qt + 1) * P],
                                      kT_a[rows, hp, 0:(qt + 1) * P], start=True, stop=False)
                            last = pe.matmul(ps[:, bank, off + qt * P:off + (qt + 1) * P], ident_r[:, :], mask_r[:, :],
                                             start=False, stop=True)
                        last.then_inc(a_s, 1)

                    pe.wait_ge(a_T_act, n * 2 + 2 + 1)
                    pe.wait_ge(a_x, n + 1)
                    scores(0)
                    pe.wait_ge(a_T_dve, n * 2 + 2 + 1)
                    scores(1)
                    for h in range(4):
                        pe.wait_ge(a_prob, n * 16 + 4 * h + 4 + 1)
                        for j, blocks in enumerate(([(0, 0), (0, 1), (0, 2), (0, 3)], [(1, 1), (1, 2), (1, 3)],
                                                    [(2, 2), (2, 3), (3, 3)])):
                            if j == 2:
                                pe.wait_ge(a_pt_act, n * 4 + h + 2)
                            elif h > 0:
                                pe.wait_ge(a_pt_dve, n * 8 + 2 * (h - 1) + j + 2)
                            elif j == 0:
                                pe.wait_ge(a_o, n + 1)
                            for m, (kt, qt) in enumerate(blocks):
                                last = pe.transpose(ps[:, 6 + (3 * h + j) % 2, m * P:(m + 1) * P],
                                                    prob_a[:, h % 2, TRI[qt] + kt * P:TRI[qt] + (kt + 1) * P], ident[:, :])
                            last.then_inc(a_pt, 1)
                        if h < 2:
                            pe.wait_ge(a_exp, n * 4 + h + 2)
                            scores(h + 2)
                    pe.wait_ge(a_pt_act, n * 4 + 4 + 1)
                    pe.wait_ge(a_pt_dve, n * 8 + 8 + 1)
                    pe.wait_ge(a_vpad, n + 2)
                    for kt in range(TPB):
                        for h in range(4):
                            last = pe.matmul(ps[32 * h:32 * h + 32, 6, kt * P:S], v_pad[:, kt, h, :],
                                             probT_a[:, h, TRI_KEYS[kt]:TRI_KEYS[kt] + S - kt * P],
                                             start=kt == 0, stop=kt == TPB - 1)
                    last.then_inc(a_pv, 1)
                    pe.wait_ge(a_o, n + 2)
                    for t in range(TPB):
                        last = pe.matmul(ps[:, t // 2, (t % 2) * D:(t % 2 + 1) * D], oT_a[:, t * P:(t + 1) * P],
                                         wo_a[:, ds(q, 1), :].rearrange("p a n -> p (a n)"), start=True, stop=True)
                    last.then_inc(a_y, 1)
            end_stage(pe, 1)
            if last_stage >= 2:
                with pe.Fori(0, B) as b:
                    pe.wait_ge(ln_xnT[1], b * KT + 1)
                    ln_transpose(pe, 1, b, 6)
                pe.wait_ge(ln_xnT[1], B * KT + 1)
                with pe.Fori(0, B * PAIRS) as i:
                    b = pe.snap(i // PAIRS)
                    pe.wait_ge(b_x, i + 1)
                    pe.wait_ge(b_o, i + 1)
                    pe.wait_ge(b_w, i * 64 + 64 + 1)
                    pe.wait_ge(b_mem, i * 16 + 16 + 1)

                    def project(bank, w_s, rhs):
                        for k in range(KT):
                            last = pe.matmul(ps[:, bank, :], w_s[:, k, :], rhs(k), start=k == 0, stop=k == KT - 1)
                        return last

                    own = lambda k: xnT[:, k, ds(b * S, S)]
                    project(6, wq_s, own).then_inc(b_pq, 1)
                    project(0, wk_s, own)
                    project(1, wm_s, lambda k: memT[:, k, 0:512])
                    project(2, wm_s, lambda k: memT[:, k, 512:1024])
                    project(3, wv_s, own).then_inc(b_pv_ps, 1)
                    pe.wait_ge(b_kv, i + 2)
                    pe.wait_ge(b_lo, i * 6 + 4 + 1)
                    for c, bank in enumerate((4, 5, 7)):
                        for m in range(4):
                            last = pe.transpose(ps[:, bank, m * P:(m + 1) * P], kv_f[:, (3, 1, 2)[c], m * P:(m + 1) * P],
                                                ident[:, :])
                        last.then_inc(b_vtr, 1)

                    def scores_b(u):
                        h, qt = u // 4, u % 4
                        for c in range(KC):
                            for part in range(2):
                                last = pe.matmul(ps[:, 3 * (u % 2) + c, :], q_dup[:, h, part, qt * P:(qt + 1) * P],
                                                 k_st2[:, h, c * 512:(c + 1) * 512], start=part == 0, stop=part == 1)
                        last.then_inc(b_s, 1)

                    pe.wait_ge(b_khi_act, i + 2)
                    pe.wait_ge(b_lo, i * 6 + 6 + 1)
                    scores_b(0)
                    pe.wait_ge(b_v, i * 3 + 3 + 1)
                    scores_b(1)
                    for u in range(8):
                        pe.wait_ge(b_prob, i * 8 + u + 2)
                        for c in range(3):
                            cc = 3 * u + c
                            if cc >= 2:
                                pu, pc = (cc - 2) // 3, (cc - 2) % 3
                                if pc == 1:
                                    pe.wait_ge(b_pt_dve, i * 8 + pu + 2)
                                else:
                                    pe.wait_ge(b_pt_act, i * 16 + 2 * pu + (1 if pc == 0 else 2) + 1)
                            for m in range(4):
                                last = pe.transpose(ps[:, 6 + cc % 2, m * P:(m + 1) * P],
                                                    prob[:, u % 2, (4 * c + m) * P:(4 * c + m + 1) * P], ident[:, :])
                            last.then_inc(b_pt, 1)
                        if u < 6:
                            pe.wait_ge(b_exp, i * 8 + u + 2)
                            scores_b(u + 2)
                    pe.wait_ge(b_pt_act, i * 16 + 16 + 1)
                    pe.wait_ge(b_pt_dve, i * 8 + 8 + 1)
                    for kt in range(KEY_TILES):
                        for h in range(2):
                            last = pe.matmul(ps[64 * h:64 * h + 64, 0, :], v_b[:, kt, 64 * h:64 * h + 64],
                                             probT[:, h, kt, :], start=kt == 0, stop=kt == KEY_TILES - 1)
                    last.then_inc(b_out, 1)
                    pe.wait_ge(b_o, i + 2)
                    pe.wait_ge(b_wo, i * 16 + 16 + 1)
                    for t in range(TPB):
                        last = pe.matmul(ps[:, 1 + t // 2, (t % 2) * D:(t % 2 + 1) * D], oT[:, t * P:(t + 1) * P],
                                         wo_s[:, :], start=True, stop=True)
                    last.then_inc(b_y, 1)
            end_stage(pe, 2)
            if last_stage >= 3:
                pe.wait_ge(load_c, 160)
                with pe.Fori(0, TPB) as p:
                    pe.wait_ge(c_yT, p * KT + 1)
                    ln_transpose(pe, 2, p, 6)
                    pe.wait_ge(ln_xnT[2], p * KT + 2 + 1)
                    pe.wait_ge(c_dve, p * C_ALL + 1)
                    for t in range(B):
                        for k in range(KT):
                            pe.matmul(ps[:, t, :], uT[:, k, t * P:(t + 1) * P], wqkv_c[:, k, 0:2 * D],
                                      start=k == 0, stop=k == KT - 1)
                    for t in range(B):
                        for k in range(KT):
                            last = pe.matmul(ps[:, 4 + t // 2, (t % 2) * D:(t % 2 + 1) * D],
                                             uT[:, k, t * P:(t + 1) * P], wqkv_c[:, k, 2 * D:3 * D],
                                             start=k == 0, stop=k == KT - 1)
                    last.then_inc(c_qk_ps, 1)
                    pe.wait_ge(c_dve, p * C_ALL + C_O + 1)
                    for k in range(KT):
                        for t in range(B):
                            last = pe.transpose(ps[:, 6 + k, t * P:(t + 1) * P], o_c[:, t, k * P:(k + 1) * P], ident[:, :])
                        last.then_inc(c_otr, 1)
                    pe.wait_ge(c_oT, p * KT + 2 + 1)
                    for t in range(B):
                        for k in range(KT):
                            last = pe.matmul(ps[:, t // 2, (t % 2) * D:(t % 2 + 1) * D], oT_c[:, k, t * P:(t + 1) * P],
                                             wo_c[:, k, :], start=k == 0, stop=k == KT - 1)
                    last.then_inc(c_proj, 1)
                    pe.wait_ge(c_dve, p * C_ALL + C_Y + 1)
                    for k in range(KT):
                        for t in range(B):
                            last = pe.transpose(ps[:, 6 + k, t * P:(t + 1) * P], r_c[:, t, k * P:(k + 1) * P], ident[:, :])
                        last.then_inc(c_ytr, 1)
                    pe.wait_ge(c_yT, p * KT + 2 + 1)
                    for t in range(B):
                        for k in range(KT):
                            last = pe.matmul(ps[:, 4, t * E:(t + 1) * E], yT_c[:, k, t * P:(t + 1) * P], wg_c[:, k, :],
                                             start=k == 0, stop=k == KT - 1)
                    last.then_inc(c_lg, 1)
            end_stage(pe, 3)
            if last_stage >= 3:
                with pe.Fori(0, E // 2) as i:
                    for q in range(2):
                        pe.wait_ge(e_w[q], i * 32 + 32 + 1)
                        pe.sem_inc(alone, 1)
                        with pe.Fori(0, B) as c:
                            n = pe.snap(i * 8 + q * 4 + c)
                            for f in range(FT):
                                if f >= 4:
                                    pe.wait_ge(e_h, n * FT + f - 3 + 1)
                                for k in range(KT):
                                    last = pe.matmul(ps[:, f % 4, :], w1[:, q, k, f * P:(f + 1) * P],
                                                     yT[:, k, ds(c * S, S)], start=k == 0, stop=k == KT - 1)
                                last.then_inc(e_h_ps, 1)
                            pe.wait_ge(e_h, n * FT + FT + 1)
                            for t in range(TPB):
                                pe.wait_ge(e_t, n * 4 + 1)
                                for f in range(FT):
                                    last = pe.matmul(ps[:, 4 + t, 0:D], hT[:, f, t * P:(t + 1) * P], w2[:, q, f, :],
                                                     start=f == 0, stop=f == FT - 1)
                                last.then_inc(e_o_ps, 1)


def layout(inputs):
    a = {k: np.ascontiguousarray(np.asarray(v)) for k, v in inputs.items()}
    pos = np.arange(S, dtype=np.float32)[:, None]
    di = np.arange(0, DA, 2, dtype=np.float32) / np.float32(DA)
    theta = pos * np.exp(-di * np.float32(np.log(10000.0))).astype(np.float32)
    cos = np.repeat(np.cos(theta), 2, axis=1).astype(np.float32)
    sin = np.repeat(np.sin(theta), 2, axis=1).astype(np.float32)
    sign = np.concatenate([-np.ones(DA // 2), np.ones(DA // 2)]).astype(np.float32)
    turn = lambda w: np.concatenate([w[1::2], w[::2]])
    qg, qb, kg, kb = (a["L0_attn_" + n] for n in ("q_gamma", "q_beta", "k_gamma", "k_beta"))
    inner = HB * DB
    return {
        "x": a["x"].reshape(B * S, D),
        "ident": np.eye(P, dtype=np.float32),
        "mask": np.triu(np.full((P, P), -1e30, np.float32), 1),
        "cos": cos, "sin": sin * sign,
        "gb": np.concatenate([qg, kg, turn(qg), turn(kg), qb, kb, turn(qb), turn(kb)]),
        "a_wqkv": np.concatenate([a["L0_attn_Wq"].T, a["L0_attn_Wk"].T, a["L0_attn_Wv"].T], axis=1),
        "a_wo": a["L0_attn_Wo"].T, "a_bo": a["L0_attn_bo"],
        "ctxT": a["ctx_1024"].transpose(0, 2, 1),
        "ln_g": a["L0_xattn_ln_g"].reshape(KT, P).T, "ln_b": a["L0_xattn_ln_b"].reshape(KT, P).T, "b_bo": a["L0_xattn_bo"],
        "b_wq": a["L0_xattn_Wq"], "b_wk": a["L0_xattn_Wkv"][:, :inner], "b_wv": a["L0_xattn_Wkv"][:, inner:],
        "b_wm": a["L0_xattn_Wm"], "b_wo": a["L0_xattn_Wo"],
        "c_wqkv": a["L0_ffn_Wqkv"].T, "c_wo": a["L0_ffn_Wo"].T, "c_wg": a["L0_ffn_Wg"].T,
        "c_bqkv": a["L0_ffn_bqkv"], "c_bo": a["L0_ffn_bo"],
        "c_g1": a["L0_ffn_g1"], "c_be1": a["L0_ffn_be1"], "c_g2": a["L0_ffn_g2"], "c_be2": a["L0_ffn_be2"],
        "rank": np.arange(E, dtype=np.float32),
        "w1": a["L0_ffn_W1"], "b1": a["L0_ffn_b1"].reshape(E, FT, P).transpose(2, 0, 1), "w2": a["L0_ffn_W2"], "b2": a["L0_ffn_b2"].reshape(E * D),
    }


def kernel(**inputs):
    import concourse.bacc as _bacc
    from concourse.bass_utils import run_bass_kernel_spmd as _run

    nc = _bacc.Bacc("TRN2", target_bir_lowering=False, num_devices=1)
    arrays, io = {}, {}
    for name, v in layout(inputs).items():
        v = np.ascontiguousarray(v)
        arrays["in_" + name] = v
        io[name] = nc.dram_tensor("in_" + name, v.shape, mybir.dt.from_np(v.dtype), kind="ExternalInput").ap()
    out = nc.dram_tensor("out_0", (B * S, D), F32, kind="ExternalOutput").ap()
    build(nc, io, out)
    r = _run(nc, [arrays], core_ids=[0])
    return r.results[0]["out_0"].reshape(B, S, D)
```

```python
from contextlib import ExitStack

import numpy as np
import concourse.bass as bass
from concourse import mybir

F32 = mybir.dt.float32
F32R = mybir.dt.float32r
ALU = mybir.AluOpType
ACT = mybir.ActivationFunctionType
AX = mybir.AxisListType.X
ds = bass.ds

P = 128
B, S, D = 4, 512, 256
KT = D // P
TPB = S // P
NT = B * TPB
EPS = 1e-5

HA, DA = 16, 16
QUADS = HA // 4
NQ = B * QUADS
TRI = [0, 128, 384, 768]
TRI_KEYS = [0, 512, 896, 1152]
TRI_LEN = 1280
HB, DB = 16, 64
CTX = 1024
KEYS = S + CTX
TRI_BLOCKS = [[(0, 0), (0, 1), (0, 2), (0, 3)], [(1, 1), (1, 2), (1, 3)], [(2, 2), (2, 3), (3, 3)]]
KC = KEYS // 512
KEY_TILES = KEYS // P
PAIRS = HB // 2
CHUNKS = 27
NPROB = 4
UNITS = 2 * TPB
C_O, C_Y, C_ALL = 22, 29, 40
HC, DC = 4, 64
E, DF = 8, 1024
FT = DF // P


class Chain:

    def __init__(self, eng, sem, base, per, alone=None):
        self.alone = alone
        self.eng, self.sem, self.base, self.per, self.k = eng, sem, base, per, 0

    def link(self, ins):
        self.k += 1
        ins.then_inc(self.sem, 1)
        self.eng.wait_ge(self.sem, self.base + self.k + 1)
        if self.alone is not None:
            self.eng.sem_inc(self.alone, 1)

    def done(self):
        assert self.k == self.per, (self.k, self.per)


def build(nc, io, out, last_stage=3):
    top = ExitStack()
    with top:
        def sb(name, shape, dt=F32, ctx=top):
            return ctx.enter_context(nc.sbuf_tensor(name, shape, dt))

        def sem(name):
            return top.enter_context(nc.semaphore(name))

        ps = top.enter_context(nc.psum_tensor("ps", [P, 8, 512], F32))

        x_sb = sb("x_sb", [P, NT, D])
        ident = sb("ident", [P, P])
        ident_r = sb("ident_r", [P, P], F32R)
        mask = sb("mask", [P, P])
        mask_r = sb("mask_r", [P, P], F32R)
        neg_half = sb("neg_half", [P, P])
        stats = sb("stats", [P, TPB, 6])
        mv = sb("mv", [P, TPB, 2])
        ve = sb("ve", [P, TPB])
        rstd = sb("rstd", [P, TPB])
        ve2 = sb("ve2", [P, TPB])
        rstd2 = sb("rstd2", [P, TPB])
        xn = sb("xn", [P, TPB, D])

        ctx_a = ExitStack()
        wqkv_a = sb("wqkv_a", [P, KT, 3 * D], ctx=ctx_a)
        wo_a = sb("wo_a", [P, QUADS, D], ctx=ctx_a)
        bo_a = sb("bo_a", [P, D], ctx=ctx_a)
        rope_cos = sb("rope_cos", [P, TPB, DA], ctx=ctx_a)
        rope_sin = sb("rope_sin", [P, TPB, DA], ctx=ctx_a)
        gb = sb("gb", [P, 8, DA], ctx=ctx_a)
        t_cos = sb("t_cos", [P, TPB, 2, DA], ctx=ctx_a)
        t_sin = sb("t_sin", [P, TPB, 2, DA], ctx=ctx_a)
        t_add = sb("t_add", [P, TPB, 2, DA], ctx=ctx_a)
        t_add2 = sb("t_add2", [P, TPB, 2, DA], ctx=ctx_a)
        xnT_a = sb("xnT_a", [P, KT, S], ctx=ctx_a)
        qk = sb("qk", [P, TPB, 2 * D], ctx=ctx_a)
        cen = sb("cen", [P, TPB, 2 * D], ctx=ctx_a)
        sq = sb("sq", [P, TPB, 2 * D], ctx=ctx_a)
        qkr = sb("qkr", [P, NT, 2 * D], ctx=ctx_a)
        v_nat = sb("v_nat", [P, NT, D], ctx=ctx_a)
        hsum = sb("hsum", [P, TPB * 32], ctx=ctx_a)
        hmean = sb("hmean", [P, TPB * 32], ctx=ctx_a)
        hvar = sb("hvar", [P, TPB * 32], ctx=ctx_a)
        hrstd = sb("hrstd", [P, TPB * 32], ctx=ctx_a)
        q_st = sb("q_st", [P, TPB, 4, 4 * DA], F32R, ctx=ctx_a)
        k_st = sb("k_st", [P, TPB, 4, 4 * DA], F32R, ctx=ctx_a)
        qT_a = sb("qT_a", [P, 2, S], F32R, ctx=ctx_a)
        kT_a = sb("kT_a", [P, 2, S], F32R, ctx=ctx_a)
        v_pad = sb("v_pad", [P, TPB, 4, 32], ctx=ctx_a)
        prob_a = sb("prob_a", [P, 4, TRI_LEN], ctx=ctx_a)
        probT_a = sb("probT_a", [P, 4, TRI_LEN], ctx=ctx_a)
        nmax_a = sb("nmax_a", [P, 4, TPB], ctx=ctx_a)
        rsum_a = sb("rsum_a", [P, 4, TPB], ctx=ctx_a)
        rinv_a = sb("rinv_a", [P, 4, TPB], ctx=ctx_a)
        oT_a = sb("oT_a", [P, S], ctx=ctx_a)
        ctx_a.close()

        ctx_b = ExitStack()
        xnT = sb("xnT", [P, KT, NT * P], ctx=ctx_b)
        lng = sb("lng", [P, KT], ctx=ctx_b)
        lnb = sb("lnb", [P, KT], ctx=ctx_b)
        bo_b = sb("bo_b", [P, D], ctx=ctx_b)
        wq_s = sb("wq_s", [P, KT, P], ctx=ctx_b)
        wk_s = sb("wk_s", [P, KT, P], ctx=ctx_b)
        wv_s = sb("wv_s", [P, KT, P], ctx=ctx_b)
        wm_s = sb("wm_s", [P, KT, P], ctx=ctx_b)
        wo_s = sb("wo_s", [P, D], ctx=ctx_b)
        memT = sb("memT", [P, KT, CTX], ctx=ctx_b)
        q_dup = sb("q_dup", [P, 2, 2, S], F32R, ctx=ctx_b)
        k_st2 = sb("k_st2", [P, 2, KEYS], F32R, ctx=ctx_b)
        kv_f = sb("kv_f", [P, 4, 512], ctx=ctx_b)
        v_b = sb("v_b", [P, KEY_TILES, P], ctx=ctx_b)
        prob = sb("prob", [P, NPROB, KEYS], ctx=ctx_b)
        probT = sb("probT", [P, 2, KEY_TILES, S], ctx=ctx_b)
        nmax = sb("nmax", [P, UNITS], ctx=ctx_b)
        rsum = sb("rsum", [P, UNITS], ctx=ctx_b)
        rinv = sb("rinv", [P, UNITS], ctx=ctx_b)
        oT = sb("oT", [P, S], ctx=ctx_b)
        ctx_b.close()

        yT = sb("yT", [P, KT, NT * P])
        y_sb = sb("y_sb", [P, NT, D])
        emask = sb("emask", [P, NT, E])
        g2 = sb("g2", [P, D])
        be2 = sb("be2", [P, D])
        ctx_c = ExitStack()
        wqkv_c = sb("wqkv_c", [P, KT, 3 * D], ctx=ctx_c)
        wo_c = sb("wo_c", [P, KT, D], ctx=ctx_c)
        wg_c = sb("wg_c", [P, KT, E], ctx=ctx_c)
        bqkv = sb("bqkv", [P, 3 * D], ctx=ctx_c)
        bo_c = sb("bo_c", [P, D], ctx=ctx_c)
        g1 = sb("g1", [P, D], ctx=ctx_c)
        be1 = sb("be1", [P, D], ctx=ctx_c)
        rank = sb("rank", [P, E], ctx=ctx_c)
        uT = sb("uT", [P, KT, S], ctx=ctx_c)
        qkv = sb("qkv", [P, TPB, 3 * D], ctx=ctx_c)
        prod = sb("prod", [P, B, D], ctx=ctx_c)
        prod2 = sb("prod2", [P, B, D], ctx=ctx_c)
        sc = sb("sc", [P, B, B, HC], ctx=ctx_c)
        scm = sb("scm", [P, B, HC], ctx=ctx_c)
        scs = sb("scs", [P, B, HC], ctx=ctx_c)
        o_c = sb("o_c", [P, B, D], ctx=ctx_c)
        r_c = sb("r_c", [P, B, D], ctx=ctx_c)
        oT_c = sb("oT_c", [P, KT, S], ctx=ctx_c)
        yT_c = sb("yT_c", [P, KT, S], ctx=ctx_c)
        lg = sb("lg", [P, B, E], ctx=ctx_c)
        lgm = sb("lgm", [P, B], ctx=ctx_c)
        lge = sb("lge", [P, B, E], ctx=ctx_c)
        lgi = sb("lgi", [P, B], ctx=ctx_c)
        ctx_c.close()
        w1 = sb("w1", [P, 2, KT, DF])
        w2 = sb("w2", [P, 2, FT, D])
        b1 = sb("b1", [P, E, FT])
        b2 = sb("b2", [P, E, D])
        hT = sb("hT", [P, FT, S])
        moe_t = sb("moe_t", [P, 2, D])
        z = sb("z", [P, TPB, D])

        load_x = sem("load_x")
        load_a = sem("load_a")
        load_b = sem("load_b")
        load_c = sem("load_c")
        load_e = sem("load_e")
        stage_end = sem("stage_end")
        alone = sem("alone")
        const_set = sem("const_set")
        counters = []

        def counter(name):
            counters.append(sem(name))
            return counters[-1]

        dve_setup = counter("dve_setup")
        ln_dve = [counter(f"ln_dve_{s}") for s in "abc"]
        ln_var = [counter(f"ln_var_{s}") for s in "abc"]
        ln_rstd = [counter(f"ln_rstd_{s}") for s in "abc"]
        ln_xn = [counter(f"ln_xn_{s}") for s in "abc"]
        ln_tr = [counter(f"ln_tr_{s}") for s in "abc"]
        ln_xnT = [counter(f"ln_xnT_{s}") for s in "abc"]
        bias_added = [counter(f"bias_added_{s}") for s in "abc"]
        a_qk_ps, a_v_ps, a_qk, a_v = counter("a_qk_ps"), counter("a_v_ps"), counter("a_qk"), counter("a_v")
        a_cen, a_sq, a_hvar, a_hrstd = counter("a_cen"), counter("a_sq"), counter("a_hvar"), counter("a_hrstd")
        a_norm_qk, a_rot, a_rope = counter("a_norm_qk"), counter("a_rot"), counter("a_rope")
        a_hi, a_lo, a_tr = counter("a_hi"), counter("a_lo"), counter("a_tr")
        a_T_act, a_T_dve = counter("a_T_act"), counter("a_T_dve")
        a_s, a_max, a_exp, a_rinv, a_prob = counter("a_s"), counter("a_max"), counter("a_exp"), counter("a_rinv"), counter("a_prob")
        a_pt, a_pt_act, a_pt_dve = counter("a_pt"), counter("a_pt_act"), counter("a_pt_dve")
        a_vpad, a_pv, a_o, a_y, a_x = counter("a_vpad"), counter("a_pv"), counter("a_o"), counter("a_y"), counter("a_x")
        b_w, b_wv, b_wo = counter("b_w"), counter("b_wv"), counter("b_wo")
        b_pq, b_pk, b_pv_ps, b_v_f = counter("b_pq"), counter("b_pk"), counter("b_pv_ps"), counter("b_v_f")
        b_hi, b_lo, b_kv, b_vtr, b_v = counter("b_hi"), counter("b_lo"), counter("b_kv"), counter("b_vtr"), counter("b_v")
        b_khi_act, b_khi_dve = counter("b_khi_act"), counter("b_khi_dve")
        b_s, b_max, b_exp, b_rinv, b_prob = counter("b_s"), counter("b_max"), counter("b_exp"), counter("b_rinv"), counter("b_prob")
        b_pt, b_pt_act, b_pt_dve = counter("b_pt"), counter("b_pt_act"), counter("b_pt_dve")
        b_out, b_o, b_y, b_x = counter("b_out"), counter("b_o"), counter("b_y"), counter("b_x")
        c_qk_ps, c_dve, c_exp_in, c_exp = counter("c_qk_ps"), counter("c_dve"), counter("c_exp_in"), counter("c_exp")
        c_otr, c_oT, c_proj, c_var, c_rstd = counter("c_otr"), counter("c_oT"), counter("c_proj"), counter("c_var"), counter("c_rstd")
        c_ytr, c_yT, c_yTg, c_lg = counter("c_ytr"), counter("c_yT"), counter("c_yTg"), counter("c_lg")
        e_w, e_h_ps, e_h, e_o_ps, e_o, e_t = [counter("e_w0"), counter("e_w1")], counter("e_h_ps"), counter("e_h"), counter("e_o_ps"), counter("e_o"), counter("e_t")
        z_dve, z_var, z_rstd, z_out, stored = counter("z_dve"), counter("z_var"), counter("z_rstd"), counter("z_out"), counter("stored")

        block = top.enter_context(nc.Block())
        ENGINES = 5

        def end_stage(eng, n):
            eng.drain().then_inc(stage_end, 1)
            eng.wait_ge(stage_end, ENGINES * n)

        def cast(ap):
            return ap.bitcast(F32)


        def ln_stats(v, s, j, tiles, chained=1):
            per = 3 + 2 * (chained - 1)
            c = Chain(v, ln_dve[s], j * per, per, alone)
            for t in range(TPB):
                last = v.bn_stats(stats[:, t, :], tiles(t))
            c.link(last)
            for t in range(TPB):
                last = v.bn_aggr(mv[:, t, :], stats[:, t, :])
            c.link(last)
            v.tensor_scalar(ve[:, :], mv[:, :, 1], EPS, None, ALU.add).then_inc(ln_var[s], 1)
            v.wait_ge(ln_rstd[s], j * chained + 2)
            if chained == 2:
                c.link(v.tensor_tensor(ve2[:, :], mv[:, :, 1], rstd[:, :], ALU.mult))
                c.link(v.tensor_tensor(ve2[:, :], ve2[:, :], rstd[:, :], ALU.mult))
                v.tensor_scalar(ve2[:, :], ve2[:, :], EPS, None, ALU.add).then_inc(ln_var[s], 1)
                v.wait_ge(ln_rstd[s], j * chained + 2 + 1)
                c.link(v.tensor_tensor(rstd[:, :], rstd[:, :], rstd2[:, :], ALU.mult))
            else:
                c.link(v.tensor_copy(rstd2[:, :], rstd[:, :]))
            c.done()
            v.wait_ge(ln_tr[s], j * KT + 1)
            for t in range(TPB):
                last = v.tensor_scalar(xn[:, t, :], tiles(t), mv[:, t, 0:1], rstd[:, t:t + 1],
                                       ALU.subtract, ALU.mult)
            last.then_inc(ln_xn[s], 1)

        def ln_power(g, s, j, chained=1):
            g.wait_ge(ln_var[s], j * chained + 2)
            if chained == 2:
                g.wait_ge(ln_xn[s], j + 1)
            g.tensor_tensor(rstd[:, :], ve[:, :], neg_half[:, 0:TPB], ALU.pow).then_inc(ln_rstd[s], 1)
            if chained == 2:
                g.wait_ge(ln_var[s], j * chained + 2 + 1)
                g.tensor_tensor(rstd2[:, :], ve2[:, :], neg_half[:, 0:TPB], ALU.pow).then_inc(ln_rstd[s], 1)

        def ln_transpose(pe, s, j, bank):
            pe.wait_ge(ln_xn[s], j + 2)
            for k in range(KT):
                for t in range(TPB):
                    last = pe.transpose(ps[:, bank + k, t * P:(t + 1) * P], xn[:, t, k * P:(k + 1) * P], ident[:, :])
                last.then_inc(ln_tr[s], 1)

        def row(ap, n):
            return ap.rearrange("(a n) -> a n", a=1).broadcast_to([P, n])

        @block.sync
        def _(sp):
            sp.dma_start(x_sb[:, :, :], io["x"].rearrange("(t p) d -> p t d", p=P)).then_inc(load_x, 16)
            sp.dma_start(ident[:, :], io["ident"]).then_inc(load_a, 16)
            sp.dma_start(mask[:, :], io["mask"]).then_inc(load_a, 16)
            sp.dma_start(wqkv_a[:, :, :], io["a_wqkv"].rearrange("(k p) n -> p k n", p=P)).then_inc(load_a, 16)
            sp.dma_start(rope_cos[:, :, :], io["cos"].rearrange("(t p) d -> p t d", p=P)).then_inc(load_a, 16)
            sp.dma_start(rope_sin[:, :, :], io["sin"].rearrange("(t p) d -> p t d", p=P)).then_inc(load_a, 16)
            sp.dma_start(gb[:, :, :].rearrange("p a d -> p (a d)"), row(io["gb"], 8 * DA)).then_inc(load_a, 16)
            sp.dma_start(bo_a[:, :], row(io["a_bo"], D)).then_inc(load_a, 16)
            for c in counters:
                sp.sem_inc(c, 1)
            sp.wait_ge(const_set, 1)
            for h in range(4):
                sp.dma_start(wo_a[32 * h:32 * h + DA, :, :],
                             io["a_wo"].rearrange("(g h d) n -> h d g n", h=4, d=DA)[h]).then_inc(load_a, 16)
            end_stage(sp, 1)
            if last_stage >= 2:
                sp.dma_start(lng[:, :], io["ln_g"]).then_inc(load_b, 16)
                sp.dma_start(lnb[:, :], io["ln_b"]).then_inc(load_b, 16)
                sp.dma_start(bo_b[:, :], row(io["b_bo"], D)).then_inc(load_b, 16)
                with sp.Fori(0, B * PAIRS) as i:
                    b = sp.snap(i // PAIRS)
                    hp = sp.snap(i % PAIRS)
                    sp.wait_ge(b_pq, i + 1)
                    for w_s, name in ((wq_s, "b_wq"), (wk_s, "b_wk"), (wm_s, "b_wm")):
                        sp.dma_start(w_s[:, :, :], io[name].rearrange("(k p) (h n) -> h p k n", p=P, n=P)[hp])\
                            .then_inc(b_w, 16)
                    sp.dma_start(memT[:, :, :], io["ctxT"].rearrange("b (k p) n -> b p k n", p=P)[b])\
                        .then_inc(b_w, 16)
                    sp.wait_ge(b_pv_ps, i + 1)
                    sp.dma_start(wv_s[:, :, :], io["b_wv"].rearrange("(k p) (h n) -> h p k n", p=P, n=P)[hp])\
                        .then_inc(b_wv, 16)
                    sp.wait_ge(b_y, i + 1)
                    sp.dma_start(wo_s[:, :], io["b_wo"].rearrange("(h p) n -> h p n", p=P)[hp]).then_inc(b_wo, 16)
            end_stage(sp, 2)
            if last_stage >= 3:
                for dst, src in ((wqkv_c, "c_wqkv"), (wo_c, "c_wo"), (wg_c, "c_wg")):
                    sp.dma_start(dst[:, :, :], io[src].rearrange("(k p) n -> p k n", p=P)).then_inc(load_c, 16)
                for dst, src, n in ((bqkv, "c_bqkv", 3 * D), (bo_c, "c_bo", D), (g1, "c_g1", D), (be1, "c_be1", D),
                                    (g2, "c_g2", D), (be2, "c_be2", D), (rank, "rank", E)):
                    sp.dma_start(dst[:, :], row(io[src], n)).then_inc(load_c, 16)
            end_stage(sp, 3)
            if last_stage >= 3:
                sp.dma_start(b1[:, :, :], io["b1"]).then_inc(load_e, 16)
                sp.dma_start(b2[:, :, :].rearrange("p e d -> p (e d)"), row(io["b2"], E * D)).then_inc(load_e, 16)
                with sp.Fori(0, E // 2) as i:
                    for q in range(2):
                        sp.wait_ge(e_o_ps, i * 32 + 1)
                        sp.dma_start(w1[:, q, :, :], io["w1"].rearrange("(i q) (k p) n -> i q p k n", q=2, p=P)[i, q])\
                            .then_inc(e_w[q], 16)
                        sp.dma_start(w2[:, q, :, :], io["w2"].rearrange("(i q) (f p) n -> i q p f n", q=2, p=P)[i, q])\
                            .then_inc(e_w[q], 16)
            outv = out.rearrange("(j t p) d -> j p t d", t=TPB, p=P)
            with sp.Fori(0, B) as j:
                sp.wait_ge(z_out, j + 2)
                sp.dma_start(outv[j], z[:, :, :]).then_inc(stored, 16)
            sp.wait_ge(stored, 16 * B + 1)

        @block.gpsimd
        def _(g):
            g.memset(wo_a[:, :, :], 0.0).then_inc(const_set, 1)
            g.memset(neg_half[:, :], -0.5).then_inc(const_set, 1)
            g.memset(v_pad[:, :, :, :], 0.0).then_inc(const_set, 1)
            g.wait_ge(const_set, 3)
            g.wait_ge(load_a, 16 * 11)
            def pool_rows(b, following):
                if following:
                    ln_power(g, 0, b + 1)
                g.wait_ge(a_hvar, b + 1 + 1)
                g.tensor_tensor(hrstd[:, :], hvar[:, :], neg_half[:, :], ALU.pow).then_inc(a_hrstd, 1)
                g.wait_ge(a_norm_qk, b + 1 + 1)
                nv = qk[:, :, :].rearrange("p t (c h d two) -> p (t c) h d two", c=2, h=HA, two=2)
                for half in range(2):
                    mv2 = cen[:, :, :].rearrange("p t (c h e d) -> p (t c) h e d", c=2, h=HA, e=2)[:, :, :, half, :]
                    ts = t_sin[:, :, :, :].rearrange("p t c (e d) -> p (t c) e d", e=2)[:, :, half, :]
                    g.tensor_tensor(mv2, nv[:, :, :, :, 1 - half],
                                    ts.unsqueeze(2).broadcast_to([P, 2 * TPB, HA, DA // 2]), ALU.mult)\
                        .then_inc(a_rot, 1)
                g.wait_ge(ln_xn[0], b + 1 + 1)
                g.tensor_tensor(x_sb[:, ds(b * TPB, TPB), :], x_sb[:, ds(b * TPB, TPB), :],
                                bo_a[:, :].unsqueeze(1).broadcast_to([P, TPB, D]), ALU.add).then_inc(bias_added[0], 1)

            ln_power(g, 0, 0)
            with g.Fori(0, B - 1) as b:
                pool_rows(b, True)
            pool_rows(B - 1, False)
            g.wait_ge(a_v, B + 1)
            with g.Fori(0, NQ) as n:
                b = g.snap(n // QUADS)
                q = g.snap(n % QUADS)

                def normed(h):
                    g.wait_ge(a_rinv, n * 4 + h + 1 + 1)
                    g.sem_inc(alone, 1)
                    for qt in range(TPB):
                        pr = prob_a[:, h, TRI[qt]:TRI[qt] + (qt + 1) * P]
                        g.tensor_scalar(pr, pr, rinv_a[:, h, qt:qt + 1], 1.0, ALU.mult, ALU.mult)\
                            .then_inc(a_prob, 1)

                normed(0)
                normed(1)
                g.wait_ge(a_pv, n + 1)
                for t in range(TPB):
                    g.tensor_copy(v_pad[:, t, :, 0:DA],
                                  v_nat[:, ds(b * TPB + t, 1), ds(q * 64, 64)].rearrange("p t (h d) -> p (t h) d", h=4))\
                        .then_inc(a_vpad, 1)
                normed(2)
                normed(3)
            end_stage(g, 1)
            if last_stage >= 2:
                g.wait_ge(load_b, 48)
                with g.Fori(0, B) as b:
                    ln_power(g, 1, b, 2)
                    g.wait_ge(ln_xn[1], b + 2)
                    g.tensor_tensor(x_sb[:, ds(b * TPB, TPB), :], x_sb[:, ds(b * TPB, TPB), :],
                                    bo_b[:, :].unsqueeze(1).broadcast_to([P, TPB, D]), ALU.add)\
                        .then_inc(bias_added[1], 1)
                with g.Fori(0, B * PAIRS) as i:
                    for u in range(UNITS):
                        g.wait_ge(b_rinv, i * UNITS + u + 2)
                        g.sem_inc(alone, 1)
                        g.tensor_scalar(prob[:, u % NPROB, :], prob[:, u % NPROB, :], rinv[:, u:u + 1], 1.0, ALU.mult, ALU.mult)\
                            .then_inc(b_prob, 1)
            end_stage(g, 2)
            if last_stage >= 3:
                g.wait_ge(load_c, 160)
                with g.Fori(0, TPB) as p:
                    ln_power(g, 2, p)
                    g.wait_ge(ln_xn[2], p + 2)
                    g.wait_ge(c_var, p + 2)
                    g.tensor_tensor(rstd2[:, :], ve2[:, :], neg_half[:, 0:TPB], ALU.pow).then_inc(c_rstd, 1)
                    g.wait_ge(c_yT, (p + 1) * 2 + 1)
                    for s in range(B):
                        g.tensor_copy(yT[:, :, ds((s * TPB + p) * P, P)], yT_c[:, :, s * P:(s + 1) * P]).then_inc(c_yTg, 1)
            end_stage(g, 3)
            if last_stage >= 3:
                with g.Fori(0, B) as j:
                    g.wait_ge(z_var, j + 2)
                    g.tensor_tensor(rstd2[:, :], ve2[:, :], neg_half[:, 0:TPB], ALU.pow).then_inc(z_rstd, 1)

        @block.scalar
        def _(a):
            a.wait_ge(load_x, 16)
            def xnT_out(b):
                for k in range(KT):
                    a.wait_ge(ln_tr[0], b * KT + k + 1 + 1)
                    a.activation(xnT_a[:, k, :], ps[:, 6 + k, :], ACT.Copy).then_inc(ln_xnT[0], 1)

            def act_rows(b, following):
                a.wait_ge(a_qk_ps, b * 4 + 4 + 1)
                a.wait_ge(a_rope, b * 6 + 1)
                a.activation(qk[:, :, :], ps[:, 0:4, :], ACT.Copy).then_inc(a_qk, 1)
                if following:
                    a.wait_ge(a_v_ps, b + 1 + 1)
                a.wait_ge(a_cen, b + 1 + 1)
                a.activation(sq[:, :, :], cen[:, :, :], ACT.Square).then_inc(a_sq, 1)
                if following:
                    xnT_out(b + 1)

            xnT_out(0)
            with a.Fori(0, B - 1) as b:
                act_rows(b, True)
            act_rows(B - 1, False)

            def high_parts(n, b, q):
                a.wait_ge(a_tr, n * 4 + 1)
                for c, (st, places) in enumerate(((q_st, (0, 2)), (k_st, (0, 1)))):
                    src = qkr[:, ds(b * TPB, TPB), ds(q * 64 + c * D, 64)].rearrange("p t (h d) -> p t h d", h=4)
                    for e in places:
                        a.activation(st[:, :, :, e * DA:(e + 1) * DA], src, ACT.Copy).then_inc(a_hi, 1)

            def T_out_act(n):
                a.wait_ge(a_tr, n * 4 + 1 + 1)
                a.activation(qT_a[:, 0, :], ps[:, 0, :], ACT.Copy).then_inc(a_T_act, 1)
                a.wait_ge(a_tr, n * 4 + 2 + 1)
                a.activation(kT_a[:, 0, :], ps[:, 1, :], ACT.Copy).then_inc(a_T_act, 1)

            def exps(n, h):
                a.wait_ge(a_max, n * 4 + h + 1 + 1)
                base = 3 * (h % 2)
                for qt in range(TPB):
                    bank, off = (base, TRI[qt]) if qt < 2 else (base + qt - 1, 0)
                    last = a.activation(prob_a[:, h, TRI[qt]:TRI[qt] + (qt + 1) * P],
                                        ps[:, bank, off:off + (qt + 1) * P], ACT.Exp,
                                        bias=nmax_a[:, h, qt:qt + 1], accum_out=rsum_a[:, h, qt:qt + 1])
                last.then_inc(a_exp, 1)

            def pta_out(n, h):
                a.wait_ge(a_pt, n * 12 + 3 * h + 1 + 1)
                a.activation(probT_a[:, h, 0:512], ps[:, 6 + (3 + 3 * h) % 2, :], ACT.Copy).then_inc(a_pt_act, 1)

            def oT_out(n):
                a.wait_ge(a_pv, n + 1 + 1)
                a.activation(oT_a[:, :], ps[:, 6, :], ACT.Copy).then_inc(a_o, 1)

            def act_quad(n, b1, q1, first, following):
                exps(n, 0)
                exps(n, 1)
                if not first:
                    oT_out(n - 1)
                exps(n, 2)
                pta_out(n, 0)
                if following:
                    high_parts(n + 1, b1, q1)
                exps(n, 3)
                pta_out(n, 1)
                pta_out(n, 2)
                if following:
                    T_out_act(n + 1)
                pta_out(n, 3)

            a.wait_ge(a_rope, B * 6 + 1)
            high_parts(0, 0, 0)
            T_out_act(0)
            act_quad(0, 0, 1, True, True)
            with a.Fori(1, NQ - 1) as n:
                act_quad(n, a.snap((n + 1) // QUADS), a.snap((n + 1) % QUADS), False, True)
            act_quad(NQ - 1, 0, 0, False, False)
            oT_out(NQ - 1)
            end_stage(a, 1)
            if last_stage >= 2:
                a.wait_ge(load_b, 48)
                with a.Fori(0, B) as b:
                    for k in range(KT):
                        a.wait_ge(ln_tr[1], b * KT + k + 2)
                        a.activation(xnT[:, k, ds(b * S, S)], ps[:, 6 + k, :], ACT.Identity,
                                     bias=lnb[:, k:k + 1], scale=lng[:, k:k + 1]).then_inc(ln_xnT[1], 1)

                def exp(i, u):
                    a.wait_ge(b_max, i * UNITS + u + 1 + 1)
                    if u >= NPROB:
                        a.wait_ge(b_pt, i * CHUNKS + 3 * (u - NPROB) + 6 + 1)
                    a.activation(prob[:, u % NPROB, :], ps[:, 3 * (u % 2):3 * (u % 2) + 3, :], ACT.Exp,
                                 bias=nmax[:, u:u + 1], accum_out=rsum[:, u:u + 1]).then_inc(b_exp, 1)

                def v_out(i, c):
                    a.wait_ge(b_pt, i * CHUNKS + c + 1 + 1)
                    a.wait_ge(b_out, i + 1)
                    a.activation(v_b[:, 4 * c:4 * c + 4, :], ps[:, 6 + c % 2, :], ACT.Copy).then_inc(b_pt_act, 1)

                def pt_out(i, u):
                    for c in (0, 2):
                        a.wait_ge(b_pt, i * CHUNKS + 3 * (u + 1) + c + 1 + 1)
                        a.activation(probT[:, u // 4, 4 * c:4 * c + 4, (u % 4) * P:(u % 4 + 1) * P],
                                     ps[:, 6 + (3 * (u + 1) + c) % 2, :], ACT.Copy).then_inc(b_pt_act, 1)

                def qk_out(n):
                    a.wait_ge(b_pq, n + 1 + 1)
                    for h in range(2):
                        for half in range(2):
                            a.activation(q_dup[64 * half:64 * half + 64, h, 0, :], ps[64 * h:64 * h + 64, 3, :],
                                         ACT.Copy, scale=DB ** -0.5).then_inc(b_hi, 1)
                    a.wait_ge(b_pk, n + 1 + 1)
                    a.activation(kv_f[:, 0:3, :], ps[:, 0:3, :], ACT.Copy).then_inc(b_kv, 1)
                    a.wait_ge(b_kv, n + 1 + 1)
                    a.activation(k_st2[0:64, 0, :], kv_f[0:64, 0:3, :], ACT.Copy).then_inc(b_khi_act, 1)

                def vf_out(n):
                    a.wait_ge(b_pv_ps, n + 1 + 1)
                    a.activation(kv_f[:, 3, :], ps[:, 5, :], ACT.Copy).then_inc(b_v_f, 1)

                def act_pair(i, following):
                    v_out(i, 0)
                    exp(i, 0)
                    v_out(i, 2)
                    exp(i, 1)
                    exp(i, 2)
                    for u in range(3, UNITS):
                        pt_out(i, u - 3)
                        exp(i, u)
                    for u in range(UNITS - 3, UNITS):
                        pt_out(i, u)
                    if following:
                        qk_out(i + 1)
                    a.wait_ge(b_out, i + 1 + 1)
                    a.activation(oT[:, :], ps[:, 4, :], ACT.Copy).then_inc(b_o, 1)
                    if following:
                        vf_out(i + 1)

                qk_out(0)
                vf_out(0)
                with a.Fori(0, B * PAIRS - 1) as i:
                    act_pair(i, True)
                act_pair(B * PAIRS - 1, False)
            end_stage(a, 2)
            if last_stage >= 3:
                with a.Fori(0, TPB) as p:
                    for k in range(KT):
                        a.wait_ge(ln_tr[2], p * KT + k + 2)
                        a.wait_ge(c_qk_ps, p + 1)
                        a.activation(uT[:, k, :], ps[:, 6 + k, :], ACT.Copy).then_inc(ln_xnT[2], 1)
                    a.wait_ge(c_exp_in, p + 2)
                    a.activation(sc[:, :, :, :], sc[:, :, :, :], ACT.Exp, scale=DC ** -0.5).then_inc(c_exp, 1)
                    for k in range(KT):
                        a.wait_ge(c_otr, p * KT + k + 2)
                        a.activation(oT_c[:, k, :], ps[:, 6 + k, :], ACT.Copy).then_inc(c_oT, 1)
                    a.wait_ge(c_yTg, p * 4 + 1)
                    for k in range(KT):
                        a.wait_ge(c_ytr, p * KT + k + 2)
                        a.activation(yT_c[:, k, :], ps[:, 6 + k, :], ACT.Copy).then_inc(c_yT, 1)
            end_stage(a, 3)
            if last_stage >= 3:
                a.wait_ge(load_e, 32)
                with a.Fori(0, E // 2) as i:
                    for q in range(2):
                        with a.Fori(0, B) as c:
                            n = a.snap(i * 8 + q * 4 + c)
                            a.wait_ge(e_o_ps, n * 4 + 1)
                            for f in range(FT):
                                a.wait_ge(e_h_ps, n * FT + f + 2)
                                a.activation(hT[:, f, :], ps[:, f % 4, :], ACT.Relu,
                                             bias=b1[:, ds(i * 2 + q, 1), f]).then_inc(e_h, 1)

        @block.vector
        def _(v):
            v.wait_ge(load_a, 16 * 11)
            v.wait_ge(load_x, 16)
            v.wait_ge(const_set, 3)
            c = Chain(v, dve_setup, 0, 8)
            c.link(v.tensor_copy(ident_r[:, :], ident[:, :]))
            c.link(v.tensor_copy(mask_r[:, :], mask[:, :]))
            gbv = gb[:, :, :].rearrange("p (a c) d -> p a c d", c=2)
            c.link(v.tensor_scalar(gbv[:, :, 0, :], gbv[:, :, 0, :], DA ** -0.5, None, ALU.mult))
            full = [P, TPB, 2, DA]

            def table(dst, trig, r):
                return v.tensor_tensor(dst[:, :, :, :], trig[:, :, :].unsqueeze(2).broadcast_to(full),
                                       gb[:, 2 * r:2 * r + 2, :].unsqueeze(1).broadcast_to(full), ALU.mult)

            c.link(table(t_cos, rope_cos, 0))
            c.link(table(t_sin, rope_sin, 1))
            c.link(table(t_add, rope_cos, 2))
            c.link(table(t_add2, rope_sin, 3))
            c.link(v.tensor_tensor(t_add[:, :, :, :], t_add[:, :, :, :], t_add2[:, :, :, :], ALU.add))
            c.done()

            heads = lambda ap: ap[:, :, :].rearrange("p t (h d) -> p (t h) d", d=DA)
            heads4 = lambda ap: ap[:, :, :].rearrange("p t (c h d) -> p (t c) h d", c=2, h=HA)
            tab = lambda ap: ap[:, :, :, :].rearrange("p t c d -> p (t c) d").unsqueeze(2).broadcast_to([P, 8, HA, DA])
            wide = lambda ap: ap[:, :].unsqueeze(2).broadcast_to([P, TPB * 32, DA])
            def dve_rows(b, following):
                v.wait_ge(a_v_ps, b + 1 + 1)
                v.tensor_copy(v_nat[:, ds(b * TPB, TPB), :], ps[:, 4:6, :].rearrange("p a n -> p (a n)")
                              .rearrange("p (t n) -> p t n", n=D)).then_inc(a_v, 1)
                v.wait_ge(a_qk, b + 1 + 1)
                c = Chain(v, a_rope, b * 6, 6)
                c.link(v.tensor_reduce(hsum[:, :], heads(qk), AX, ALU.add))
                c.link(v.tensor_scalar(hmean[:, :], hsum[:, :], 1.0 / DA, None, ALU.mult))
                v.tensor_tensor(heads(cen), heads(qk), wide(hmean), ALU.subtract).then_inc(a_cen, 1)
                if following:
                    ln_stats(v, 0, b + 1, lambda t: x_sb[:, ds((b + 1) * TPB + t, 1), :].rearrange("p t d -> p (t d)"))
                v.wait_ge(a_sq, b + 1 + 1)
                c.link(v.tensor_reduce(hsum[:, :], heads(sq), AX, ALU.add))
                v.tensor_scalar(hvar[:, :], hsum[:, :], 1.0 / DA, EPS, ALU.mult, ALU.add).then_inc(a_hvar, 1)
                v.wait_ge(a_hrstd, b + 1 + 1)
                v.tensor_tensor(heads(qk), heads(cen), wide(hrstd), ALU.mult).then_inc(a_norm_qk, 1)
                v.wait_ge(a_norm_qk, b + 1 + 1)
                c.link(v.tensor_tensor(heads4(sq), heads4(qk), tab(t_cos), ALU.mult))
                v.wait_ge(a_rot, b * 2 + 2 + 1)
                c.link(v.tensor_tensor(sq[:, :, :], sq[:, :, :], cen[:, :, :], ALU.add))
                c.link(v.tensor_tensor(qkr[:, ds(b * TPB, TPB), :].rearrange("p t (c h d) -> p (t c) h d", c=2, h=HA),
                                       heads4(sq), tab(t_add), ALU.add))
                c.done()

            ln_stats(v, 0, 0, lambda t: x_sb[:, t, :])
            with v.Fori(0, B - 1) as b:
                dve_rows(b, True)
                v.sem_inc(alone, 1)
            dve_rows(B - 1, False)

            def low_parts(n, b, q):
                for c2, (st, places) in enumerate(((q_st, (1, 3)), (k_st, (2, 3)))):
                    src = qkr[:, ds(b * TPB, TPB), ds(q * 64 + c2 * D, 64)].rearrange("p t (h d) -> p t h d", h=4)
                    v.wait_ge(a_hi, n * 4 + 2 * c2 + 1 + 1)
                    for e in places:
                        v.tensor_tensor(st[:, :, :, e * DA:(e + 1) * DA], src,
                                        cast(st[:, :, :, 0:DA]), ALU.subtract).then_inc(a_lo, 1)

            def T_out_dve(n):
                v.wait_ge(a_tr, n * 4 + 3 + 1)
                v.tensor_copy(qT_a[:, 1, :], ps[:, 2, :]).then_inc(a_T_dve, 1)
                v.wait_ge(a_tr, n * 4 + 4 + 1)
                v.tensor_copy(kT_a[:, 1, :], ps[:, 3, :]).then_inc(a_T_dve, 1)

            def maxes(n, h):
                v.wait_ge(a_s, n * 4 + h + 1 + 1)
                base = 3 * (h % 2)
                for qt in range(TPB):
                    bank, off = (base, TRI[qt]) if qt < 2 else (base + qt - 1, 0)
                    last = v.tensor_reduce(nmax_a[:, h, qt:qt + 1], ps[:, bank, off:off + (qt + 1) * P],
                                           AX, ALU.max, negate=True)
                last.then_inc(a_max, 1)

            def inverse(n, h):
                v.wait_ge(a_exp, n * 4 + h + 1 + 1)
                v.reciprocal(rinv_a[:, h, :], rsum_a[:, h, :]).then_inc(a_rinv, 1)

            def pta_out_dve(n, h):
                for j in (1, 2):
                    v.wait_ge(a_pt, n * 12 + 3 * h + j + 1 + 1)
                    v.tensor_copy(probT_a[:, h, 512 + 384 * (j - 1):512 + 384 * j],
                                  ps[:, 6 + (3 + 3 * h + j) % 2, 0:384]).then_inc(a_pt_dve, 1)

            def add_out(n, b):
                for half in range(2):
                    v.wait_ge(a_y, 2 * n + half + 1 + 1)
                    xb = x_sb[:, ds(b * TPB + 2 * half, 2), :]
                    v.tensor_tensor(xb, ps[:, 7 - half, :].rearrange("p (t n) -> p t n", n=D), xb, ALU.add)\
                        .then_inc(a_x, 1)

            def dve_quad(n, b0, b1, q1, first, following):
                maxes(n, 0)
                maxes(n, 1)
                inverse(n, 0)
                if not first:
                    v.wait_ge(a_x, 2 * n - 2 + 1)
                maxes(n, 2)
                inverse(n, 1)
                if not first:
                    add_out(n - 1, b0)
                pta_out_dve(n, 0)
                maxes(n, 3)
                inverse(n, 2)
                pta_out_dve(n, 1)
                if following:
                    low_parts(n + 1, b1, q1)
                inverse(n, 3)
                pta_out_dve(n, 2)
                if following:
                    T_out_dve(n + 1)
                pta_out_dve(n, 3)

            v.wait_ge(a_rope, B * 6 + 1)
            v.wait_ge(bias_added[0], B + 1)
            low_parts(0, 0, 0)
            T_out_dve(0)
            dve_quad(0, 0, 0, 1, True, True)
            with v.Fori(1, NQ - 1) as n:
                dve_quad(n, v.snap((n - 1) // QUADS), v.snap((n + 1) // QUADS), v.snap((n + 1) % QUADS), False, True)
            dve_quad(NQ - 1, B - 1, 0, 0, False, False)
            v.wait_ge(a_x, 2 * NQ - 2 + 1)
            add_out(NQ - 1, B - 1)
            end_stage(v, 1)
            if last_stage >= 2:
                with v.Fori(0, B) as b:
                    ln_stats(v, 1, b, lambda t: x_sb[:, b * TPB + t, :], 2)
                v.wait_ge(bias_added[1], B + 1)

                def rowmax(i, u):
                    v.wait_ge(b_s, i * UNITS + u + 1 + 1)
                    v.tensor_reduce(nmax[:, u:u + 1], ps[:, 3 * (u % 2):3 * (u % 2) + 3, :]
                                    .rearrange("p a n -> p (a n)"), AX, ALU.max, negate=True).then_inc(b_max, 1)

                def inverse_b(i, u):
                    v.wait_ge(b_exp, i * UNITS + u + 1 + 1)
                    v.reciprocal(rinv[:, u:u + 1], rsum[:, u:u + 1]).then_inc(b_rinv, 1)

                def v_out_dve(i):
                    v.wait_ge(b_pt, i * CHUNKS + 2 + 1)
                    v.wait_ge(b_out, i + 1)
                    v.tensor_copy(v_b[:, 4:8, :], ps[:, 7, :].rearrange("p (a n) -> p a n", a=4)).then_inc(b_pt_dve, 1)

                def pt_out_dve(i, u):
                    cc = 3 * (u + 1) + 1
                    v.wait_ge(b_pt, i * CHUNKS + cc + 1 + 1)
                    v.tensor_copy(probT[:, u // 4, 4:8, (u % 4) * P:(u % 4 + 1) * P],
                                  ps[:, 6 + cc % 2, :].rearrange("p (a n) -> p a n", a=4)).then_inc(b_pt_dve, 1)

                def qk_out_dve(n):
                    v.wait_ge(b_hi, n * 4 + 4 + 1)
                    for h in range(2):
                        for half in range(2):
                            v.scalar_tensor_tensor(q_dup[64 * half:64 * half + 64, h, 1, :],
                                                   ps[64 * h:64 * h + 64, 3, :], DB ** -0.5,
                                                   cast(q_dup[64 * h:64 * h + 64, h, 0, :]), ALU.mult, ALU.subtract)\
                                .then_inc(b_lo, 1)
                    v.wait_ge(b_kv, n + 1 + 1)
                    v.tensor_copy(k_st2[64:128, 1, :], kv_f[64:128, 0:3, :].rearrange("p a n -> p (a n)"))\
                        .then_inc(b_khi_dve, 1)
                    for h in (1, 0):
                        v.wait_ge((b_khi_act, b_khi_dve)[h], n + 1 + 1)
                        o = 64 * (1 - h)
                        v.tensor_tensor(k_st2[o:o + 64, h, :], kv_f[64 * h:64 * h + 64, 0:3, :].rearrange("p a n -> p (a n)"),
                                        cast(k_st2[64 * h:64 * h + 64, h, :]), ALU.subtract).then_inc(b_lo, 1)

                def dve_pair(i, b, following):
                    rowmax(i, 0)
                    rowmax(i, 1)
                    inverse_b(i, 0)
                    v_out_dve(i)
                    rowmax(i, 2)
                    inverse_b(i, 1)
                    for u in range(3, UNITS):
                        rowmax(i, u)
                        inverse_b(i, u - 1)
                        pt_out_dve(i, u - 3)
                    inverse_b(i, UNITS - 1)
                    for u in range(UNITS - 3, UNITS):
                        pt_out_dve(i, u)
                    if following:
                        qk_out_dve(i + 1)
                    v.wait_ge(b_y, i + 1 + 1)
                    xb = x_sb[:, ds(b * TPB, TPB), :]
                    v.tensor_tensor(xb, ps[:, 6:8, :].rearrange("p a n -> p (a n)").rearrange("p (t n) -> p t n", n=D),
                                    xb, ALU.add).then_inc(b_x, 1)
                    v.wait_ge(b_x, i + 1 + 1)

                qk_out_dve(0)
                with v.Fori(0, B * PAIRS - 1) as i:
                    dve_pair(i, v.snap(i // PAIRS), True)
                dve_pair(B * PAIRS - 1, B - 1, False)
            end_stage(v, 2)
            if last_stage >= 3:
                v.wait_ge(load_c, 160)
                with v.Fori(0, TPB) as p:
                    ln_stats(v, 2, p, lambda t: x_sb[:, t * TPB + p, :])
                    c = Chain(v, c_dve, p * C_ALL, C_ALL, alone)
                    v.wait_ge(c_qk_ps, p + 2)
                    c.link(v.tensor_tensor(qkv[:, :, 0:2 * D], ps[:, 0:4, :],
                                           bqkv[:, 0:2 * D].unsqueeze(1).broadcast_to([P, B, 2 * D]), ALU.add))
                    c.link(v.tensor_tensor(qkv[:, :, 2 * D:3 * D], ps[:, 4:6, :].rearrange("p a n -> p (a n)")
                                           .rearrange("p (t n) -> p t n", n=D),
                                           bqkv[:, 2 * D:3 * D].unsqueeze(1).broadcast_to([P, B, D]), ALU.add))
                    for s in range(B):
                        c.link(v.tensor_tensor(prod[:, :, :], qkv[:, :, D:2 * D],
                                               qkv[:, s, 0:D].unsqueeze(1).broadcast_to([P, B, D]), ALU.mult))
                        c.link(v.tensor_reduce(sc[:, s, :, :], prod[:, :, :].rearrange("p s (h d) -> p s h d", h=HC),
                                               AX, ALU.add))
                    c.link(v.tensor_reduce(scm[:, :, :], sc[:, :, :, :].rearrange("p s k h -> p s h k"), AX, ALU.max))
                    v.tensor_tensor(sc[:, :, :, :], sc[:, :, :, :], scm[:, :, :].unsqueeze(2)
                                    .broadcast_to([P, B, B, HC]), ALU.subtract).then_inc(c_exp_in, 1)
                    v.wait_ge(c_exp, p + 2)
                    c.link(v.tensor_reduce(scs[:, :, :], sc[:, :, :, :].rearrange("p s k h -> p s h k"), AX, ALU.add))
                    c.link(v.reciprocal(scs[:, :, :], scs[:, :, :]))
                    c.link(v.tensor_tensor(sc[:, :, :, :], sc[:, :, :, :], scs[:, :, :].unsqueeze(2)
                                           .broadcast_to([P, B, B, HC]), ALU.mult))
                    for s in range(B):
                        for k in range(B):
                            last = v.tensor_tensor(prod2[:, k, :].rearrange("p (h d) -> p h d", h=HC),
                                                   qkv[:, k, 2 * D:3 * D].rearrange("p (h d) -> p h d", h=HC),
                                                   sc[:, s, k, :].unsqueeze(2).broadcast_to([P, HC, DC]), ALU.mult)
                        c.link(last)
                        c.link(v.tensor_reduce(o_c[:, s, :], prod2[:, :, :].rearrange("p k n -> p n k"), AX, ALU.add))
                    assert c.k == C_O
                    v.wait_ge(c_proj, p + 2)
                    c.link(v.tensor_tensor(r_c[:, :, :], xn[:, :, :], ps[:, 0:2, :].rearrange("p a n -> p (a n)")
                                           .rearrange("p (t n) -> p t n", n=D), ALU.add))
                    c.link(v.tensor_tensor(r_c[:, :, :], r_c[:, :, :], bo_c[:, :].unsqueeze(1)
                                           .broadcast_to([P, B, D]), ALU.add))
                    for t in range(B):
                        last = v.bn_stats(stats[:, t, :], r_c[:, t, :])
                    c.link(last)
                    for t in range(B):
                        last = v.bn_aggr(mv[:, t, :], stats[:, t, :])
                    c.link(last)
                    v.tensor_scalar(ve2[:, :], mv[:, :, 1], EPS, None, ALU.add).then_inc(c_var, 1)
                    v.wait_ge(c_rstd, p + 2)
                    for t in range(B):
                        last = v.tensor_scalar(r_c[:, t, :], r_c[:, t, :], mv[:, t, 0:1], rstd2[:, t:t + 1],
                                               ALU.subtract, ALU.mult)
                    c.link(last)
                    c.link(v.tensor_tensor(r_c[:, :, :], r_c[:, :, :], g1[:, :].unsqueeze(1)
                                           .broadcast_to([P, B, D]), ALU.mult))
                    c.link(v.tensor_tensor(r_c[:, :, :], r_c[:, :, :], be1[:, :].unsqueeze(1)
                                           .broadcast_to([P, B, D]), ALU.add))
                    assert c.k == C_Y
                    c.link(v.tensor_copy(y_sb[:, :, :].rearrange("p (s q) d -> p q s d", s=B)[:, ds(p, 1), :, :]
                                         .rearrange("p a s d -> p (a s) d"), r_c[:, :, :]))
                    v.wait_ge(c_lg, p + 2)
                    c.link(v.tensor_copy(lg[:, :, :], ps[:, 4, 0:B * E].rearrange("p (s e) -> p s e", e=E)))
                    c.link(v.tensor_reduce(lgm[:, :], lg[:, :, :], AX, ALU.max))
                    c.link(v.tensor_tensor(lge[:, :, :], lg[:, :, :], lgm[:, :].unsqueeze(2)
                                           .broadcast_to([P, B, E]), ALU.is_equal))
                    c.link(v.tensor_scalar(lge[:, :, :], lge[:, :, :], -float(E), float(E), ALU.mult, ALU.add))
                    c.link(v.tensor_tensor(lge[:, :, :], lge[:, :, :], rank[:, :].unsqueeze(1)
                                           .broadcast_to([P, B, E]), ALU.add))
                    c.link(v.tensor_reduce(lgi[:, :], lge[:, :, :], AX, ALU.min))
                    for s in range(B):
                        c.link(v.tensor_scalar(emask[:, ds(s * TPB + p, 1), :].rearrange("p a e -> p (a e)"),
                                               rank[:, :], lgi[:, s:s + 1], None, ALU.is_equal))
                    c.done()
            end_stage(v, 3)
            if last_stage >= 3:
                v.wait_ge(load_e, 32)
                with v.Fori(0, E // 2) as i:
                    for q in range(2):
                        with v.Fori(0, B) as c4:
                            n = v.snap(i * 8 + q * 4 + c4)
                            ex = v.snap(i * 2 + q)
                            for t in range(TPB):
                                v.wait_ge(e_o_ps, n * 4 + t + 2)
                                v.tensor_tensor(moe_t[:, t % 2, :], ps[:, 4 + t, 0:D],
                                                b2[:, ds(ex, 1), :].rearrange("p a d -> p (a d)"), ALU.add)\
                                    .then_inc(e_t, 1)
                                v.wait_ge(e_t, n * 4 + t + 2)
                                yt = y_sb[:, ds(c4 * TPB + t, 1), :].rearrange("p a d -> p (a d)")
                                v.scalar_tensor_tensor(yt, moe_t[:, t % 2, :],
                                                       emask[:, ds(c4 * TPB + t, 1), ds(ex, 1)].rearrange("p a e -> p (a e)"),
                                                       yt, ALU.mult, ALU.add).then_inc(e_o, 1)
                v.wait_ge(e_o, E * NT + 1)
                with v.Fori(0, B) as j:
                    c = Chain(v, z_dve, j * 5, 5, alone)
                    yt = lambda t: y_sb[:, j * TPB + t, :]
                    for t in range(TPB):
                        last = v.bn_stats(stats[:, t, :], yt(t))
                    c.link(last)
                    for t in range(TPB):
                        last = v.bn_aggr(mv[:, t, :], stats[:, t, :])
                    c.link(last)
                    v.tensor_scalar(ve2[:, :], mv[:, :, 1], EPS, None, ALU.add).then_inc(z_var, 1)
                    v.wait_ge(z_rstd, j + 2)
                    v.wait_ge(stored, j * 16 + 1)
                    for t in range(TPB):
                        last = v.tensor_scalar(z[:, t, :], yt(t), mv[:, t, 0:1], rstd2[:, t:t + 1],
                                               ALU.subtract, ALU.mult)
                    c.link(last)
                    c.link(v.tensor_tensor(z[:, :, :], z[:, :, :], g2[:, :].unsqueeze(1)
                                           .broadcast_to([P, TPB, D]), ALU.mult))
                    c.link(v.tensor_tensor(z[:, :, :], z[:, :, :], be2[:, :].unsqueeze(1)
                                           .broadcast_to([P, TPB, D]), ALU.add))
                    c.done()
                    v.tensor_tensor(z[:, :, :], z[:, :, :], x_sb[:, ds(j * TPB, TPB), :], ALU.add).then_inc(z_out, 1)
            else:
                with v.Fori(0, B) as j:
                    v.wait_ge(stored, j * 16 + 1)
                    v.tensor_copy(z[:, :, :], x_sb[:, ds(j * TPB, TPB), :]).then_inc(z_out, 1)

        @block.tensor
        def _(pe):
            pe.wait_ge(load_a, 16 * 11)
            pe.wait_ge(dve_setup, 9)
            def pe_rows(b, following):
                pe.wait_ge(ln_xnT[0], b * KT + 2 + 1)
                pe.wait_ge(a_qk, b + 1)
                for t in range(TPB):
                    for k in range(KT):
                        last = pe.matmul(ps[:, t, :], xnT_a[:, k, t * P:(t + 1) * P], wqkv_a[:, k, 0:2 * D],
                                         start=k == 0, stop=k == KT - 1)
                    last.then_inc(a_qk_ps, 1)
                pe.wait_ge(a_v, b + 1)
                for t in range(TPB):
                    for k in range(KT):
                        last = pe.matmul(ps[:, 4 + t // 2, (t % 2) * D:(t % 2 + 1) * D],
                                         xnT_a[:, k, t * P:(t + 1) * P], wqkv_a[:, k, 2 * D:3 * D],
                                         start=k == 0, stop=k == KT - 1)
                last.then_inc(a_v_ps, 1)
                if following:
                    ln_transpose(pe, 0, b + 1, 6)

            ln_transpose(pe, 0, 0, 6)
            with pe.Fori(0, B - 1) as b:
                pe_rows(b, True)
            pe_rows(B - 1, False)

            def stacks(n):
                pe.wait_ge(a_hi, n * 4 + 4 + 1)
                pe.wait_ge(a_lo, n * 4 + 4 + 1)
                for bank, (st, hp) in enumerate(((q_st, 0), (k_st, 0), (q_st, 1), (k_st, 1))):
                    pe.wait_ge(a_exp, n * 4 - (1 if bank < 3 else 0) + 1) if not isinstance(n, int) or n > 0 else None
                    for t in range(TPB):
                        last = pe.transpose(ps[:, bank, t * P:(t + 1) * P],
                                            cast(st[:, t, 2 * hp:2 * hp + 2, :].rearrange("p h d -> p (h d)")),
                                            ident[:, :])
                    last.then_inc(a_tr, 1)

            def scores(n, h):
                hp, rows = h // 2, slice(64 * (h % 2), 64 * (h % 2) + 64)
                base = 3 * (h % 2)
                if h < 2:
                    pe.wait_ge(a_T_act, n * 2 + 2 + 1)
                    pe.wait_ge(a_T_dve, n * 2 + 2 + 1)
                else:
                    pe.wait_ge(a_exp, n * 4 + h - 2 + 1 + 1)
                for qt in range(TPB):
                    bank, off = (base, TRI[qt]) if qt < 2 else (base + qt - 1, 0)
                    pe.matmul(ps[:, bank, off:off + (qt + 1) * P], qT_a[rows, hp, qt * P:(qt + 1) * P],
                              kT_a[rows, hp, 0:(qt + 1) * P], start=True, stop=False)
                    last = pe.matmul(ps[:, bank, off + qt * P:off + (qt + 1) * P], ident_r[:, :], mask_r[:, :],
                                     start=False, stop=True)
                last.then_inc(a_s, 1)

            def turn_a(n, h, first):
                pe.wait_ge(a_prob, n * 16 + 4 * h + 4 + 1)
                for j, blocks in enumerate(TRI_BLOCKS):
                    if j == 2:
                        pe.wait_ge(a_pt_act, n * 4 + h + 1 + 1)
                    elif h > 0:
                        pe.wait_ge(a_pt_dve, n * 8 + 2 * (h - 1) + j + 1 + 1)
                    elif not first:
                        pe.wait_ge(a_x, 2 * (n - 1) + j + 1 + 1)
                    for m, (kt, qt) in enumerate(blocks):
                        last = pe.transpose(ps[:, 6 + (3 + 3 * h + j) % 2, m * P:(m + 1) * P],
                                            prob_a[:, h, TRI[qt] + kt * P:TRI[qt] + (kt + 1) * P], ident[:, :])
                    last.then_inc(a_pt, 1)

            def weigh(n):
                pe.wait_ge(a_pt_act, n * 4 + 4 + 1)
                pe.wait_ge(a_pt_dve, n * 8 + 8 + 1)
                pe.wait_ge(a_vpad, n * 4 + 4 + 1)
                for kt in range(TPB):
                    for h in range(4):
                        last = pe.matmul(ps[32 * h:32 * h + 32, 6, kt * P:S], v_pad[:, kt, h, :],
                                         probT_a[:, h, TRI_KEYS[kt]:TRI_KEYS[kt] + S - kt * P],
                                         start=kt == 0, stop=kt == TPB - 1)
                last.then_inc(a_pv, 1)

            def out_a(n, q):
                pe.wait_ge(a_o, n + 1 + 1)
                for t in range(TPB):
                    last = pe.matmul(ps[:, 7 - t // 2, (t % 2) * D:(t % 2 + 1) * D], oT_a[:, t * P:(t + 1) * P],
                                     wo_a[:, ds(q, 1), :].rearrange("p a n -> p (a n)"), start=True, stop=True)
                    if t % 2:
                        last.then_inc(a_y, 1)

            def pe_quad(n, q0, first, following):
                scores(n, 0)
                scores(n, 1)
                if not first:
                    weigh(n - 1)
                scores(n, 2)
                if not first:
                    out_a(n - 1, q0)
                turn_a(n, 0, first)
                scores(n, 3)
                turn_a(n, 1, first)
                turn_a(n, 2, first)
                if following:
                    stacks(n + 1)
                turn_a(n, 3, first)

            stacks(0)
            pe_quad(0, 0, True, True)
            with pe.Fori(1, NQ - 1) as n:
                pe_quad(n, pe.snap((n - 1) % QUADS), False, True)
            pe_quad(NQ - 1, (NQ - 2) % QUADS, False, False)
            weigh(NQ - 1)
            out_a(NQ - 1, QUADS - 1)
            end_stage(pe, 1)
            if last_stage >= 2:
                with pe.Fori(0, B) as b:
                    pe.wait_ge(ln_xnT[1], b * KT + 1)
                    ln_transpose(pe, 1, b, 6)
                pe.wait_ge(ln_xnT[1], B * KT + 1)

                def project(bank, w_s, rhs):
                    for k in range(KT):
                        last = pe.matmul(ps[:, bank, :], w_s[:, k, :], rhs(k), start=k == 0, stop=k == KT - 1)
                    return last

                own = lambda n: lambda k: xnT[:, k, ds((n // PAIRS) * S, S)]

                def project_k(n):
                    pe.wait_ge(b_w, n * 64 + 64 + 1)
                    project(0, wk_s, own(n))
                    project(1, wm_s, lambda k: memT[:, k, 0:512])
                    project(2, wm_s, lambda k: memT[:, k, 512:1024]).then_inc(b_pk, 1)

                def project_q(n):
                    project(3, wq_s, own(n)).then_inc(b_pq, 1)

                def project_v(n):
                    pe.wait_ge(b_wv, n * 16 + 16 + 1)
                    project(5, wv_s, own(n)).then_inc(b_pv_ps, 1)

                def scores_b(i, u):
                    if u >= 2:
                        pe.wait_ge(b_exp, i * UNITS + u - 2 + 1 + 1)
                    h, qt = u // 4, u % 4
                    for c in range(KC):
                        for part in range(2):
                            last = pe.matmul(ps[:, 3 * (u % 2) + c, :], q_dup[:, h, part, qt * P:(qt + 1) * P],
                                             k_st2[:, h, c * 512:(c + 1) * 512], start=part == 0, stop=part == 1)
                    last.then_inc(b_s, 1)

                def bank_free(i, cc):
                    u, c = cc // 3, cc % 3
                    if cc < 0:
                        pe.wait_ge(b_x, i + 1)
                    elif c == 1:
                        pe.wait_ge(b_pt_dve, i * 9 + u + 1 + 1)
                    else:
                        pe.wait_ge(b_pt_act, i * 18 + 2 * u + (1 if c == 0 else 2) + 1)

                def turn(i, u):
                    if u < 0:
                        pe.wait_ge(b_v_f, i + 1 + 1)
                    else:
                        pe.wait_ge(b_prob, i * UNITS + u + 1 + 1)
                    for c in range(3):
                        cc = 3 * (u + 1) + c
                        bank_free(i, cc - 2)
                        for m in range(4):
                            src = kv_f[:, (3, 1, 2)[c], m * P:(m + 1) * P] if u < 0 else \
                                prob[:, u % NPROB, (4 * c + m) * P:(4 * c + m + 1) * P]
                            last = pe.transpose(ps[:, 6 + cc % 2, m * P:(m + 1) * P], src, ident[:, :])
                        last.then_inc(b_pt, 1)

                def pe_pair(i, following):
                    pe.wait_ge(b_khi_act, i + 1 + 1)
                    pe.wait_ge(b_lo, i * 6 + 6 + 1)
                    scores_b(i, 0)
                    pe.wait_ge(b_v_f, i + 1 + 1)
                    scores_b(i, 1)
                    turn(i, -1)
                    scores_b(i, 2)
                    for u in range(3, UNITS):
                        scores_b(i, u)
                        turn(i, u - 3)
                    if following:
                        pe.wait_ge(b_exp, i * UNITS + UNITS - 1 + 1)
                        project_k(i + 1)
                    turn(i, UNITS - 3)
                    if following:
                        pe.wait_ge(b_exp, i * UNITS + UNITS + 1)
                        project_q(i + 1)
                    turn(i, UNITS - 2)
                    turn(i, UNITS - 1)
                    pe.wait_ge(b_pt_act, i * 18 + 18 + 1)
                    pe.wait_ge(b_pt_dve, i * 9 + 9 + 1)
                    for kt in range(KEY_TILES):
                        for h in range(2):
                            last = pe.matmul(ps[64 * h:64 * h + 64, 4, :], v_b[:, kt, 64 * h:64 * h + 64],
                                             probT[:, h, kt, :], start=kt == 0, stop=kt == KEY_TILES - 1)
                    last.then_inc(b_out, 1)
                    if following:
                        project_v(i + 1)
                    pe.wait_ge(b_o, i + 1 + 1)
                    pe.wait_ge(b_wo, i * 16 + 16 + 1)
                    for t in range(TPB):
                        last = pe.matmul(ps[:, 6 + t // 2, (t % 2) * D:(t % 2 + 1) * D], oT[:, t * P:(t + 1) * P],
                                         wo_s[:, :], start=True, stop=True)
                    last.then_inc(b_y, 1)

                project_k(0)
                project_q(0)
                project_v(0)
                with pe.Fori(0, B * PAIRS - 1) as i:
                    pe_pair(i, True)
                pe_pair(B * PAIRS - 1, False)
            end_stage(pe, 2)
            if last_stage >= 3:
                pe.wait_ge(load_c, 160)
                with pe.Fori(0, TPB) as p:
                    pe.wait_ge(c_yT, p * KT + 1)
                    ln_transpose(pe, 2, p, 6)
                    pe.wait_ge(ln_xnT[2], p * KT + 2 + 1)
                    pe.wait_ge(c_dve, p * C_ALL + 1)
                    for t in range(B):
                        for k in range(KT):
                            pe.matmul(ps[:, t, :], uT[:, k, t * P:(t + 1) * P], wqkv_c[:, k, 0:2 * D],
                                      start=k == 0, stop=k == KT - 1)
                    for t in range(B):
                        for k in range(KT):
                            last = pe.matmul(ps[:, 4 + t // 2, (t % 2) * D:(t % 2 + 1) * D],
                                             uT[:, k, t * P:(t + 1) * P], wqkv_c[:, k, 2 * D:3 * D],
                                             start=k == 0, stop=k == KT - 1)
                    last.then_inc(c_qk_ps, 1)
                    pe.wait_ge(c_dve, p * C_ALL + C_O + 1)
                    for k in range(KT):
                        for t in range(B):
                            last = pe.transpose(ps[:, 6 + k, t * P:(t + 1) * P], o_c[:, t, k * P:(k + 1) * P], ident[:, :])
                        last.then_inc(c_otr, 1)
                    pe.wait_ge(c_oT, p * KT + 2 + 1)
                    for t in range(B):
                        for k in range(KT):
                            last = pe.matmul(ps[:, t // 2, (t % 2) * D:(t % 2 + 1) * D], oT_c[:, k, t * P:(t + 1) * P],
                                             wo_c[:, k, :], start=k == 0, stop=k == KT - 1)
                    last.then_inc(c_proj, 1)
                    pe.wait_ge(c_dve, p * C_ALL + C_Y + 1)
                    for k in range(KT):
                        for t in range(B):
                            last = pe.transpose(ps[:, 6 + k, t * P:(t + 1) * P], r_c[:, t, k * P:(k + 1) * P], ident[:, :])
                        last.then_inc(c_ytr, 1)
                    pe.wait_ge(c_yT, p * KT + 2 + 1)
                    for t in range(B):
                        for k in range(KT):
                            last = pe.matmul(ps[:, 4, t * E:(t + 1) * E], yT_c[:, k, t * P:(t + 1) * P], wg_c[:, k, :],
                                             start=k == 0, stop=k == KT - 1)
                    last.then_inc(c_lg, 1)
            end_stage(pe, 3)
            if last_stage >= 3:
                with pe.Fori(0, E // 2) as i:
                    for q in range(2):
                        pe.wait_ge(e_w[q], i * 32 + 32 + 1)
                        pe.sem_inc(alone, 1)
                        with pe.Fori(0, B) as c:
                            n = pe.snap(i * 8 + q * 4 + c)
                            for f in range(FT):
                                if f >= 4:
                                    pe.wait_ge(e_h, n * FT + f - 3 + 1)
                                for k in range(KT):
                                    last = pe.matmul(ps[:, f % 4, :], w1[:, q, k, f * P:(f + 1) * P],
                                                     yT[:, k, ds(c * S, S)], start=k == 0, stop=k == KT - 1)
                                last.then_inc(e_h_ps, 1)
                            pe.wait_ge(e_h, n * FT + FT + 1)
                            for t in range(TPB):
                                pe.wait_ge(e_t, n * 4 + 1)
                                for f in range(FT):
                                    last = pe.matmul(ps[:, 4 + t, 0:D], hT[:, f, t * P:(t + 1) * P], w2[:, q, f, :],
                                                     start=f == 0, stop=f == FT - 1)
                                last.then_inc(e_o_ps, 1)


def layout(inputs):
    a = {k: np.ascontiguousarray(np.asarray(v)) for k, v in inputs.items()}
    pos = np.arange(S, dtype=np.float32)[:, None]
    di = np.arange(0, DA, 2, dtype=np.float32) / np.float32(DA)
    theta = pos * np.exp(-di * np.float32(np.log(10000.0))).astype(np.float32)
    cos = np.repeat(np.cos(theta), 2, axis=1).astype(np.float32)
    sin = np.repeat(np.sin(theta), 2, axis=1).astype(np.float32)
    sign = np.concatenate([-np.ones(DA // 2), np.ones(DA // 2)]).astype(np.float32)
    turn = lambda w: np.concatenate([w[1::2], w[::2]])
    qg, qb, kg, kb = (a["L0_attn_" + n] for n in ("q_gamma", "q_beta", "k_gamma", "k_beta"))
    inner = HB * DB
    return {
        "x": a["x"].reshape(B * S, D),
        "ident": np.eye(P, dtype=np.float32),
        "mask": np.triu(np.full((P, P), -1e30, np.float32), 1),
        "cos": cos, "sin": sin * sign,
        "gb": np.concatenate([qg, kg, turn(qg), turn(kg), qb, kb, turn(qb), turn(kb)]),
        "a_wqkv": np.concatenate([a["L0_attn_Wq"].T, a["L0_attn_Wk"].T, a["L0_attn_Wv"].T], axis=1),
        "a_wo": a["L0_attn_Wo"].T, "a_bo": a["L0_attn_bo"],
        "ctxT": a["ctx_1024"].transpose(0, 2, 1),
        "ln_g": a["L0_xattn_ln_g"].reshape(KT, P).T, "ln_b": a["L0_xattn_ln_b"].reshape(KT, P).T, "b_bo": a["L0_xattn_bo"],
        "b_wq": a["L0_xattn_Wq"], "b_wk": a["L0_xattn_Wkv"][:, :inner], "b_wv": a["L0_xattn_Wkv"][:, inner:],
        "b_wm": a["L0_xattn_Wm"], "b_wo": a["L0_xattn_Wo"],
        "c_wqkv": a["L0_ffn_Wqkv"].T, "c_wo": a["L0_ffn_Wo"].T, "c_wg": a["L0_ffn_Wg"].T,
        "c_bqkv": a["L0_ffn_bqkv"], "c_bo": a["L0_ffn_bo"],
        "c_g1": a["L0_ffn_g1"], "c_be1": a["L0_ffn_be1"], "c_g2": a["L0_ffn_g2"], "c_be2": a["L0_ffn_be2"],
        "rank": np.arange(E, dtype=np.float32),
        "w1": a["L0_ffn_W1"], "b1": a["L0_ffn_b1"].reshape(E, FT, P).transpose(2, 0, 1), "w2": a["L0_ffn_W2"], "b2": a["L0_ffn_b2"].reshape(E * D),
    }


def kernel(**inputs):
    import concourse.bacc as _bacc
    from concourse.bass_utils import run_bass_kernel_spmd as _run

    nc = _bacc.Bacc("TRN2", target_bir_lowering=False, num_devices=1)
    arrays, io = {}, {}
    for name, v in layout(inputs).items():
        v = np.ascontiguousarray(v)
        arrays["in_" + name] = v
        io[name] = nc.dram_tensor("in_" + name, v.shape, mybir.dt.from_np(v.dtype), kind="ExternalInput").ap()
    out = nc.dram_tensor("out_0", (B * S, D), F32, kind="ExternalOutput").ap()
    build(nc, io, out)
    r = _run(nc, [arrays], core_ids=[0])
    return r.results[0]["out_0"].reshape(B, S, D)
```

```python
from contextlib import ExitStack

import numpy as np
import concourse.bass as bass
from concourse import mybir

F32 = mybir.dt.float32
F32R = mybir.dt.float32r
ALU = mybir.AluOpType
ACT = mybir.ActivationFunctionType
AX = mybir.AxisListType.X
ds = bass.ds

P = 128
B, S, D = 4, 512, 256
KT = D // P
TPB = S // P
NT = B * TPB
EPS = 1e-5

HA, DA = 16, 16
QUADS = HA // 4
NQ = B * QUADS
TRI = [0, 128, 384, 768]
TRI_KEYS = [0, 512, 896, 1152]
TRI_LEN = 1280
HB, DB = 16, 64
CTX = 1024
KEYS = S + CTX
TRI_BLOCKS = [[(0, 0), (0, 1), (0, 2), (0, 3)], [(1, 1), (1, 2), (1, 3)], [(2, 2), (2, 3), (3, 3)]]
KC = KEYS // 512
KEY_TILES = KEYS // P
PAIRS = HB // 2
CHUNKS = 27
NPROB = 4
UNITS = 2 * TPB
A_ROPE = 12
C_O, C_Y, C_ALL = 22, 29, 40
HC, DC = 4, 64
E, DF = 8, 1024
FT = DF // P
MT = (B * S + E * (P - 1)) // P
STEPS = MT - 1
assert MT % 2 == 1
W1_LEN, W2_LEN = KT * DF, FT * D
X1_LEN, X2_LEN = W1_LEN + FT, W2_LEN + D


class Chain:

    def __init__(self, eng, sem, base, per, alone=None):
        self.alone = alone
        self.eng, self.sem, self.base, self.per, self.k = eng, sem, base, per, 0

    def link(self, ins):
        self.k += 1
        ins.then_inc(self.sem, 1)
        self.eng.wait_ge(self.sem, self.base + self.k + 1)
        if self.alone is not None:
            self.eng.sem_inc(self.alone, 1)

    def done(self):
        assert self.k == self.per, (self.k, self.per)


def build(nc, io, out, last_stage=3):
    top = ExitStack()
    with top:
        def sb(name, shape, dt=F32, ctx=top):
            return ctx.enter_context(nc.sbuf_tensor(name, shape, dt))

        def sem(name):
            return top.enter_context(nc.semaphore(name))

        ps = top.enter_context(nc.psum_tensor("ps", [P, 8, 512], F32))

        x_sb = sb("x_sb", [P, NT, D])
        ident = sb("ident", [P, P])
        ident_r = sb("ident_r", [P, P], F32R)
        mask = sb("mask", [P, P])
        mask_r = sb("mask_r", [P, P], F32R)
        neg_half = sb("neg_half", [P, P])
        stats = sb("stats", [P, TPB, 6])
        mv = sb("mv", [P, TPB, 2])
        ve = sb("ve", [P, TPB])
        rstd = sb("rstd", [P, TPB])
        ve2 = sb("ve2", [P, TPB])
        rstd2 = sb("rstd2", [P, TPB])
        xn = sb("xn", [P, TPB, D])

        ctx_a = ExitStack()
        wqkv_a = sb("wqkv_a", [P, KT, 3 * D], ctx=ctx_a)
        wo_a = sb("wo_a", [P, QUADS, D], ctx=ctx_a)
        bo_a = sb("bo_a", [P, D], ctx=ctx_a)
        rope_cos = sb("rope_cos", [P, TPB, DA], ctx=ctx_a)
        rope_sin = sb("rope_sin", [P, TPB, DA], ctx=ctx_a)
        gb = sb("gb", [P, 8, DA], ctx=ctx_a)
        t_cos = sb("t_cos", [P, TPB, 2, DA], ctx=ctx_a)
        t_sin = sb("t_sin", [P, TPB, 2, DA], ctx=ctx_a)
        t_add = sb("t_add", [P, TPB, 2, DA], ctx=ctx_a)
        t_add2 = sb("t_add2", [P, TPB, 2, DA], ctx=ctx_a)
        xnT_a = sb("xnT_a", [P, KT, S], ctx=ctx_a)
        qk = sb("qk", [P, TPB, 2 * D], ctx=ctx_a)
        cen = sb("cen", [P, TPB, 2 * D], ctx=ctx_a)
        sq = sb("sq", [P, TPB, 2 * D], ctx=ctx_a)
        qkr = sb("qkr", [P, NT, 2 * D], ctx=ctx_a)
        v_nat = sb("v_nat", [P, NT, D], ctx=ctx_a)
        hsum = sb("hsum", [P, TPB * 32], ctx=ctx_a)
        hmean = sb("hmean", [P, TPB * 32], ctx=ctx_a)
        hvar = sb("hvar", [P, TPB * 32], ctx=ctx_a)
        hstd = sb("hstd", [P, TPB * 32], ctx=ctx_a)
        hrstd = sb("hrstd", [P, TPB * 32], ctx=ctx_a)
        q_st = sb("q_st", [P, TPB, 4, 4 * DA], F32R, ctx=ctx_a)
        k_st = sb("k_st", [P, TPB, 4, 4 * DA], F32R, ctx=ctx_a)
        qT_a = sb("qT_a", [P, 2, S], F32R, ctx=ctx_a)
        kT_a = sb("kT_a", [P, 2, S], F32R, ctx=ctx_a)
        v_pad = sb("v_pad", [P, TPB, 4, 32], ctx=ctx_a)
        prob_a = sb("prob_a", [P, 4, TRI_LEN], ctx=ctx_a)
        probT_a = sb("probT_a", [P, 4, TRI_LEN], ctx=ctx_a)
        nmax_a = sb("nmax_a", [P, 4, TPB], ctx=ctx_a)
        rsum_a = sb("rsum_a", [P, 4, TPB], ctx=ctx_a)
        rinv_a = sb("rinv_a", [P, 4, TPB], ctx=ctx_a)
        oT_a = sb("oT_a", [P, S], ctx=ctx_a)
        ctx_a.close()

        ctx_b = ExitStack()
        xnT = sb("xnT", [P, KT, NT * P], ctx=ctx_b)
        lng = sb("lng", [P, KT], ctx=ctx_b)
        lnb = sb("lnb", [P, KT], ctx=ctx_b)
        bo_b = sb("bo_b", [P, D], ctx=ctx_b)
        wq_s = sb("wq_s", [P, KT, P], ctx=ctx_b)
        wk_s = sb("wk_s", [P, KT, P], ctx=ctx_b)
        wv_s = sb("wv_s", [P, KT, P], ctx=ctx_b)
        wm_s = sb("wm_s", [P, KT, P], ctx=ctx_b)
        wo_s = sb("wo_s", [P, D], ctx=ctx_b)
        memT = sb("memT", [P, KT, CTX], ctx=ctx_b)
        q_dup = sb("q_dup", [P, 2, 2, S], F32R, ctx=ctx_b)
        k_st2 = sb("k_st2", [P, 2, KEYS], F32R, ctx=ctx_b)
        kv_f = sb("kv_f", [P, 4, 512], ctx=ctx_b)
        v_b = sb("v_b", [P, KEY_TILES, P], ctx=ctx_b)
        prob = sb("prob", [P, NPROB, KEYS], ctx=ctx_b)
        probT = sb("probT", [P, 2, KEY_TILES, S], ctx=ctx_b)
        nmax = sb("nmax", [P, UNITS], ctx=ctx_b)
        rsum = sb("rsum", [P, UNITS], ctx=ctx_b)
        rinv = sb("rinv", [P, UNITS], ctx=ctx_b)
        oT = sb("oT", [P, S], ctx=ctx_b)
        ctx_b.close()

        y_sb = sb("y_sb", [P, NT, D])
        emask = sb("emask", [P, NT, E])
        g2 = sb("g2", [P, D])
        be2 = sb("be2", [P, D])
        zeros = sb("zeros", [P, D])
        before = sb("before", [P, P])
        ones = sb("ones", [P, P])
        route_c = sb("route_c", [P, NT + E * E + MT])
        lane = sb("lane", [P, 1])
        ctx_c = ExitStack()
        wqkv_c = sb("wqkv_c", [P, KT, 3 * D], ctx=ctx_c)
        wo_c = sb("wo_c", [P, KT, D], ctx=ctx_c)
        wg_c = sb("wg_c", [P, KT, E], ctx=ctx_c)
        bqkv = sb("bqkv", [P, 3 * D], ctx=ctx_c)
        bo_c = sb("bo_c", [P, D], ctx=ctx_c)
        g1 = sb("g1", [P, D], ctx=ctx_c)
        be1 = sb("be1", [P, D], ctx=ctx_c)
        rank = sb("rank", [P, E], ctx=ctx_c)
        uT = sb("uT", [P, KT, S], ctx=ctx_c)
        qkv = sb("qkv", [P, TPB, 3 * D], ctx=ctx_c)
        prod = sb("prod", [P, B, D], ctx=ctx_c)
        prod2 = sb("prod2", [P, B, D], ctx=ctx_c)
        sc = sb("sc", [P, B, B, HC], ctx=ctx_c)
        scm = sb("scm", [P, B, HC], ctx=ctx_c)
        scs = sb("scs", [P, B, HC], ctx=ctx_c)
        o_c = sb("o_c", [P, B, D], ctx=ctx_c)
        r_c = sb("r_c", [P, B, D], ctx=ctx_c)
        oT_c = sb("oT_c", [P, KT, S], ctx=ctx_c)
        yT_c = sb("yT_c", [P, KT, S], ctx=ctx_c)
        lg = sb("lg", [P, B, E], ctx=ctx_c)
        lgm = sb("lgm", [P, B], ctx=ctx_c)
        lge = sb("lge", [P, B, E], ctx=ctx_c)
        lgi = sb("lgi", [P, B], ctx=ctx_c)
        ctx_c.close()
        x1 = sb("x1", [P, 2, X1_LEN])
        x2 = sb("x2", [P, 2, X2_LEN])
        w1 = lambda q: x1[:, q, 0:W1_LEN].rearrange("p (k n) -> p k n", n=DF)
        w2 = lambda q: x2[:, q, 0:W2_LEN].rearrange("p (f n) -> p f n", n=D)
        r_over = sb("r_over", [P, E, NT])
        r_cnt = sb("r_cnt", [P, E])
        r_tiles = sb("r_tiles", [P, E])
        r_low = sb("r_low", [P, E, E])
        r_start = sb("r_start", [P, E])
        r_end = sb("r_end", [P, E])
        r_slot = sb("r_slot", [P, NT, E])
        r_posf = sb("r_posf", [P, NT])
        r_past = sb("r_past", [P, MT, E - 1])
        r_exp = sb("r_exp", [P, MT])
        r_pos = sb("r_pos", [P, NT], mybir.dt.int32)
        r_row = sb("r_row", [P, MT], mybir.dt.int32)
        row_q = sb("row_q", [P, 4], mybir.dt.int32)
        ys = sb("ys", [P, 2, D])
        ysT = sb("ysT", [P, 2, KT, P])
        hT = sb("hT", [P, 2, FT, P])
        eo = sb("eo", [P, 2, D])
        moe = sb("moe", [P, NT, D])
        sorted_y = nc.dram_tensor("sorted_y", (MT * P, D), F32, kind="Internal").ap()
        sorted_o = nc.dram_tensor("sorted_o", (MT * P, D), F32, kind="Internal").ap()
        z = sb("z", [P, TPB, D])

        load_x = sem("load_x")
        load_a = sem("load_a")
        load_b = sem("load_b")
        load_c = sem("load_c")
        load_e = sem("load_e")
        stage_end = sem("stage_end")
        alone = sem("alone")
        const_set = sem("const_set")
        counters = []

        def counter(name):
            counters.append(sem(name))
            return counters[-1]

        dve_setup = counter("dve_setup")
        ln_dve = [counter(f"ln_dve_{s}") for s in "abc"]
        ln_var = [counter(f"ln_var_{s}") for s in "abc"]
        ln_rstd = [counter(f"ln_rstd_{s}") for s in "abc"]
        ln_xn = [counter(f"ln_xn_{s}") for s in "abc"]
        ln_tr = [counter(f"ln_tr_{s}") for s in "abc"]
        ln_xnT = [counter(f"ln_xnT_{s}") for s in "abc"]
        bias_added = [counter(f"bias_added_{s}") for s in "abc"]
        a_qk_ps, a_v_ps, a_qk, a_v = counter("a_qk_ps"), counter("a_v_ps"), counter("a_qk"), counter("a_v")
        a_cen, a_sq, a_hvar, a_hstd = counter("a_cen"), counter("a_sq"), counter("a_hvar"), counter("a_hstd")
        a_norm_qk, a_rot, a_rope = counter("a_norm_qk"), counter("a_rot"), counter("a_rope")
        a_hi, a_lo, a_tr = counter("a_hi"), counter("a_lo"), counter("a_tr")
        a_T_act, a_T_dve = counter("a_T_act"), counter("a_T_dve")
        a_s, a_max, a_exp, a_rinv, a_prob = counter("a_s"), counter("a_max"), counter("a_exp"), counter("a_rinv"), counter("a_prob")
        a_pt, a_pt_act, a_pt_dve = counter("a_pt"), counter("a_pt_act"), counter("a_pt_dve")
        a_vpad, a_pv, a_o, a_y, a_x = counter("a_vpad"), counter("a_pv"), counter("a_o"), counter("a_y"), counter("a_x")
        b_w, b_wv, b_wo = counter("b_w"), counter("b_wv"), counter("b_wo")
        b_pq, b_pk, b_pv_ps, b_v_f = counter("b_pq"), counter("b_pk"), counter("b_pv_ps"), counter("b_v_f")
        b_hi, b_lo, b_kv, b_vtr, b_v = counter("b_hi"), counter("b_lo"), counter("b_kv"), counter("b_vtr"), counter("b_v")
        b_khi_act, b_khi_dve = counter("b_khi_act"), counter("b_khi_dve")
        b_s, b_max, b_exp, b_rinv, b_prob = counter("b_s"), counter("b_max"), counter("b_exp"), counter("b_rinv"), counter("b_prob")
        b_pt, b_pt_act, b_pt_dve = counter("b_pt"), counter("b_pt_act"), counter("b_pt_dve")
        b_out, b_o, b_y, b_x = counter("b_out"), counter("b_o"), counter("b_y"), counter("b_x")
        c_qk_ps, c_dve, c_exp_in, c_exp = counter("c_qk_ps"), counter("c_dve"), counter("c_exp_in"), counter("c_exp")
        c_otr, c_oT, c_proj, c_var, c_rstd = counter("c_otr"), counter("c_oT"), counter("c_proj"), counter("c_var"), counter("c_rstd")
        c_ytr, c_yT, c_lg = counter("c_ytr"), counter("c_yT"), counter("c_lg")
        r_ps, r_dve, r_rows, r_slots = counter("r_ps"), counter("r_dve"), counter("r_rows"), counter("r_slots")
        zeroed, zero_set = counter("zeroed"), counter("zero_set")
        row_set = counter("row_set")
        e_scat, e_back = sem("e_scat"), sem("e_back")
        e_w1 = [sem("e_w1_0"), sem("e_w1_1")]
        e_w2 = [sem("e_w2_0"), sem("e_w2_1")]
        e_y = [counter("e_y0"), counter("e_y1")]
        e_st = [counter("e_st0"), counter("e_st1")]
        e_tr, e_yT, e_h_ps, e_h = counter("e_tr"), counter("e_yT"), counter("e_h_ps"), counter("e_h")
        e_o_ps, e_o = counter("e_o_ps"), counter("e_o")
        z_dve, z_var, z_rstd, z_out, stored = counter("z_dve"), counter("z_var"), counter("z_rstd"), counter("z_out"), counter("stored")

        block = top.enter_context(nc.Block())
        ENGINES = 5

        def end_stage(eng, n):
            eng.drain().then_inc(stage_end, 1)
            eng.wait_ge(stage_end, ENGINES * n)

        def cast(ap):
            return ap.bitcast(F32)

        def rotated(eng, half):
            nv = qk[:, :, :].rearrange("p t (c h d two) -> p (t c) h d two", c=2, h=HA, two=2)
            mv2 = cen[:, :, :].rearrange("p t (c h e d) -> p (t c) h e d", c=2, h=HA, e=2)[:, :, :, half, :]
            ts = t_sin[:, :, :, :].rearrange("p t c (e d) -> p (t c) e d", e=2)[:, :, half, :]
            return eng.tensor_tensor(mv2, nv[:, :, :, :, 1 - half],
                                     ts.unsqueeze(2).broadcast_to([P, 2 * TPB, HA, DA // 2]), ALU.mult)


        def ln_stats(v, s, j, tiles, chained=1):
            per = 3 + 2 * (chained - 1)
            c = Chain(v, ln_dve[s], j * per, per, alone)
            for t in range(TPB):
                last = v.bn_stats(stats[:, t, :], tiles(t))
            c.link(last)
            for t in range(TPB):
                last = v.bn_aggr(mv[:, t, :], stats[:, t, :])
            c.link(last)
            v.tensor_scalar(ve[:, :], mv[:, :, 1], EPS, None, ALU.add).then_inc(ln_var[s], 1)
            v.wait_ge(ln_rstd[s], j * chained + 2)
            if chained == 2:
                c.link(v.tensor_tensor(ve2[:, :], mv[:, :, 1], rstd[:, :], ALU.mult))
                c.link(v.tensor_tensor(ve2[:, :], ve2[:, :], rstd[:, :], ALU.mult))
                v.tensor_scalar(ve2[:, :], ve2[:, :], EPS, None, ALU.add).then_inc(ln_var[s], 1)
                v.wait_ge(ln_rstd[s], j * chained + 2 + 1)
                c.link(v.tensor_tensor(rstd[:, :], rstd[:, :], rstd2[:, :], ALU.mult))
            else:
                c.link(v.tensor_copy(rstd2[:, :], rstd[:, :]))
            c.done()
            v.wait_ge(ln_tr[s], j * KT + 1)
            for t in range(TPB):
                last = v.tensor_scalar(xn[:, t, :], tiles(t), mv[:, t, 0:1], rstd[:, t:t + 1],
                                       ALU.subtract, ALU.mult)
            last.then_inc(ln_xn[s], 1)

        def ln_power(g, s, j, chained=1):
            g.wait_ge(ln_var[s], j * chained + 2)
            if chained == 2:
                g.wait_ge(ln_xn[s], j + 1)
            g.tensor_tensor(rstd[:, :], ve[:, :], neg_half[:, 0:TPB], ALU.pow).then_inc(ln_rstd[s], 1)
            if chained == 2:
                g.wait_ge(ln_var[s], j * chained + 2 + 1)
                g.tensor_tensor(rstd2[:, :], ve2[:, :], neg_half[:, 0:TPB], ALU.pow).then_inc(ln_rstd[s], 1)

        def ln_transpose(pe, s, j, bank):
            pe.wait_ge(ln_xn[s], j + 2)
            for k in range(KT):
                for t in range(TPB):
                    last = pe.transpose(ps[:, bank + k, t * P:(t + 1) * P], xn[:, t, k * P:(k + 1) * P], ident[:, :])
                last.then_inc(ln_tr[s], 1)

        def row(ap, n):
            return ap.rearrange("(a n) -> a n", a=1).broadcast_to([P, n])

        @block.sync
        def _(sp):
            sp.dma_start(x_sb[:, :, :], io["x"].rearrange("(t p) d -> p t d", p=P)).then_inc(load_x, 16)
            sp.dma_start(ident[:, :], io["ident"]).then_inc(load_a, 16)
            sp.dma_start(mask[:, :], io["mask"]).then_inc(load_a, 16)
            sp.dma_start(wqkv_a[:, :, :], io["a_wqkv"].rearrange("(k p) n -> p k n", p=P)).then_inc(load_a, 16)
            sp.dma_start(rope_cos[:, :, :], io["cos"].rearrange("(t p) d -> p t d", p=P)).then_inc(load_a, 16)
            sp.dma_start(rope_sin[:, :, :], io["sin"].rearrange("(t p) d -> p t d", p=P)).then_inc(load_a, 16)
            sp.dma_start(gb[:, :, :].rearrange("p a d -> p (a d)"), row(io["gb"], 8 * DA)).then_inc(load_a, 16)
            sp.dma_start(bo_a[:, :], row(io["a_bo"], D)).then_inc(load_a, 16)
            for c in counters:
                sp.sem_inc(c, 1)
            sp.wait_ge(const_set, 1)
            for h in range(4):
                sp.dma_start(wo_a[32 * h:32 * h + DA, :, :],
                             io["a_wo"].rearrange("(g h d) n -> h d g n", h=4, d=DA)[h]).then_inc(load_a, 16)
            end_stage(sp, 1)
            if last_stage >= 2:
                sp.dma_start(lng[:, :], io["ln_g"]).then_inc(load_b, 16)
                sp.dma_start(lnb[:, :], io["ln_b"]).then_inc(load_b, 16)
                sp.dma_start(bo_b[:, :], row(io["b_bo"], D)).then_inc(load_b, 16)
                with sp.Fori(0, B * PAIRS) as i:
                    b = sp.snap(i // PAIRS)
                    hp = sp.snap(i % PAIRS)
                    sp.wait_ge(b_pq, i + 1)
                    for w_s, name in ((wq_s, "b_wq"), (wk_s, "b_wk"), (wm_s, "b_wm")):
                        sp.dma_start(w_s[:, :, :], io[name].rearrange("(k p) (h n) -> h p k n", p=P, n=P)[hp])\
                            .then_inc(b_w, 16)
                    sp.dma_start(memT[:, :, :], io["ctxT"].rearrange("b (k p) n -> b p k n", p=P)[b])\
                        .then_inc(b_w, 16)
                    sp.wait_ge(b_pv_ps, i + 1)
                    sp.dma_start(wv_s[:, :, :], io["b_wv"].rearrange("(k p) (h n) -> h p k n", p=P, n=P)[hp])\
                        .then_inc(b_wv, 16)
                    sp.wait_ge(b_y, i + 1)
                    sp.dma_start(wo_s[:, :], io["b_wo"].rearrange("(h p) n -> h p n", p=P)[hp]).then_inc(b_wo, 16)
            end_stage(sp, 2)
            if last_stage >= 3:
                sp.wait_ge(zero_set, 1 + 1)
                sp.dma_start(sorted_y.rearrange("(j p) d -> p j d", p=P),
                             zeros[:, :].unsqueeze(1).broadcast_to([P, MT, D])).then_inc(zeroed, 16)
                for dst, src in ((wqkv_c, "c_wqkv"), (wo_c, "c_wo"), (wg_c, "c_wg")):
                    sp.dma_start(dst[:, :, :], io[src].rearrange("(k p) n -> p k n", p=P)).then_inc(load_c, 16)
                for dst, src, n in ((bqkv, "c_bqkv", 3 * D), (bo_c, "c_bo", D), (g1, "c_g1", D), (be1, "c_be1", D),
                                    (g2, "c_g2", D), (be2, "c_be2", D), (rank, "rank", E)):
                    sp.dma_start(dst[:, :], row(io[src], n)).then_inc(load_c, 16)
                sp.dma_start(route_c[:, :], row(io["route"], NT + E * E + MT)).then_inc(load_e, 16)
                for dst, src in ((lane, "lane"), (before, "before"), (ones, "ones")):
                    sp.dma_start(dst[:, :], io[src]).then_inc(load_e, 16)
            end_stage(sp, 3)
            if last_stage >= 3:
                ysv = sorted_y.rearrange("(j p) d -> j p d", p=P)
                eov = sorted_o.rearrange("(j p) d -> j p d", p=P)

                def load_tile(n, q):
                    sp.dma_start(ys[:, q, :], ysv[n]).then_inc(e_y[q], 16)

                def sp_step(i, q, ahead):
                    n = i * 2 + q
                    if ahead:
                        sp.wait_ge(e_tr, n + 1 + 1)
                        load_tile(n + 2, q)
                    sp.wait_ge(e_o, n + 1 + 1)
                    sp.dma_start(eov[n], eo[:, q, :]).then_inc(e_st[q], 16)

                sp.wait_ge(e_scat, 16 * NT)
                load_tile(0, 0)
                load_tile(1, 1)
                with sp.Fori(0, MT // 2 - 1) as i:
                    for q in range(2):
                        sp_step(i, q, True)
                i = MT // 2 - 1
                sp_step(i, 0, True)
                sp_step(i, 1, False)
                sp_step(i + 1, 0, False)
            outv = out.rearrange("(j t p) d -> j p t d", t=TPB, p=P)
            with sp.Fori(0, B) as j:
                sp.wait_ge(z_out, j + 2)
                sp.dma_start(outv[j], z[:, :, :]).then_inc(stored, 16)
            sp.wait_ge(stored, 16 * B + 1)

        @block.gpsimd
        def _(g):
            g.memset(wo_a[:, :, :], 0.0).then_inc(const_set, 1)
            g.memset(neg_half[:, :], -0.5).then_inc(const_set, 1)
            g.memset(v_pad[:, :, :, :], 0.0).then_inc(const_set, 1)
            g.wait_ge(const_set, 3)
            g.wait_ge(load_a, 16 * 11)
            def pool_rows(b, following):
                if following:
                    ln_power(g, 0, b + 1)
                g.wait_ge(a_norm_qk, b + 1 + 1)
                rotated(g, 0).then_inc(a_rot, 1)
                g.wait_ge(ln_xn[0], b + 1 + 1)
                g.tensor_tensor(x_sb[:, ds(b * TPB, TPB), :], x_sb[:, ds(b * TPB, TPB), :],
                                bo_a[:, :].unsqueeze(1).broadcast_to([P, TPB, D]), ALU.add).then_inc(bias_added[0], 1)

            ln_power(g, 0, 0)
            with g.Fori(0, B - 1) as b:
                pool_rows(b, True)
            pool_rows(B - 1, False)
            g.wait_ge(a_v, B + 1)
            with g.Fori(0, NQ) as n:
                b = g.snap(n // QUADS)
                q = g.snap(n % QUADS)

                def normed(h):
                    g.wait_ge(a_rinv, n * 4 + h + 1 + 1)
                    g.sem_inc(alone, 1)
                    for qt in range(TPB):
                        pr = prob_a[:, h, TRI[qt]:TRI[qt] + (qt + 1) * P]
                        g.tensor_scalar(pr, pr, rinv_a[:, h, qt:qt + 1], 1.0, ALU.mult, ALU.mult)\
                            .then_inc(a_prob, 1)

                normed(0)
                normed(1)
                g.wait_ge(a_pv, n + 1)
                for t in range(TPB):
                    g.tensor_copy(v_pad[:, t, :, 0:DA],
                                  v_nat[:, ds(b * TPB + t, 1), ds(q * 64, 64)].rearrange("p t (h d) -> p (t h) d", h=4))\
                        .then_inc(a_vpad, 1)
                normed(2)
                normed(3)
            end_stage(g, 1)
            if last_stage >= 2:
                g.wait_ge(load_b, 48)
                with g.Fori(0, B) as b:
                    ln_power(g, 1, b, 2)
                    g.wait_ge(ln_xn[1], b + 2)
                    g.tensor_tensor(x_sb[:, ds(b * TPB, TPB), :], x_sb[:, ds(b * TPB, TPB), :],
                                    bo_b[:, :].unsqueeze(1).broadcast_to([P, TPB, D]), ALU.add)\
                        .then_inc(bias_added[1], 1)
                with g.Fori(0, B * PAIRS) as i:
                    for u in range(UNITS):
                        g.wait_ge(b_rinv, i * UNITS + u + 2)
                        g.sem_inc(alone, 1)
                        g.tensor_scalar(prob[:, u % NPROB, :], prob[:, u % NPROB, :], rinv[:, u:u + 1], 1.0, ALU.mult, ALU.mult)\
                            .then_inc(b_prob, 1)
            end_stage(g, 2)
            if last_stage >= 3:
                g.memset(zeros[:, :], 0.0).then_inc(zero_set, 1)
                g.wait_ge(load_c, 160)
                with g.Fori(0, TPB) as p:
                    ln_power(g, 2, p)
                    g.wait_ge(ln_xn[2], p + 2)
                    g.wait_ge(c_var, p + 2)
                    g.tensor_tensor(rstd2[:, :], ve2[:, :], neg_half[:, 0:TPB], ALU.pow).then_inc(c_rstd, 1)
            end_stage(g, 3)
            if last_stage >= 3:
                def load_w(layer, n, q, k):
                    table, dst, signal = ((io["experts1"], x1, e_w1), (io["experts2"], x2, e_w2))[layer]
                    index = row_q[:, 2 * layer + q:2 * layer + q + 1]
                    g.tensor_copy(index, r_row[:, ds(n, 1)]).then_inc(row_set, 1)
                    g.wait_ge(row_set, k + 1 + 1)
                    g.sem_inc(alone, 1)
                    g.indirect_dma_start(dst[:, q, :], None, table, bass.IndirectOffsetOnAxis(ap=index, axis=0))\
                        .then_inc(signal[q], 16)

                def rows_back(j):
                    for t in range(TPB):
                        n = j * TPB + t
                        g.indirect_dma_start(moe[:, n, :], None, sorted_o,
                                             bass.IndirectOffsetOnAxis(ap=r_pos[:, n:n + 1], axis=0)).then_inc(e_back, 16)

                def z_power(j):
                    g.wait_ge(z_var, j + 1 + 1)
                    g.tensor_tensor(rstd2[:, :], ve2[:, :], neg_half[:, 0:TPB], ALU.pow).then_inc(z_rstd, 1)

                g.wait_ge(r_rows, 1 + 1)
                load_w(0, 0, 0, 0)
                g.wait_ge(r_slots, 1 + 1)
                g.wait_ge(zeroed, 16 + 1)
                for t in range(NT):
                    g.indirect_dma_start(sorted_y, bass.IndirectOffsetOnAxis(ap=r_pos[:, t:t + 1], axis=0),
                                         y_sb[:, t, :], None).then_inc(e_scat, 16)
                load_w(1, 0, 0, 1)
                load_w(0, 1, 1, 2)
                load_w(1, 1, 1, 3)
                g.wait_ge(e_h, FT + 1)
                load_w(0, 2, 0, 4)

                def pool_step(i, q):
                    n = i * 2 + q
                    g.wait_ge(e_h, (n + 2) * FT + 1)
                    g.sem_inc(alone, 1)
                    load_w(0, n + 3, 1 - q, n * 2 + 5)
                    g.wait_ge(e_o, n + 1 + 1)
                    g.sem_inc(alone, 1)
                    load_w(1, n + 2, q, n * 2 + 6)

                with g.Fori(0, MT // 2 - 1) as i:
                    for q in range(2):
                        pool_step(i, q)
                g.wait_ge(e_o, MT - 2 + 1)
                load_w(1, MT - 1, 0, 2 * MT - 1)
                g.wait_ge(e_st[0], 16 * (MT // 2 + 1) + 1)
                g.wait_ge(e_st[1], 16 * (MT // 2) + 1)
                rows_back(0)
                for j in range(B - 1):
                    g.wait_ge(e_back, (j + 1) * 16 * TPB)
                    rows_back(j + 1)
                    z_power(j)
                z_power(B - 1)
        @block.scalar
        def _(a):
            a.wait_ge(load_x, 16)
            def xnT_out(b):
                for k in range(KT):
                    a.wait_ge(ln_tr[0], b * KT + k + 1 + 1)
                    a.activation(xnT_a[:, k, :], ps[:, 6 + k, :], ACT.Copy).then_inc(ln_xnT[0], 1)

            def act_rows(b, following):
                a.wait_ge(a_qk_ps, b * 4 + 4 + 1)
                a.wait_ge(a_rope, b * A_ROPE + 1)
                a.activation(qk[:, :, :], ps[:, 0:4, :], ACT.Copy).then_inc(a_qk, 1)
                if following:
                    a.wait_ge(a_v_ps, b + 1 + 1)
                a.wait_ge(a_cen, b + 1 + 1)
                a.activation(sq[:, :, :], cen[:, :, :], ACT.Square).then_inc(a_sq, 1)
                if following:
                    xnT_out(b + 1)
                a.wait_ge(a_hvar, b + 1 + 1)
                a.activation(hstd[:, :], hvar[:, :], ACT.Sqrt).then_inc(a_hstd, 1)

            xnT_out(0)
            with a.Fori(0, B - 1) as b:
                act_rows(b, True)
            act_rows(B - 1, False)

            def high_parts(n, b, q):
                a.wait_ge(a_tr, n * 4 + 1)
                for c, (st, places) in enumerate(((q_st, (0, 2)), (k_st, (0, 1)))):
                    src = qkr[:, ds(b * TPB, TPB), ds(q * 64 + c * D, 64)].rearrange("p t (h d) -> p t h d", h=4)
                    for e in places:
                        a.activation(st[:, :, :, e * DA:(e + 1) * DA], src, ACT.Copy).then_inc(a_hi, 1)

            def T_out_act(n):
                a.wait_ge(a_tr, n * 4 + 1 + 1)
                a.activation(qT_a[:, 0, :], ps[:, 0, :], ACT.Copy).then_inc(a_T_act, 1)
                a.wait_ge(a_tr, n * 4 + 2 + 1)
                a.activation(kT_a[:, 0, :], ps[:, 1, :], ACT.Copy).then_inc(a_T_act, 1)

            def exps(n, h):
                a.wait_ge(a_max, n * 4 + h + 1 + 1)
                base = 3 * (h % 2)
                for qt in range(TPB):
                    bank, off = (base, TRI[qt]) if qt < 2 else (base + qt - 1, 0)
                    last = a.activation(prob_a[:, h, TRI[qt]:TRI[qt] + (qt + 1) * P],
                                        ps[:, bank, off:off + (qt + 1) * P], ACT.Exp,
                                        bias=nmax_a[:, h, qt:qt + 1], accum_out=rsum_a[:, h, qt:qt + 1])
                last.then_inc(a_exp, 1)

            def pta_out(n, h):
                a.wait_ge(a_pt, n * 12 + 3 * h + 1 + 1)
                a.activation(probT_a[:, h, 0:512], ps[:, 6 + (3 + 3 * h) % 2, :], ACT.Copy).then_inc(a_pt_act, 1)

            def oT_out(n):
                a.wait_ge(a_pv, n + 1 + 1)
                a.activation(oT_a[:, :], ps[:, 6, :], ACT.Copy).then_inc(a_o, 1)

            def act_quad(n, b1, q1, first, following):
                exps(n, 0)
                exps(n, 1)
                if not first:
                    oT_out(n - 1)
                exps(n, 2)
                pta_out(n, 0)
                if following:
                    high_parts(n + 1, b1, q1)
                exps(n, 3)
                pta_out(n, 1)
                pta_out(n, 2)
                if following:
                    T_out_act(n + 1)
                pta_out(n, 3)

            a.wait_ge(a_rope, B * A_ROPE + 1)
            high_parts(0, 0, 0)
            T_out_act(0)
            act_quad(0, 0, 1, True, True)
            with a.Fori(1, NQ - 1) as n:
                act_quad(n, a.snap((n + 1) // QUADS), a.snap((n + 1) % QUADS), False, True)
            act_quad(NQ - 1, 0, 0, False, False)
            oT_out(NQ - 1)
            end_stage(a, 1)
            if last_stage >= 2:
                a.wait_ge(load_b, 48)
                with a.Fori(0, B) as b:
                    for k in range(KT):
                        a.wait_ge(ln_tr[1], b * KT + k + 2)
                        a.activation(xnT[:, k, ds(b * S, S)], ps[:, 6 + k, :], ACT.Identity,
                                     bias=lnb[:, k:k + 1], scale=lng[:, k:k + 1]).then_inc(ln_xnT[1], 1)

                def exp(i, u):
                    a.wait_ge(b_max, i * UNITS + u + 1 + 1)
                    if u >= NPROB:
                        a.wait_ge(b_pt, i * CHUNKS + 3 * (u - NPROB) + 6 + 1)
                    a.activation(prob[:, u % NPROB, :], ps[:, 3 * (u % 2):3 * (u % 2) + 3, :], ACT.Exp,
                                 bias=nmax[:, u:u + 1], accum_out=rsum[:, u:u + 1]).then_inc(b_exp, 1)

                def v_out(i, c):
                    a.wait_ge(b_pt, i * CHUNKS + c + 1 + 1)
                    a.wait_ge(b_out, i + 1)
                    a.activation(v_b[:, 4 * c:4 * c + 4, :], ps[:, 6 + c % 2, :], ACT.Copy).then_inc(b_pt_act, 1)

                def pt_out(i, u, chunks=(1, 2)):
                    for c in chunks:
                        a.wait_ge(b_pt, i * CHUNKS + 3 * (u + 1) + c + 1 + 1)
                        a.activation(probT[:, u // 4, 4 * c:4 * c + 4, (u % 4) * P:(u % 4 + 1) * P],
                                     ps[:, 6 + (3 * (u + 1) + c) % 2, :], ACT.Copy).then_inc(b_pt_act, 1)

                def qk_out(n):
                    a.wait_ge(b_pq, n + 1 + 1)
                    for h in range(2):
                        for half in range(2):
                            a.activation(q_dup[64 * half:64 * half + 64, h, 0, :], ps[64 * h:64 * h + 64, 3, :],
                                         ACT.Copy, scale=DB ** -0.5).then_inc(b_hi, 1)
                    a.wait_ge(b_pk, n + 1 + 1)
                    a.activation(kv_f[:, 0:3, :], ps[:, 0:3, :], ACT.Copy).then_inc(b_kv, 1)
                    a.wait_ge(b_kv, n + 1 + 1)
                    a.activation(k_st2[0:64, 0, :], kv_f[0:64, 0:3, :], ACT.Copy).then_inc(b_khi_act, 1)

                def vf_out(n):
                    a.wait_ge(b_pv_ps, n + 1 + 1)
                    a.activation(kv_f[:, 3, :], ps[:, 5, :], ACT.Copy).then_inc(b_v_f, 1)

                def act_pair(i, following):
                    exp(i, 0)
                    v_out(i, 1)
                    exp(i, 1)
                    v_out(i, 2)
                    exp(i, 2)
                    for u in range(3, UNITS):
                        pt_out(i, u - 3)
                        exp(i, u)
                    for u in range(UNITS - 3, UNITS):
                        pt_out(i, u)
                    if following:
                        qk_out(i + 1)
                    a.wait_ge(b_out, i + 1 + 1)
                    a.activation(oT[:, :], ps[:, 4, :], ACT.Copy).then_inc(b_o, 1)
                    if following:
                        vf_out(i + 1)

                qk_out(0)
                vf_out(0)
                with a.Fori(0, B * PAIRS - 1) as i:
                    act_pair(i, True)
                act_pair(B * PAIRS - 1, False)
            end_stage(a, 2)
            if last_stage >= 3:
                with a.Fori(0, TPB) as p:
                    for k in range(KT):
                        a.wait_ge(ln_tr[2], p * KT + k + 2)
                        a.wait_ge(c_qk_ps, p + 1)
                        a.activation(uT[:, k, :], ps[:, 6 + k, :], ACT.Copy).then_inc(ln_xnT[2], 1)
                    a.wait_ge(c_exp_in, p + 2)
                    a.activation(sc[:, :, :, :], sc[:, :, :, :], ACT.Exp, scale=DC ** -0.5).then_inc(c_exp, 1)
                    for k in range(KT):
                        a.wait_ge(c_otr, p * KT + k + 2)
                        a.activation(oT_c[:, k, :], ps[:, 6 + k, :], ACT.Copy).then_inc(c_oT, 1)
                    a.wait_ge(c_lg, p + 1)
                    for k in range(KT):
                        a.wait_ge(c_ytr, p * KT + k + 2)
                        a.activation(yT_c[:, k, :], ps[:, 6 + k, :], ACT.Copy).then_inc(c_yT, 1)
            end_stage(a, 3)
            if last_stage >= 3:
                def act_tile(i, q, used=True):
                    n = i * 2 + q
                    a.wait_ge(e_w1[q], i * 16 + 16)
                    if used:
                        a.wait_ge(e_o_ps, n - 1 + 1)
                    for half in range(2):
                        a.wait_ge(e_h_ps, n * 2 + half + 1 + 1)
                        for f in range(4 * half, 4 * half + 4):
                            a.activation(hT[:, q, f, :], ps[:, 2 * q + half, (f % 4) * P:(f % 4 + 1) * P], ACT.Relu,
                                         bias=x1[:, q, W1_LEN + f:W1_LEN + f + 1]).then_inc(e_h, 1)

                act_tile(0, 0, False)
                act_tile(0, 1, False)
                with a.Fori(1, MT // 2) as i:
                    for q in range(2):
                        act_tile(i, q)
                act_tile(MT // 2, 0)

        @block.vector
        def _(v):
            v.wait_ge(load_a, 16 * 11)
            v.wait_ge(load_x, 16)
            v.wait_ge(const_set, 3)
            c = Chain(v, dve_setup, 0, 8)
            c.link(v.tensor_copy(ident_r[:, :], ident[:, :]))
            c.link(v.tensor_copy(mask_r[:, :], mask[:, :]))
            gbv = gb[:, :, :].rearrange("p (a c) d -> p a c d", c=2)
            c.link(v.tensor_scalar(gbv[:, :, 0, :], gbv[:, :, 0, :], DA ** -0.5, None, ALU.mult))
            full = [P, TPB, 2, DA]

            def table(dst, trig, r):
                return v.tensor_tensor(dst[:, :, :, :], trig[:, :, :].unsqueeze(2).broadcast_to(full),
                                       gb[:, 2 * r:2 * r + 2, :].unsqueeze(1).broadcast_to(full), ALU.mult)

            c.link(table(t_cos, rope_cos, 0))
            c.link(table(t_sin, rope_sin, 1))
            c.link(table(t_add, rope_cos, 2))
            c.link(table(t_add2, rope_sin, 3))
            c.link(v.tensor_tensor(t_add[:, :, :, :], t_add[:, :, :, :], t_add2[:, :, :, :], ALU.add))
            c.done()

            heads = lambda ap: ap[:, :, :].rearrange("p t (h d) -> p (t h) d", d=DA)
            heads4 = lambda ap: ap[:, :, :].rearrange("p t (c h d) -> p (t c) h d", c=2, h=HA)
            tab = lambda ap: ap[:, :, :, :].rearrange("p t c d -> p (t c) d").unsqueeze(2).broadcast_to([P, 8, HA, DA])
            wide = lambda ap: ap[:, :].unsqueeze(2).broadcast_to([P, TPB * 32, DA])
            def dve_rows(b, following):
                v.wait_ge(a_v_ps, b + 1 + 1)
                v.tensor_copy(v_nat[:, ds(b * TPB, TPB), :], ps[:, 4:6, :].rearrange("p a n -> p (a n)")
                              .rearrange("p (t n) -> p t n", n=D)).then_inc(a_v, 1)
                v.wait_ge(a_qk, b + 1 + 1)
                c = Chain(v, a_rope, b * A_ROPE, A_ROPE)
                c.link(v.tensor_reduce(hsum[:, :], heads(qk), AX, ALU.add))
                c.link(v.tensor_scalar(hmean[:, :], hsum[:, :], 1.0 / DA, None, ALU.mult))
                v.tensor_tensor(heads(cen), heads(qk), wide(hmean), ALU.subtract).then_inc(a_cen, 1)
                if following:
                    ln_stats(v, 0, b + 1, lambda t: x_sb[:, ds((b + 1) * TPB + t, 1), :].rearrange("p t d -> p (t d)"))
                v.wait_ge(a_sq, b + 1 + 1)
                c.link(v.tensor_reduce(hsum[:, :], heads(sq), AX, ALU.add))
                v.tensor_scalar(hvar[:, :], hsum[:, :], 1.0 / DA, EPS, ALU.mult, ALU.add).then_inc(a_hvar, 1)
                v.wait_ge(a_hstd, b + 1 + 1)
                c.link(v.reciprocal(hrstd[:, :], hstd[:, :]))
                c.link(v.tensor_tensor(hmean[:, :], hrstd[:, :], hrstd[:, :], ALU.mult))
                c.link(v.tensor_tensor(hmean[:, :], hmean[:, :], hvar[:, :], ALU.mult))
                c.link(v.tensor_scalar(hmean[:, :], hmean[:, :], -0.5, 1.5, ALU.mult, ALU.add))
                c.link(v.tensor_tensor(hrstd[:, :], hrstd[:, :], hmean[:, :], ALU.mult))
                v.tensor_tensor(heads(qk), heads(cen), wide(hrstd), ALU.mult).then_inc(a_norm_qk, 1)
                v.wait_ge(a_norm_qk, b + 1 + 1)
                c.link(v.tensor_tensor(heads4(sq), heads4(qk), tab(t_cos), ALU.mult))
                c.link(rotated(v, 1))
                v.wait_ge(a_rot, b + 1 + 1)
                c.link(v.tensor_tensor(sq[:, :, :], sq[:, :, :], cen[:, :, :], ALU.add))
                c.link(v.tensor_tensor(qkr[:, ds(b * TPB, TPB), :].rearrange("p t (c h d) -> p (t c) h d", c=2, h=HA),
                                       heads4(sq), tab(t_add), ALU.add))
                c.done()

            ln_stats(v, 0, 0, lambda t: x_sb[:, t, :])
            with v.Fori(0, B - 1) as b:
                dve_rows(b, True)
                v.sem_inc(alone, 1)
            dve_rows(B - 1, False)

            def low_parts(n, b, q):
                for c2, (st, places) in enumerate(((q_st, (1, 3)), (k_st, (2, 3)))):
                    src = qkr[:, ds(b * TPB, TPB), ds(q * 64 + c2 * D, 64)].rearrange("p t (h d) -> p t h d", h=4)
                    v.wait_ge(a_hi, n * 4 + 2 * c2 + 1 + 1)
                    for e in places:
                        v.tensor_tensor(st[:, :, :, e * DA:(e + 1) * DA], src,
                                        cast(st[:, :, :, 0:DA]), ALU.subtract).then_inc(a_lo, 1)

            def T_out_dve(n):
                v.wait_ge(a_tr, n * 4 + 3 + 1)
                v.tensor_copy(qT_a[:, 1, :], ps[:, 2, :]).then_inc(a_T_dve, 1)
                v.wait_ge(a_tr, n * 4 + 4 + 1)
                v.tensor_copy(kT_a[:, 1, :], ps[:, 3, :]).then_inc(a_T_dve, 1)

            def maxes(n, h):
                v.wait_ge(a_s, n * 4 + h + 1 + 1)
                base = 3 * (h % 2)
                for qt in range(TPB):
                    bank, off = (base, TRI[qt]) if qt < 2 else (base + qt - 1, 0)
                    last = v.tensor_reduce(nmax_a[:, h, qt:qt + 1], ps[:, bank, off:off + (qt + 1) * P],
                                           AX, ALU.max, negate=True)
                last.then_inc(a_max, 1)

            def inverse(n, h):
                v.wait_ge(a_exp, n * 4 + h + 1 + 1)
                v.reciprocal(rinv_a[:, h, :], rsum_a[:, h, :]).then_inc(a_rinv, 1)

            def pta_out_dve(n, h):
                for j in (1, 2):
                    v.wait_ge(a_pt, n * 12 + 3 * h + j + 1 + 1)
                    v.tensor_copy(probT_a[:, h, 512 + 384 * (j - 1):512 + 384 * j],
                                  ps[:, 6 + (3 + 3 * h + j) % 2, 0:384]).then_inc(a_pt_dve, 1)

            def add_out(n, b):
                for half in range(2):
                    v.wait_ge(a_y, 2 * n + half + 1 + 1)
                    xb = x_sb[:, ds(b * TPB + 2 * half, 2), :]
                    v.tensor_tensor(xb, ps[:, 7 - half, :].rearrange("p (t n) -> p t n", n=D), xb, ALU.add)\
                        .then_inc(a_x, 1)

            def dve_quad(n, b0, b1, q1, first, following):
                maxes(n, 0)
                maxes(n, 1)
                inverse(n, 0)
                if not first:
                    v.wait_ge(a_x, 2 * n - 2 + 1)
                maxes(n, 2)
                inverse(n, 1)
                if not first:
                    add_out(n - 1, b0)
                pta_out_dve(n, 0)
                maxes(n, 3)
                inverse(n, 2)
                pta_out_dve(n, 1)
                if following:
                    low_parts(n + 1, b1, q1)
                inverse(n, 3)
                pta_out_dve(n, 2)
                if following:
                    T_out_dve(n + 1)
                pta_out_dve(n, 3)

            v.wait_ge(a_rope, B * A_ROPE + 1)
            v.wait_ge(bias_added[0], B + 1)
            low_parts(0, 0, 0)
            T_out_dve(0)
            dve_quad(0, 0, 0, 1, True, True)
            with v.Fori(1, NQ - 1) as n:
                dve_quad(n, v.snap((n - 1) // QUADS), v.snap((n + 1) // QUADS), v.snap((n + 1) % QUADS), False, True)
            dve_quad(NQ - 1, B - 1, 0, 0, False, False)
            v.wait_ge(a_x, 2 * NQ - 2 + 1)
            add_out(NQ - 1, B - 1)
            end_stage(v, 1)
            if last_stage >= 2:
                with v.Fori(0, B) as b:
                    ln_stats(v, 1, b, lambda t: x_sb[:, b * TPB + t, :], 2)
                v.wait_ge(bias_added[1], B + 1)

                def rowmax(i, u):
                    v.wait_ge(b_s, i * UNITS + u + 1 + 1)
                    v.tensor_reduce(nmax[:, u:u + 1], ps[:, 3 * (u % 2):3 * (u % 2) + 3, :]
                                    .rearrange("p a n -> p (a n)"), AX, ALU.max, negate=True).then_inc(b_max, 1)

                def inverse_b(i, u):
                    v.wait_ge(b_exp, i * UNITS + u + 1 + 1)
                    v.reciprocal(rinv[:, u:u + 1], rsum[:, u:u + 1]).then_inc(b_rinv, 1)

                def v_out_dve(i):
                    v.wait_ge(b_pt, i * CHUNKS + 1 + 1)
                    v.wait_ge(b_out, i + 1)
                    v.tensor_copy(v_b[:, 0:4, :], ps[:, 6, :].rearrange("p (a n) -> p a n", a=4)).then_inc(b_pt_dve, 1)

                def pt_out_dve(i, u):
                    cc = 3 * (u + 1)
                    v.wait_ge(b_pt, i * CHUNKS + cc + 1 + 1)
                    v.tensor_copy(probT[:, u // 4, 0:4, (u % 4) * P:(u % 4 + 1) * P],
                                  ps[:, 6 + cc % 2, :].rearrange("p (a n) -> p a n", a=4)).then_inc(b_pt_dve, 1)

                def qk_out_dve(n):
                    v.wait_ge(b_hi, n * 4 + 4 + 1)
                    for h in range(2):
                        for half in range(2):
                            v.scalar_tensor_tensor(q_dup[64 * half:64 * half + 64, h, 1, :],
                                                   ps[64 * h:64 * h + 64, 3, :], DB ** -0.5,
                                                   cast(q_dup[64 * h:64 * h + 64, h, 0, :]), ALU.mult, ALU.subtract)\
                                .then_inc(b_lo, 1)
                    v.wait_ge(b_kv, n + 1 + 1)
                    v.tensor_copy(k_st2[64:128, 1, :], kv_f[64:128, 0:3, :].rearrange("p a n -> p (a n)"))\
                        .then_inc(b_khi_dve, 1)
                    for h in (1, 0):
                        v.wait_ge((b_khi_act, b_khi_dve)[h], n + 1 + 1)
                        o = 64 * (1 - h)
                        v.tensor_tensor(k_st2[o:o + 64, h, :], kv_f[64 * h:64 * h + 64, 0:3, :].rearrange("p a n -> p (a n)"),
                                        cast(k_st2[64 * h:64 * h + 64, h, :]), ALU.subtract).then_inc(b_lo, 1)

                def dve_pair(i, b, following):
                    rowmax(i, 1)
                    inverse_b(i, 0)
                    v_out_dve(i)
                    rowmax(i, 2)
                    inverse_b(i, 1)
                    for u in range(3, UNITS):
                        pt_out_dve(i, u - 3)
                        rowmax(i, u)
                        inverse_b(i, u - 1)
                    inverse_b(i, UNITS - 1)
                    for u in range(UNITS - 3, UNITS):
                        pt_out_dve(i, u)
                    if following:
                        qk_out_dve(i + 1)
                        rowmax(i + 1, 0)
                    v.wait_ge(b_y, i + 1 + 1)
                    xb = x_sb[:, ds(b * TPB, TPB), :]
                    v.tensor_tensor(xb, ps[:, 6:8, :].rearrange("p a n -> p (a n)").rearrange("p (t n) -> p t n", n=D),
                                    xb, ALU.add).then_inc(b_x, 1)
                    v.wait_ge(b_x, i + 1 + 1)

                qk_out_dve(0)
                rowmax(0, 0)
                with v.Fori(0, B * PAIRS - 1) as i:
                    dve_pair(i, v.snap(i // PAIRS), True)
                dve_pair(B * PAIRS - 1, B - 1, False)
            end_stage(v, 2)
            if last_stage >= 3:
                v.wait_ge(load_c, 160)
                with v.Fori(0, TPB) as p:
                    ln_stats(v, 2, p, lambda t: x_sb[:, t * TPB + p, :])
                    c = Chain(v, c_dve, p * C_ALL, C_ALL, alone)
                    v.wait_ge(c_qk_ps, p + 2)
                    c.link(v.tensor_tensor(qkv[:, :, 0:2 * D], ps[:, 0:4, :],
                                           bqkv[:, 0:2 * D].unsqueeze(1).broadcast_to([P, B, 2 * D]), ALU.add))
                    c.link(v.tensor_tensor(qkv[:, :, 2 * D:3 * D], ps[:, 4:6, :].rearrange("p a n -> p (a n)")
                                           .rearrange("p (t n) -> p t n", n=D),
                                           bqkv[:, 2 * D:3 * D].unsqueeze(1).broadcast_to([P, B, D]), ALU.add))
                    for s in range(B):
                        c.link(v.tensor_tensor(prod[:, :, :], qkv[:, :, D:2 * D],
                                               qkv[:, s, 0:D].unsqueeze(1).broadcast_to([P, B, D]), ALU.mult))
                        c.link(v.tensor_reduce(sc[:, s, :, :], prod[:, :, :].rearrange("p s (h d) -> p s h d", h=HC),
                                               AX, ALU.add))
                    c.link(v.tensor_reduce(scm[:, :, :], sc[:, :, :, :].rearrange("p s k h -> p s h k"), AX, ALU.max))
                    v.tensor_tensor(sc[:, :, :, :], sc[:, :, :, :], scm[:, :, :].unsqueeze(2)
                                    .broadcast_to([P, B, B, HC]), ALU.subtract).then_inc(c_exp_in, 1)
                    v.wait_ge(c_exp, p + 2)
                    c.link(v.tensor_reduce(scs[:, :, :], sc[:, :, :, :].rearrange("p s k h -> p s h k"), AX, ALU.add))
                    c.link(v.reciprocal(scs[:, :, :], scs[:, :, :]))
                    c.link(v.tensor_tensor(sc[:, :, :, :], sc[:, :, :, :], scs[:, :, :].unsqueeze(2)
                                           .broadcast_to([P, B, B, HC]), ALU.mult))
                    for s in range(B):
                        for k in range(B):
                            last = v.tensor_tensor(prod2[:, k, :].rearrange("p (h d) -> p h d", h=HC),
                                                   qkv[:, k, 2 * D:3 * D].rearrange("p (h d) -> p h d", h=HC),
                                                   sc[:, s, k, :].unsqueeze(2).broadcast_to([P, HC, DC]), ALU.mult)
                        c.link(last)
                        c.link(v.tensor_reduce(o_c[:, s, :], prod2[:, :, :].rearrange("p k n -> p n k"), AX, ALU.add))
                    assert c.k == C_O
                    v.wait_ge(c_proj, p + 2)
                    c.link(v.tensor_tensor(r_c[:, :, :], xn[:, :, :], ps[:, 0:2, :].rearrange("p a n -> p (a n)")
                                           .rearrange("p (t n) -> p t n", n=D), ALU.add))
                    c.link(v.tensor_tensor(r_c[:, :, :], r_c[:, :, :], bo_c[:, :].unsqueeze(1)
                                           .broadcast_to([P, B, D]), ALU.add))
                    for t in range(B):
                        last = v.bn_stats(stats[:, t, :], r_c[:, t, :])
                    c.link(last)
                    for t in range(B):
                        last = v.bn_aggr(mv[:, t, :], stats[:, t, :])
                    c.link(last)
                    v.tensor_scalar(ve2[:, :], mv[:, :, 1], EPS, None, ALU.add).then_inc(c_var, 1)
                    v.wait_ge(c_rstd, p + 2)
                    for t in range(B):
                        last = v.tensor_scalar(r_c[:, t, :], r_c[:, t, :], mv[:, t, 0:1], rstd2[:, t:t + 1],
                                               ALU.subtract, ALU.mult)
                    c.link(last)
                    c.link(v.tensor_tensor(r_c[:, :, :], r_c[:, :, :], g1[:, :].unsqueeze(1)
                                           .broadcast_to([P, B, D]), ALU.mult))
                    c.link(v.tensor_tensor(r_c[:, :, :], r_c[:, :, :], be1[:, :].unsqueeze(1)
                                           .broadcast_to([P, B, D]), ALU.add))
                    assert c.k == C_Y
                    c.link(v.tensor_copy(y_sb[:, :, :].rearrange("p (s q) d -> p q s d", s=B)[:, ds(p, 1), :, :]
                                         .rearrange("p a s d -> p (a s) d"), r_c[:, :, :]))
                    v.wait_ge(c_lg, p + 2)
                    c.link(v.tensor_copy(lg[:, :, :], ps[:, 4, 0:B * E].rearrange("p (s e) -> p s e", e=E)))
                    c.link(v.tensor_reduce(lgm[:, :], lg[:, :, :], AX, ALU.max))
                    c.link(v.tensor_tensor(lge[:, :, :], lg[:, :, :], lgm[:, :].unsqueeze(2)
                                           .broadcast_to([P, B, E]), ALU.is_equal))
                    c.link(v.tensor_scalar(lge[:, :, :], lge[:, :, :], -float(E), float(E), ALU.mult, ALU.add))
                    c.link(v.tensor_tensor(lge[:, :, :], lge[:, :, :], rank[:, :].unsqueeze(1)
                                           .broadcast_to([P, B, E]), ALU.add))
                    c.link(v.tensor_reduce(lgi[:, :], lge[:, :, :], AX, ALU.min))
                    for s in range(B):
                        c.link(v.tensor_scalar(emask[:, ds(s * TPB + p, 1), :].rearrange("p a e -> p (a e)"),
                                               rank[:, :], lgi[:, s:s + 1], None, ALU.is_equal))
                    c.done()
            end_stage(v, 3)
            if last_stage >= 3:
                v.wait_ge(load_e, 16 * 4)
                v.wait_ge(r_ps, 1 + 1)
                v.wait_ge(c_dve, TPB * C_ALL + 1)
                c = Chain(v, r_dve, 0, 13)
                step128 = route_c[:, 0:NT].unsqueeze(1).broadcast_to([P, E, NT])
                lower = route_c[:, NT:NT + E * E].rearrange("p (a b) -> p a b", b=E)
                c.link(v.tensor_copy(r_cnt[:, :], ps[:, 1, 0:E]))
                c.link(v.tensor_tensor(r_over[:, :, :], r_cnt[:, :].unsqueeze(2).broadcast_to([P, E, NT]), step128, ALU.is_gt))
                c.link(v.tensor_reduce(r_tiles[:, :], r_over[:, :, :], AX, ALU.add))
                c.link(v.tensor_tensor(r_low[:, :, :], r_tiles[:, :].unsqueeze(1).broadcast_to([P, E, E]), lower, ALU.mult))
                c.link(v.tensor_reduce(r_start[:, :], r_low[:, :, :], AX, ALU.add))
                c.link(v.tensor_tensor(r_end[:, :], r_start[:, :], r_tiles[:, :], ALU.add))
                c.link(v.tensor_tensor(r_past[:, :, :], r_end[:, 0:E - 1].unsqueeze(1).broadcast_to([P, MT, E - 1]),
                                       route_c[:, NT + E * E:].unsqueeze(2).broadcast_to([P, MT, E - 1]), ALU.is_le))
                c.link(v.tensor_reduce(r_exp[:, :], r_past[:, :, :], AX, ALU.add))
                c.link(v.tensor_scalar(r_exp[:, :], r_exp[:, :], float(P), None, ALU.mult))
                v.tensor_tensor(r_row[:, :], r_exp[:, :], lane[:, 0:1].broadcast_to([P, MT]), ALU.add).then_inc(r_rows, 1)
                c.link(v.tensor_scalar(r_start[:, :], r_start[:, :], float(P), None, ALU.mult))
                c.link(v.tensor_tensor(r_slot[:, :, :], ps[:, 0, 0:NT * E].rearrange("p (t e) -> p t e", e=E),
                                       r_start[:, :].unsqueeze(1).broadcast_to([P, NT, E]), ALU.add))
                c.link(v.tensor_tensor(r_slot[:, :, :], r_slot[:, :, :], emask[:, :, :], ALU.mult))
                c.link(v.tensor_reduce(r_posf[:, :], r_slot[:, :, :], AX, ALU.add))
                c.done()
                v.tensor_copy(r_pos[:, :], r_posf[:, :]).then_inc(r_slots, 1)

                def rows_T(n, q):
                    v.wait_ge(e_tr, n + 1 + 1)
                    v.tensor_copy(ysT[:, q, :, :], ps[:, 4 + q, 0:KT * P].rearrange("p (k n) -> p k n", k=KT))\
                        .then_inc(e_yT, 1)

                def dve_step(i, q, ahead):
                    n = i * 2 + q
                    if ahead:
                        rows_T(n + 2, q)
                    v.wait_ge(e_o_ps, n + 1 + 1)
                    v.wait_ge(e_w2[q], i * 16 + 16)
                    v.wait_ge(e_st[q], i * 16 + 1)
                    v.tensor_tensor(eo[:, q, :], ps[:, 6 + q, 0:D], x2[:, q, W2_LEN:X2_LEN], ALU.add).then_inc(e_o, 1)

                rows_T(0, 0)
                rows_T(1, 1)
                with v.Fori(0, MT // 2 - 1) as i:
                    for q in range(2):
                        dve_step(i, q, True)
                i = MT // 2 - 1
                dve_step(i, 0, True)
                dve_step(i, 1, False)
                dve_step(i + 1, 0, False)
                with v.Fori(0, B) as j:
                    c = Chain(v, z_dve, j * 6, 6, alone)
                    yt = lambda t: y_sb[:, j * TPB + t, :]
                    v.wait_ge(e_back, (j + 1) * 16 * TPB)
                    v.wait_ge(e_scat, 16 * NT)
                    c.link(v.tensor_tensor(y_sb[:, ds(j * TPB, TPB), :], y_sb[:, ds(j * TPB, TPB), :],
                                           moe[:, ds(j * TPB, TPB), :], ALU.add))
                    for t in range(TPB):
                        last = v.bn_stats(stats[:, t, :], yt(t))
                    c.link(last)
                    for t in range(TPB):
                        last = v.bn_aggr(mv[:, t, :], stats[:, t, :])
                    c.link(last)
                    v.tensor_scalar(ve2[:, :], mv[:, :, 1], EPS, None, ALU.add).then_inc(z_var, 1)
                    v.wait_ge(z_rstd, j + 2)
                    v.wait_ge(stored, j * 16 + 1)
                    for t in range(TPB):
                        last = v.tensor_scalar(z[:, t, :], yt(t), mv[:, t, 0:1], rstd2[:, t:t + 1],
                                               ALU.subtract, ALU.mult)
                    c.link(last)
                    c.link(v.tensor_tensor(z[:, :, :], z[:, :, :], g2[:, :].unsqueeze(1)
                                           .broadcast_to([P, TPB, D]), ALU.mult))
                    c.link(v.tensor_tensor(z[:, :, :], z[:, :, :], be2[:, :].unsqueeze(1)
                                           .broadcast_to([P, TPB, D]), ALU.add))
                    c.done()
                    v.tensor_tensor(z[:, :, :], z[:, :, :], x_sb[:, ds(j * TPB, TPB), :], ALU.add).then_inc(z_out, 1)
            else:
                with v.Fori(0, B) as j:
                    v.wait_ge(stored, j * 16 + 1)
                    v.tensor_copy(z[:, :, :], x_sb[:, ds(j * TPB, TPB), :]).then_inc(z_out, 1)

        @block.tensor
        def _(pe):
            pe.wait_ge(load_a, 16 * 11)
            pe.wait_ge(dve_setup, 9)
            def pe_rows(b, following):
                pe.wait_ge(ln_xnT[0], b * KT + 2 + 1)
                pe.wait_ge(a_qk, b + 1)
                for t in range(TPB):
                    for k in range(KT):
                        last = pe.matmul(ps[:, t, :], xnT_a[:, k, t * P:(t + 1) * P], wqkv_a[:, k, 0:2 * D],
                                         start=k == 0, stop=k == KT - 1)
                    last.then_inc(a_qk_ps, 1)
                pe.wait_ge(a_v, b + 1)
                for t in range(TPB):
                    for k in range(KT):
                        last = pe.matmul(ps[:, 4 + t // 2, (t % 2) * D:(t % 2 + 1) * D],
                                         xnT_a[:, k, t * P:(t + 1) * P], wqkv_a[:, k, 2 * D:3 * D],
                                         start=k == 0, stop=k == KT - 1)
                last.then_inc(a_v_ps, 1)
                if following:
                    ln_transpose(pe, 0, b + 1, 6)

            ln_transpose(pe, 0, 0, 6)
            with pe.Fori(0, B - 1) as b:
                pe_rows(b, True)
            pe_rows(B - 1, False)

            def stacks(n):
                pe.wait_ge(a_hi, n * 4 + 4 + 1)
                pe.wait_ge(a_lo, n * 4 + 4 + 1)
                for bank, (st, hp) in enumerate(((q_st, 0), (k_st, 0), (q_st, 1), (k_st, 1))):
                    pe.wait_ge(a_exp, n * 4 - (1 if bank < 3 else 0) + 1) if not isinstance(n, int) or n > 0 else None
                    for t in range(TPB):
                        last = pe.transpose(ps[:, bank, t * P:(t + 1) * P],
                                            cast(st[:, t, 2 * hp:2 * hp + 2, :].rearrange("p h d -> p (h d)")),
                                            ident[:, :])
                    last.then_inc(a_tr, 1)

            def scores(n, h):
                hp, rows = h // 2, slice(64 * (h % 2), 64 * (h % 2) + 64)
                base = 3 * (h % 2)
                if h < 2:
                    pe.wait_ge(a_T_act, n * 2 + 2 + 1)
                    pe.wait_ge(a_T_dve, n * 2 + 2 + 1)
                else:
                    pe.wait_ge(a_exp, n * 4 + h - 2 + 1 + 1)
                for qt in range(TPB):
                    bank, off = (base, TRI[qt]) if qt < 2 else (base + qt - 1, 0)
                    pe.matmul(ps[:, bank, off:off + (qt + 1) * P], qT_a[rows, hp, qt * P:(qt + 1) * P],
                              kT_a[rows, hp, 0:(qt + 1) * P], start=True, stop=False)
                    last = pe.matmul(ps[:, bank, off + qt * P:off + (qt + 1) * P], ident_r[:, :], mask_r[:, :],
                                     start=False, stop=True)
                last.then_inc(a_s, 1)

            def turn_a(n, h, first):
                pe.wait_ge(a_prob, n * 16 + 4 * h + 4 + 1)
                for j, blocks in enumerate(TRI_BLOCKS):
                    if j == 2:
                        pe.wait_ge(a_pt_act, n * 4 + h + 1 + 1)
                    elif h > 0:
                        pe.wait_ge(a_pt_dve, n * 8 + 2 * (h - 1) + j + 1 + 1)
                    elif not first:
                        pe.wait_ge(a_x, 2 * (n - 1) + j + 1 + 1)
                    for m, (kt, qt) in enumerate(blocks):
                        last = pe.transpose(ps[:, 6 + (3 + 3 * h + j) % 2, m * P:(m + 1) * P],
                                            prob_a[:, h, TRI[qt] + kt * P:TRI[qt] + (kt + 1) * P], ident[:, :])
                    last.then_inc(a_pt, 1)

            def weigh(n):
                pe.wait_ge(a_pt_act, n * 4 + 4 + 1)
                pe.wait_ge(a_pt_dve, n * 8 + 8 + 1)
                pe.wait_ge(a_vpad, n * 4 + 4 + 1)
                for kt in range(TPB):
                    for h in range(4):
                        last = pe.matmul(ps[32 * h:32 * h + 32, 6, kt * P:S], v_pad[:, kt, h, :],
                                         probT_a[:, h, TRI_KEYS[kt]:TRI_KEYS[kt] + S - kt * P],
                                         start=kt == 0, stop=kt == TPB - 1)
                last.then_inc(a_pv, 1)

            def out_a(n, q):
                pe.wait_ge(a_o, n + 1 + 1)
                for t in range(TPB):
                    last = pe.matmul(ps[:, 7 - t // 2, (t % 2) * D:(t % 2 + 1) * D], oT_a[:, t * P:(t + 1) * P],
                                     wo_a[:, ds(q, 1), :].rearrange("p a n -> p (a n)"), start=True, stop=True)
                    if t % 2:
                        last.then_inc(a_y, 1)

            def pe_quad(n, q0, first, following):
                scores(n, 0)
                scores(n, 1)
                if not first:
                    weigh(n - 1)
                scores(n, 2)
                if not first:
                    out_a(n - 1, q0)
                turn_a(n, 0, first)
                scores(n, 3)
                turn_a(n, 1, first)
                turn_a(n, 2, first)
                if following:
                    stacks(n + 1)
                turn_a(n, 3, first)

            stacks(0)
            pe_quad(0, 0, True, True)
            with pe.Fori(1, NQ - 1) as n:
                pe_quad(n, pe.snap((n - 1) % QUADS), False, True)
            pe_quad(NQ - 1, (NQ - 2) % QUADS, False, False)
            weigh(NQ - 1)
            out_a(NQ - 1, QUADS - 1)
            end_stage(pe, 1)
            if last_stage >= 2:
                with pe.Fori(0, B) as b:
                    pe.wait_ge(ln_xnT[1], b * KT + 1)
                    ln_transpose(pe, 1, b, 6)
                pe.wait_ge(ln_xnT[1], B * KT + 1)

                def project(bank, w_s, rhs):
                    for k in range(KT):
                        last = pe.matmul(ps[:, bank, :], w_s[:, k, :], rhs(k), start=k == 0, stop=k == KT - 1)
                    return last

                own = lambda n: lambda k: xnT[:, k, ds((n // PAIRS) * S, S)]

                def project_k(n):
                    pe.wait_ge(b_w, n * 64 + 64 + 1)
                    project(0, wk_s, own(n))
                    project(1, wm_s, lambda k: memT[:, k, 0:512])
                    project(2, wm_s, lambda k: memT[:, k, 512:1024]).then_inc(b_pk, 1)

                def project_q(n):
                    project(3, wq_s, own(n)).then_inc(b_pq, 1)

                def project_v(n):
                    pe.wait_ge(b_wv, n * 16 + 16 + 1)
                    project(5, wv_s, own(n)).then_inc(b_pv_ps, 1)

                def scores_b(i, u, chunks=range(KC)):
                    if u >= 2 and chunks[0] == 0:
                        pe.wait_ge(b_exp, i * UNITS + u - 2 + 1 + 1)
                    h, qt = u // 4, u % 4
                    for c in chunks:
                        for part in range(2):
                            last = pe.matmul(ps[:, 3 * (u % 2) + c, :], q_dup[:, h, part, qt * P:(qt + 1) * P],
                                             k_st2[:, h, c * 512:(c + 1) * 512], start=part == 0, stop=part == 1)
                    if chunks[-1] == KC - 1:
                        last.then_inc(b_s, 1)

                def bank_free(i, cc):
                    u, c = cc // 3, cc % 3
                    if cc < 0:
                        pe.wait_ge(b_x, i + 1)
                    elif c == 0:
                        pe.wait_ge(b_pt_dve, i * 9 + u + 1 + 1)
                    else:
                        pe.wait_ge(b_pt_act, i * 18 + 2 * u + c + 1)

                def turn(i, u, chunks=range(3)):
                    if u < 0:
                        pe.wait_ge(b_v_f, i + 1 + 1)
                    elif chunks[0] == 0:
                        pe.wait_ge(b_prob, i * UNITS + u + 1 + 1)
                    for c in chunks:
                        cc = 3 * (u + 1) + c
                        bank_free(i, cc - 2)
                        for m in range(4):
                            src = kv_f[:, (3, 1, 2)[c], m * P:(m + 1) * P] if u < 0 else \
                                prob[:, u % NPROB, (4 * c + m) * P:(4 * c + m + 1) * P]
                            last = pe.transpose(ps[:, 6 + cc % 2, m * P:(m + 1) * P], src, ident[:, :])
                        last.then_inc(b_pt, 1)

                def first_scores(n):
                    pe.wait_ge(b_khi_act, n + 1 + 1)
                    pe.wait_ge(b_lo, n * 6 + 6 + 1)
                    scores_b(n, 0)

                def pe_pair(i, following):
                    pe.wait_ge(b_v_f, i + 1 + 1)
                    pe.wait_ge(b_o, i + 1)
                    scores_b(i, 1)
                    turn(i, -1, (0, 1))
                    scores_b(i, 2)
                    turn(i, -1, (2,))
                    for u in range(3, UNITS):
                        scores_b(i, u, (0, 1))
                        turn(i, u - 3, (0,))
                        scores_b(i, u, (2,))
                        turn(i, u - 3, (1, 2))
                    if following:
                        pe.wait_ge(b_exp, i * UNITS + UNITS - 1 + 1)
                        pe.wait_ge(b_w, (i + 1) * 64 + 64 + 1)
                        project(0, wk_s, own(i + 1))
                    turn(i, UNITS - 3, (0,))
                    if following:
                        project(1, wm_s, lambda k: memT[:, k, 0:512])
                    turn(i, UNITS - 3, (1,))
                    if following:
                        project(2, wm_s, lambda k: memT[:, k, 512:1024]).then_inc(b_pk, 1)
                    turn(i, UNITS - 3, (2,))
                    turn(i, UNITS - 2, (0,))
                    if following:
                        pe.wait_ge(b_exp, i * UNITS + UNITS + 1)
                        project_q(i + 1)
                    turn(i, UNITS - 2, (1, 2))
                    turn(i, UNITS - 1, (0, 1))
                    pe.wait_ge(b_pt_dve, i * 9 + 9 + 1)
                    for kt in range(KEY_TILES):
                        if kt == 4:
                            turn(i, UNITS - 1, (2,))
                            pe.wait_ge(b_pt_act, i * 18 + 17 + 1)
                        if kt == 8:
                            pe.wait_ge(b_pt_act, i * 18 + 18 + 1)
                        for h in range(2):
                            last = pe.matmul(ps[64 * h:64 * h + 64, 4, :], v_b[:, kt, 64 * h:64 * h + 64],
                                             probT[:, h, kt, :], start=kt == 0, stop=kt == KEY_TILES - 1)
                    last.then_inc(b_out, 1)
                    if following:
                        project_v(i + 1)
                        first_scores(i + 1)
                    pe.wait_ge(b_o, i + 1 + 1)
                    pe.wait_ge(b_wo, i * 16 + 16 + 1)
                    for t in range(TPB):
                        last = pe.matmul(ps[:, 6 + t // 2, (t % 2) * D:(t % 2 + 1) * D], oT[:, t * P:(t + 1) * P],
                                         wo_s[:, :], start=True, stop=True)
                    last.then_inc(b_y, 1)

                project_k(0)
                project_q(0)
                project_v(0)
                first_scores(0)
                with pe.Fori(0, B * PAIRS - 1) as i:
                    pe_pair(i, True)
                pe_pair(B * PAIRS - 1, False)
            end_stage(pe, 2)
            if last_stage >= 3:
                pe.wait_ge(load_c, 160)
                with pe.Fori(0, TPB) as p:
                    pe.wait_ge(c_yT, p * KT + 1)
                    ln_transpose(pe, 2, p, 6)
                    pe.wait_ge(ln_xnT[2], p * KT + 2 + 1)
                    pe.wait_ge(c_dve, p * C_ALL + 1)
                    for t in range(B):
                        for k in range(KT):
                            pe.matmul(ps[:, t, :], uT[:, k, t * P:(t + 1) * P], wqkv_c[:, k, 0:2 * D],
                                      start=k == 0, stop=k == KT - 1)
                    for t in range(B):
                        for k in range(KT):
                            last = pe.matmul(ps[:, 4 + t // 2, (t % 2) * D:(t % 2 + 1) * D],
                                             uT[:, k, t * P:(t + 1) * P], wqkv_c[:, k, 2 * D:3 * D],
                                             start=k == 0, stop=k == KT - 1)
                    last.then_inc(c_qk_ps, 1)
                    pe.wait_ge(c_dve, p * C_ALL + C_O + 1)
                    for k in range(KT):
                        for t in range(B):
                            last = pe.transpose(ps[:, 6 + k, t * P:(t + 1) * P], o_c[:, t, k * P:(k + 1) * P], ident[:, :])
                        last.then_inc(c_otr, 1)
                    pe.wait_ge(c_oT, p * KT + 2 + 1)
                    for t in range(B):
                        for k in range(KT):
                            last = pe.matmul(ps[:, t // 2, (t % 2) * D:(t % 2 + 1) * D], oT_c[:, k, t * P:(t + 1) * P],
                                             wo_c[:, k, :], start=k == 0, stop=k == KT - 1)
                    last.then_inc(c_proj, 1)
                    pe.wait_ge(c_dve, p * C_ALL + C_Y + 1)
                    for k in range(KT):
                        for t in range(B):
                            last = pe.transpose(ps[:, 6 + k, t * P:(t + 1) * P], r_c[:, t, k * P:(k + 1) * P], ident[:, :])
                        last.then_inc(c_ytr, 1)
                    pe.wait_ge(c_yT, p * KT + 2 + 1)
                    for t in range(B):
                        for k in range(KT):
                            last = pe.matmul(ps[:, 4, t * E:(t + 1) * E], yT_c[:, k, t * P:(t + 1) * P], wg_c[:, k, :],
                                             start=k == 0, stop=k == KT - 1)
                    last.then_inc(c_lg, 1)
            end_stage(pe, 3)
            if last_stage >= 3:
                pe.wait_ge(load_e, 16 * 4)
                pe.wait_ge(c_dve, TPB * C_ALL + 1)
                pe.matmul(ps[:, 0, 0:NT * E], before[:, :], emask[:, :, :].rearrange("p t e -> p (t e)"),
                          start=True, stop=False)
                for t in range(1, NT):
                    pe.matmul(ps[:, 0, t * E:NT * E], ones[:, :], emask[:, 0:NT - t, :].rearrange("p t e -> p (t e)"),
                              start=False, stop=t == NT - 1)
                for t in range(NT):
                    last = pe.matmul(ps[:, 1, 0:E], ones[:, :], emask[:, t, :], start=t == 0, stop=t == NT - 1)
                last.then_inc(r_ps, 1)

                def transpose_rows(i, q):
                    pe.wait_ge(e_y[q], i * 16 + 16 + 1)
                    for k in range(KT):
                        last = pe.transpose(ps[:, 4 + q, k * P:(k + 1) * P], ys[:, q, k * P:(k + 1) * P], ident[:, :])
                    last.then_inc(e_tr, 1)

                def first_layer(i, q):
                    pe.wait_ge(e_w1[q], i * 16 + 16)
                    pe.wait_ge(e_yT, i * 2 + q + 1 + 1)
                    for f in range(FT):
                        for k in range(KT):
                            last = pe.matmul(ps[:, 2 * q + f // 4, (f % 4) * P:(f % 4 + 1) * P],
                                             w1(q)[:, k, f * P:(f + 1) * P], ysT[:, q, k, :],
                                             start=k == 0, stop=k == KT - 1)
                        if f % 4 == 3:
                            last.then_inc(e_h_ps, 1)

                def second_layer(i, q, used=True):
                    n = i * 2 + q
                    pe.wait_ge(e_w2[q], i * 16 + 16)
                    pe.wait_ge(e_h, n * FT + FT + 1)
                    if used:
                        pe.wait_ge(e_o, n - 1 + 1)
                    for f in range(FT):
                        last = pe.matmul(ps[:, 6 + q, 0:D], hT[:, q, f, :], w2(q)[:, f, :],
                                         start=f == 0, stop=f == FT - 1)
                    last.then_inc(e_o_ps, 1)

                pe.wait_ge(r_slots, 1 + 1)
                transpose_rows(0, 0)
                transpose_rows(0, 1)
                def two_tiles(i, used=True):
                    first_layer(i, 1)
                    transpose_rows(i + 1, 0)
                    second_layer(i, 0, used)
                    first_layer(i + 1, 0)
                    transpose_rows(i + 1, 1)
                    second_layer(i, 1, used)

                first_layer(0, 0)
                two_tiles(0, False)
                with pe.Fori(1, MT // 2 - 1) as i:
                    two_tiles(i)
                i = MT // 2 - 1
                first_layer(i, 1)
                transpose_rows(i + 1, 0)
                second_layer(i, 0)
                first_layer(i + 1, 0)
                second_layer(i, 1)
                second_layer(i + 1, 0)


def layout(inputs):
    a = {k: np.ascontiguousarray(np.asarray(v)) for k, v in inputs.items()}
    pos = np.arange(S, dtype=np.float32)[:, None]
    di = np.arange(0, DA, 2, dtype=np.float32) / np.float32(DA)
    theta = pos * np.exp(-di * np.float32(np.log(10000.0))).astype(np.float32)
    cos = np.repeat(np.cos(theta), 2, axis=1).astype(np.float32)
    sin = np.repeat(np.sin(theta), 2, axis=1).astype(np.float32)
    sign = np.concatenate([-np.ones(DA // 2), np.ones(DA // 2)]).astype(np.float32)
    turn = lambda w: np.concatenate([w[1::2], w[::2]])
    qg, qb, kg, kb = (a["L0_attn_" + n] for n in ("q_gamma", "q_beta", "k_gamma", "k_beta"))
    inner = HB * DB
    return {
        "x": a["x"].reshape(B * S, D),
        "ident": np.eye(P, dtype=np.float32),
        "mask": np.triu(np.full((P, P), -1e30, np.float32), 1),
        "cos": cos, "sin": sin * sign,
        "gb": np.concatenate([qg, kg, turn(qg), turn(kg), qb, kb, turn(qb), turn(kb)]),
        "a_wqkv": np.concatenate([a["L0_attn_Wq"].T, a["L0_attn_Wk"].T, a["L0_attn_Wv"].T], axis=1),
        "a_wo": a["L0_attn_Wo"].T, "a_bo": a["L0_attn_bo"],
        "ctxT": a["ctx_1024"].transpose(0, 2, 1),
        "ln_g": a["L0_xattn_ln_g"].reshape(KT, P).T, "ln_b": a["L0_xattn_ln_b"].reshape(KT, P).T, "b_bo": a["L0_xattn_bo"],
        "b_wq": a["L0_xattn_Wq"], "b_wk": a["L0_xattn_Wkv"][:, :inner], "b_wv": a["L0_xattn_Wkv"][:, inner:],
        "b_wm": a["L0_xattn_Wm"], "b_wo": a["L0_xattn_Wo"],
        "c_wqkv": a["L0_ffn_Wqkv"].T, "c_wo": a["L0_ffn_Wo"].T, "c_wg": a["L0_ffn_Wg"].T,
        "c_bqkv": a["L0_ffn_bqkv"], "c_bo": a["L0_ffn_bo"],
        "c_g1": a["L0_ffn_g1"], "c_be1": a["L0_ffn_be1"], "c_g2": a["L0_ffn_g2"], "c_be2": a["L0_ffn_be2"],
        "rank": np.arange(E, dtype=np.float32),
        "route": np.concatenate([np.arange(NT) * P, np.tril(np.ones((E, E)), -1).ravel(), np.arange(MT)]).astype(np.float32),
        "lane": np.arange(P, dtype=np.float32)[:, None],
        "before": np.triu(np.ones((P, P), np.float32), 1), "ones": np.ones((P, P), np.float32),
        "experts1": np.concatenate([a["L0_ffn_W1"].reshape(E, KT, P, DF).transpose(0, 2, 1, 3).reshape(E * P, W1_LEN),
                                    a["L0_ffn_b1"].reshape(E, FT, P).transpose(0, 2, 1).reshape(E * P, FT)], axis=1),
        "experts2": np.concatenate([a["L0_ffn_W2"].reshape(E, FT, P, D).transpose(0, 2, 1, 3).reshape(E * P, W2_LEN),
                                    np.repeat(a["L0_ffn_b2"], P, axis=0)], axis=1),
    }


def kernel(**inputs):
    import concourse.bacc as _bacc
    from concourse.bass_utils import run_bass_kernel_spmd as _run

    nc = _bacc.Bacc("TRN2", target_bir_lowering=False, num_devices=1)
    arrays, io = {}, {}
    for name, v in layout(inputs).items():
        v = np.ascontiguousarray(v)
        arrays["in_" + name] = v
        io[name] = nc.dram_tensor("in_" + name, v.shape, mybir.dt.from_np(v.dtype), kind="ExternalInput").ap()
    out = nc.dram_tensor("out_0", (B * S, D), F32, kind="ExternalOutput").ap()
    build(nc, io, out)
    r = _run(nc, [arrays], core_ids=[0])
    return r.results[0]["out_0"].reshape(B, S, D)
```
